# Optimizing a Trainium2 kernel written in Bass

```python
import numpy as np
import jax
import jax.numpy as jnp

def _softmax(x, axis=-1):
    return jax.nn.softmax(x, axis=axis)

def _gelu(x):
    return jax.nn.gelu(x, approximate=True)

def _silu(x):
    return jax.nn.silu(x)

def _sigmoid(x):
    return jax.nn.sigmoid(x)

def _layernorm(x, axis=-1, eps=1e-05):
    m = jnp.mean(x, axis=axis, keepdims=True)
    v = jnp.var(x, axis=axis, keepdims=True)
    return (x - m) / jnp.sqrt(v + eps)

def _scatter_add(tgt, idx, src, axis=0):
    return tgt.at[idx].add(src)

def _segment_sum(src, seg, n):
    return jax.ops.segment_sum(src, seg, n)
kernel_name = 'mk_gps_d1_gnn_r16_cf8a9a'

def setup_inputs(seed: int=0):
    np.random.seed(seed)
    _w = jnp.asarray

    def _rec_inputs():
        import jax
        import jax.numpy as jnp
        _gk = jax.random.key(seed)
        x = -0.0002117 + 1 * jax.random.normal(jax.random.fold_in(_gk, 1), (6250, 256), jnp.float32)
        src = jax.random.randint(jax.random.fold_in(_gk, 2), (100000,), 0, 6250, jnp.int32)
        dst = jnp.minimum((6250 * jax.random.uniform(jax.random.fold_in(_gk, 3), (100000,)) ** 2.0).astype(jnp.int32), 99999)
        _o = jnp.argsort(dst, stable=True)
        src = src[_o]
        dst = dst[_o]
        return (x, src, dst)
    x, src, dst = _rec_inputs()

    def _L0_gnn_setup():
        import jax, jax.numpy as jnp
        import numpy as np
        N = 6250
        E = 200000
        D = 256

        def _gcn_norm(edge_index, num_nodes):
            loop = jnp.arange(num_nodes, dtype=edge_index.dtype)
            src = jnp.concatenate([edge_index[0], loop])
            dst = jnp.concatenate([edge_index[1], loop])
            ones = jnp.ones(src.shape[0], dtype=jnp.float32)
            deg = jax.ops.segment_sum(ones, dst, num_segments=num_nodes)
            dis = jnp.where(deg > 0, jax.lax.rsqrt(deg), 0.0)
            norm = dis[src] * dis[dst]
            return (src, dst, norm)

        def _gcn_layer(x, src, dst, norm, W, b, num_nodes):
            xw = x @ W
            msg = xw[src] * norm[:, None]
            out = jax.ops.segment_sum(msg, dst, num_segments=num_nodes)
            return out + b
        key = jax.random.key(seed)
        k1, k2, k3, k4 = jax.random.split(key, 4)
        x = jax.random.normal(k1, (N, D), dtype=jnp.float32)
        edge_index = jax.random.randint(k2, (2, E), 0, N, dtype=jnp.int64)
        s = 1.0 / np.sqrt(D)
        W1 = jax.random.normal(k3, (D, D), dtype=jnp.float32) * s
        W2 = jax.random.normal(k4, (D, D), dtype=jnp.float32) * s
        b1 = jnp.zeros((D,), dtype=jnp.float32)
        b2 = jnp.zeros((D,), dtype=jnp.float32)
        return {'x': x, 'edge_index': edge_index, 'W1': W1, 'b1': b1, 'W2': W2, 'b2': b2}
    _L0_gnn_all = _L0_gnn_setup()
    _L0_gnn_in = {k: v for k, v in _L0_gnn_all.items() if k in ('W1', 'b1', 'W2', 'b2')}
    del _L0_gnn_all

    def _L0_mix_setup():
        import jax, jax.numpy as jnp
        import numpy as np
        NUM_HEADS = 8
        key = jax.random.key(seed)
        ks = jax.random.split(key, 5)
        B, N, C = (8, 1024, 256)
        x = jax.random.normal(ks[0], (B, N, C), dtype=jnp.float32)
        Wq = jax.random.normal(ks[1], (C, C), dtype=jnp.float32) * 0.02
        Wkv = jax.random.normal(ks[2], (2 * C, C), dtype=jnp.float32) * 0.02
        Wproj = jax.random.normal(ks[3], (C, C), dtype=jnp.float32) * 0.02
        bproj = jnp.zeros((C,), dtype=jnp.float32)
        return {'x': x, 'Wq': Wq, 'Wkv': Wkv, 'Wproj': Wproj, 'bproj': bproj}
    _L0_mix_all = _L0_mix_setup()
    _L0_mix_in = {k: v for k, v in _L0_mix_all.items() if k in ('Wq', 'Wkv', 'Wproj', 'bproj')}
    del _L0_mix_all

    def _L0_ffn_setup():
        import jax, jax.numpy as jnp
        import numpy as np
        TOP_K = 2
        LN_EPS = 1e-05
        key = jax.random.key(seed)
        ks = jax.random.split(key, 8)
        B, S, D, E, H = (16, 1024, 256, 8, 1024)
        x = jax.random.normal(ks[0], (B, S, D), dtype=jnp.float32)
        Wr = jax.random.normal(ks[1], (D, E), dtype=jnp.float32) * 0.1
        br = jnp.zeros((E,), dtype=jnp.float32)
        ln_g = jnp.ones((E, D), dtype=jnp.float32)
        ln_b = jnp.zeros((E, D), dtype=jnp.float32)
        W1 = jax.random.normal(ks[2], (E, D, H), dtype=jnp.float32) * (1.0 / np.sqrt(D))
        b1 = jnp.zeros((E, H), dtype=jnp.float32)
        W2 = jax.random.normal(ks[3], (E, H, D), dtype=jnp.float32) * (1.0 / np.sqrt(H))
        b2 = jnp.zeros((E, D), dtype=jnp.float32)
        return {'x': x, 'Wr': Wr, 'br': br, 'ln_g': ln_g, 'ln_b': ln_b, 'W1': W1, 'b1': b1, 'W2': W2, 'b2': b2}
    _L0_ffn_all = _L0_ffn_setup()
    _L0_ffn_in = {k: v for k, v in _L0_ffn_all.items() if k in ('Wr', 'br', 'ln_g', 'ln_b', 'W1', 'b1', 'W2', 'b2')}
    del _L0_ffn_all
    return {'x': x, 'src': src, 'dst': dst, 'L0_gnn_W1': _L0_gnn_in['W1'], 'L0_gnn_b1': _L0_gnn_in['b1'], 'L0_gnn_W2': _L0_gnn_in['W2'], 'L0_gnn_b2': _L0_gnn_in['b2'], 'L0_mix_Wq': _L0_mix_in['Wq'], 'L0_mix_Wkv': _L0_mix_in['Wkv'], 'L0_mix_Wproj': _L0_mix_in['Wproj'], 'L0_mix_bproj': _L0_mix_in['bproj'], 'L0_ffn_Wr': _L0_ffn_in['Wr'], 'L0_ffn_br': _L0_ffn_in['br'], 'L0_ffn_ln_g': _L0_ffn_in['ln_g'], 'L0_ffn_ln_b': _L0_ffn_in['ln_b'], 'L0_ffn_W1': _L0_ffn_in['W1'], 'L0_ffn_b1': _L0_ffn_in['b1'], 'L0_ffn_W2': _L0_ffn_in['W2'], 'L0_ffn_b2': _L0_ffn_in['b2']}

def reference(x, src, dst, L0_gnn_W1, L0_gnn_b1, L0_gnn_W2, L0_gnn_b2, L0_mix_Wq, L0_mix_Wkv, L0_mix_Wproj, L0_mix_bproj, L0_ffn_Wr, L0_ffn_br, L0_ffn_ln_g, L0_ffn_ln_b, L0_ffn_W1, L0_ffn_b1, L0_ffn_W2, L0_ffn_b2):
    import jax
    import jax.numpy as jnp

    def _L0_gnn_ref(x, edge_index, W1, b1, W2, b2):
        import jax, jax.numpy as jnp
        import numpy as np
        N = 6250
        E = 200000
        D = 256

        def _gcn_norm(edge_index, num_nodes):
            loop = jnp.arange(num_nodes, dtype=edge_index.dtype)
            src = jnp.concatenate([edge_index[0], loop])
            dst = jnp.concatenate([edge_index[1], loop])
            ones = jnp.ones(src.shape[0], dtype=jnp.float32)
            deg = jax.ops.segment_sum(ones, dst, num_segments=num_nodes)
            dis = jnp.where(deg > 0, jax.lax.rsqrt(deg), 0.0)
            norm = dis[src] * dis[dst]
            return (src, dst, norm)

        def _gcn_layer(x, src, dst, norm, W, b, num_nodes):
            xw = x @ W
            msg = xw[src] * norm[:, None]
            out = jax.ops.segment_sum(msg, dst, num_segments=num_nodes)
            return out + b
        src, dst, norm = _gcn_norm(edge_index, N)
        h = jax.nn.elu(_gcn_layer(x, src, dst, norm, W1, b1, N))
        h = jax.nn.elu(_gcn_layer(h, src, dst, norm, W2, b2, N))
        return h

    def _L0_mix_ref(x, Wq, Wkv, Wproj, bproj):
        import jax, jax.numpy as jnp
        import numpy as np
        NUM_HEADS = 8
        B, N, C = x.shape
        h = NUM_HEADS
        d = C // h
        q = jnp.einsum('bnc,oc->bno', x, Wq).reshape(B, N, h, d).transpose(0, 2, 1, 3)
        kv = jnp.einsum('bnc,oc->bno', x, Wkv).reshape(B, N, 2, h, d)
        k = kv[:, :, 0].transpose(0, 2, 1, 3)
        v = kv[:, :, 1].transpose(0, 2, 1, 3)
        q = jax.nn.elu(q) + 1.0
        k = jax.nn.elu(k) + 1.0
        k_sum = k.sum(axis=2)
        D_inv = 1.0 / jnp.maximum(jnp.einsum('bhnd,bhd->bhn', q, k_sum), 1e-06)
        context = jnp.einsum('bhnd,bhne->bhde', k, v)
        attn = jnp.einsum('bhnd,bhde->bhne', q, context) * D_inv[..., None]
        out = attn.transpose(0, 2, 1, 3).reshape(B, N, C)
        out = jnp.einsum('bnc,oc->bno', out, Wproj) + bproj
        return out

    def _L0_ffn_ref(x, Wr, br, ln_g, ln_b, W1, b1, W2, b2):
        import jax, jax.numpy as jnp
        import numpy as np
        TOP_K = 2
        LN_EPS = 1e-05
        B, S, D = x.shape
        N = B * S
        xt = x.reshape(N, D)
        logits = xt @ Wr + br
        probs = jax.nn.softmax(logits, axis=-1)
        top_p, top_idx = jax.lax.top_k(probs, TOP_K)
        weights = top_p / top_p.sum(axis=-1, keepdims=True)
        mu = xt.mean(axis=-1, keepdims=True)
        var = ((xt - mu) ** 2).mean(axis=-1, keepdims=True)
        xn = (xt - mu) * jax.lax.rsqrt(var + LN_EPS)
        xe = xn[None, :, :] * ln_g[:, None, :] + ln_b[:, None, :]
        h = jax.nn.gelu(jnp.einsum('end,edh->enh', xe, W1) + b1[:, None, :], approximate=False)
        y = jnp.einsum('enh,ehd->end', h, W2) + b2[:, None, :]
        y_tok = jnp.transpose(y, (1, 0, 2))
        sel = jnp.take_along_axis(y_tok, top_idx[:, :, None], axis=1)
        out = (weights[:, :, None] * sel).sum(axis=1)
        return out.reshape(B, S, D)
    edge_index = jnp.stack([src, dst])
    xn = _layernorm(x, axis=-1)
    x = x + _L0_gnn_ref(xn, edge_index, L0_gnn_W1, L0_gnn_b1, L0_gnn_W2, L0_gnn_b2) + _L0_mix_ref(xn[None], L0_mix_Wq, L0_mix_Wkv, L0_mix_Wproj, L0_mix_bproj)[0]
    x = x + _L0_ffn_ref(_layernorm(x, axis=-1)[None], L0_ffn_Wr, L0_ffn_br, L0_ffn_ln_g, L0_ffn_ln_b, L0_ffn_W1, L0_ffn_b1, L0_ffn_W2, L0_ffn_b2)[0]
    return x

_drawn_inputs = setup_inputs


def setup_inputs(seed=0):
    import zlib

    import numpy as np

    out = dict(_drawn_inputs(seed))
    spreads = {'L0_gnn_b1': (0.0, 0.1),
     'L0_gnn_b2': (0.0, 0.1),
     'L0_mix_bproj': (0.0, 0.1),
     'L0_ffn_br': (0.0, 0.1),
     'L0_ffn_ln_g': (1.0, 0.2),
     'L0_ffn_ln_b': (0.0, 0.1),
     'L0_ffn_b1': (0.0, 0.1),
     'L0_ffn_b2': (0.0, 0.1)}
    factors = {'L0_mix_Wq': 8.0, 'L0_mix_Wkv': 6.882, 'L0_mix_Wproj': 6.752}
    for name, (base, spread) in spreads.items():
        noise = np.random.default_rng([zlib.crc32(name.encode()), seed]).standard_normal(out[name].shape)
        drawn = base * np.exp(spread * noise) if base else spread * noise
        out[name] = jnp.asarray(drawn.astype(out[name].dtype))
    for name, factor in factors.items():
        out[name] = (out[name] * factor).astype(out[name].dtype)
    return out
```

```python
import concourse.bass as bass
from concourse import mybir
from contextlib import ExitStack

F32 = mybir.dt.float32
I32 = mybir.dt.int32
BF16 = mybir.dt.bfloat16
ALU = mybir.AluOpType
ACT = mybir.ActivationFunctionType
AX = mybir.AxisListType
DVE_ENGINE = mybir.EngineType.DVE
SP_ENGINE = mybir.EngineType.SP

P = 128
N, D, E = 6250, 256, 100000
NT = -(-N // P)
TAIL = N - (NT - 1) * P
ET = -(-E // P)
EPAD = ET * P - E
PAD_DST = 1 << 14
SPI = 17
STEPS = NT * SPI
assert STEPS >= ET + NT - 1
BLOCKS = NT + STEPS - (ET + NT - 1)
SG = -(-STEPS // P)
OFFROW = 20
HEADS, HD = 8, 32
NX, HID = 8, 1024
KC = D // P
HC = HID // P
TS = 256
FT = (2 * N + NX * (TS - 1)) // TS
DUMP = FT * TS
ZROWS = 4
ZDMAS = -(-(DUMP + 2 * P) // (P * ZROWS))
SLOTS = ZDMAS * P * ZROWS
PACK = KC * HID + HC * D + HC + 2 * KC + D
O_W2 = KC * HID
O_B1 = O_W2 + HC * D
O_G = O_B1 + HC
O_B = O_G + KC
O_B2 = O_B + KC
SP_P, SP_W = 125, 800
assert SP_P * SP_W == E
XCH = 7
LN_EPS = 1e-5
DEN_MIN = 1e-6
QSTAGE = [(0, 6), (6, 12), (12, SPI)]
PSB = 3


def gps_layer(nc, x, src, dst, wqkv, wproj, bproj, gw1, gb1, gw2, gb2, wr, br, experts, out):
    whole = ExitStack()
    sems = {}

    def sem(name):
        if name not in sems:
            sems[name] = whole.enter_context(nc.semaphore(name))
        return sems[name]

    def dram(name, shape, dt):
        return nc.dram_tensor(name, shape, dt, kind="Internal").ap()

    def sb(ctx, name, shape, dt=F32):
        return ctx.enter_context(nc.sbuf_tensor(name, shape, dt))

    def banks(ctx, n):
        return [ctx.enter_context(nc.psum_tensor(f"{ctx_name[0]}_bank{i}", [P, 512], F32)) for i in range(n)]

    ctx_name = ["p"]
    tallies = {}

    def link(eng, s, ins):
        tallies[s] = tallies.get(s, 0) + 1
        ins.then_inc(sem(s), 1)
        eng.wait_ge(sem(s), tallies[s])

    e_dst = dram("edges_dst", [ET * P, 1], I32)
    e_src = dram("edges_src", [ET * P, 1], I32)
    off_d = dram("step_offsets", [SG * P], I32)
    table = [dram(f"rows_layer{i}", [NT * P, D], F32) for i in range(2)]
    slots_x = dram("slots_x", [SLOTS, D], F32)
    slots_y = dram("slots_y", [FT * TS, D], F32)
    e_dst_rows = e_dst.rearrange("(t p) o -> t (p o)", p=P)
    e_src_rows = e_src.rearrange("(t p) o -> t (p o)", p=P)

    with whole, nc.allow_non_contiguous_dma("a few columns of one word"):
        node = sb(whole, "node", [P, NT, D])
        acc = sb(whole, "acc", [P, BLOCKS * D])
        accv = acc[:, 0:NT * D].rearrange("p (t d) -> p t d", d=D)
        ident = sb(whole, "ident", [P, P])
        ones = sb(whole, "ones", [P, P])
        dis = sb(whole, "dis", [P, NT])
        valid = sb(whole, "valid", [P, NT])
        w_qkv = sb(whole, "w_qkv", [P, KC, 3 * D])
        w_proj = sb(whole, "w_proj", [P, KC, D])
        w_g = [sb(whole, f"w_g{i}", [P, KC, D]) for i in range(2)]
        b_g = [sb(whole, f"b_g{i}", [P, D]) for i in range(2)]
        b_proj = sb(whole, "b_proj", [P, D])
        w_r = sb(whole, "w_r", [P, KC, NX])
        b_r = sb(whole, "b_r", [P, NX])
        pos_i = sb(whole, "pos_i", [P, 2, NT], I32)
        wts = sb(whole, "wts", [P, 2, NT])

        which_i = sb(whole, "which_i", [1, FT], I32)

        steps_ctx = ExitStack()
        iota_n = sb(steps_ctx, "iota_n", [P, P])
        dloc = sb(steps_ctx, "dloc", [P, SG * P])
        srcs = sb(steps_ctx, "srcs", [P, SG * P], I32)
        offs = sb(steps_ctx, "offs", [1, NT * OFFROW], I32)
        ctx_q = sb(steps_ctx, "ctx_q", [P, KC, D])
        ks_h = sb(steps_ctx, "ks_h", [P, KC, HEADS])
        hmask = sb(steps_ctx, "hmask", [P, KC, HEADS])
        zero = sb(steps_ctx, "zero", [P, ZROWS * D])

        with ExitStack() as ph:
            ctx_name[0] = "order"
            d_pm = sb(ph, "d_pm", [SP_P, SP_W + 1], I32)
            s_pm = sb(ph, "s_pm", [SP_P, SP_W], I32)
            b_i = sb(ph, "b_i", [SP_P, SP_W + 1], I32)
            b_f = sb(ph, "b_f", [SP_P, SP_W + 1])
            mask = sb(ph, "mask", [SP_P, SP_W])
            scan = sb(ph, "scan", [SP_P, SP_W])
            onesr = sb(ph, "onesr", [SP_P, SP_W])
            rank = sb(ph, "rank", [SP_P, SP_W])
            rank_i = sb(ph, "rank_i", [SP_P, SP_W], I32)
            tri = sb(ph, "tri", [P, P])
            bcur = sb(ph, "bcur", [SP_P, 1])
            base = sb(ph, "base", [SP_P, 1])
            shift = sb(ph, "shift", [SP_P, 1])
            viol = sb(ph, "viol", [SP_P, 1])
            flag = sb(ph, "flag", [1, 1], I32)
            padd = sb(ph, "padd", [1, EPAD], I32)
            pads = sb(ph, "pads", [1, EPAD], I32)
            ps = banks(ph, 2)
            with nc.Block() as block:
                @block.sync
                def _(sp):
                    sp.dma_start(e_dst[0:E, :].rearrange("(a b) o -> a (b o)", a=32),
                                 dst.rearrange("(a b) -> a b", a=32)).then_inc(sem("copy_d"), 16)
                    sp.dma_start(e_src[0:E, :].rearrange("(a b) o -> a (b o)", a=32),
                                 src.rearrange("(a b) -> a b", a=32)).then_inc(sem("copy_s"), 16)
                    sp.dma_start(d_pm[:, 0:SP_W], dst.rearrange("(p w) -> p w", w=SP_W)).then_inc(sem("dpm"), 16)
                    sp.wait_ge(sem("edge_mem"), 3)
                    sp.dma_start(d_pm[0:SP_P - 1, SP_W:SP_W + 1],
                                 dst.rearrange("(p w) -> p w", w=SP_W)[1:SP_P, 0:1]).then_inc(sem("dpm_next"), 16)
                    sp.dma_start(e_dst[E:ET * P, :].rearrange("n o -> o n"), padd[:, :]).then_inc(sem("pad_d"), 16)
                    sp.dma_start(e_src[E:ET * P, :].rearrange("n o -> o n"), pads[:, :]).then_inc(sem("pad_s"), 16)
                    for s in ("copy_d", "copy_s", "pad_d", "pad_s"):
                        sp.wait_ge(sem(s), 16)

                @block.gpsimd
                def _(pool):
                    pool.memset(ones[:, :], 1.0).then_inc(sem("consts"), 1)
                    pool.memset(ident[:, :], 0.0).then_inc(sem("consts"), 1)
                    pool.memset(onesr[:, :], 1.0).then_inc(sem("consts"), 1)
                    pool.memset(valid[:, :], 1.0).then_inc(sem("consts"), 1)
                    pool.memset(hmask[:, :, :], 1.0).then_inc(sem("consts"), 1)
                    pool.iota(iota_n[:, :], pattern=[[1, P]], base=0, channel_multiplier=0,
                              allow_small_or_imprecise_dtypes=True).then_inc(sem("consts"), 1)
                    pool.wait_ge(sem("consts"), 6)
                    pool.affine_select(out=ident[:, :], in_=ident[:, :], compare_op=ALU.not_equal, fill=1.0, base=0,
                                       pattern=[[-1, P]], channel_multiplier=1).then_inc(sem("consts"), 1)
                    pool.affine_select(out=tri[:, :], in_=ones[:, :], compare_op=ALU.is_gt, fill=0.0, base=0,
                                       pattern=[[1, P]], channel_multiplier=-1).then_inc(sem("consts"), 1)
                    pool.affine_select(out=valid[:, :], in_=valid[:, :], compare_op=ALU.is_gt, fill=0.0, base=N,
                                       pattern=[[-P, NT]], channel_multiplier=-1).then_inc(sem("consts"), 1)
                    pool.affine_select(out=hmask[:, :, :], in_=hmask[:, :, :], compare_op=ALU.is_ge, fill=0.0, base=0,
                                       pattern=[[P, KC], [-HD, HEADS]], channel_multiplier=1).then_inc(sem("consts"), 1)
                    pool.wait_ge(sem("consts"), 10)
                    pool.affine_select(out=hmask[:, :, :], in_=hmask[:, :, :], compare_op=ALU.is_gt, fill=0.0, base=HD,
                                       pattern=[[-P, KC], [HD, HEADS]], channel_multiplier=-1).then_inc(sem("consts"), 1)

                @block.vector
                def _(v):
                    v.memset(padd[:, :], PAD_DST).then_inc(sem("edge_mem"), 1)
                    v.memset(pads[:, :], 0).then_inc(sem("edge_mem"), 1)
                    v.memset(d_pm[:, SP_W:SP_W + 1], PAD_DST).then_inc(sem("edge_mem"), 1)
                    v.memset(zero[:, :], 0.0).then_inc(sem("zeroed"), 1)
                    v.wait_ge(sem("dpm"), 16)
                    v.wait_ge(sem("dpm_next"), 16)
                    link(v, "ord", v.tensor_scalar(b_i[:, :], d_pm[:, :], 7, None, ALU.arith_shift_right))
                    link(v, "ord", v.tensor_scalar(b_f[:, :], b_i[:, :], float(NT - 1), None, ALU.min))
                    link(v, "ord", v.tensor_tensor(mask[:, :], b_f[:, 0:SP_W], b_f[:, 1:SP_W + 1], ALU.is_gt))
                    v.tensor_reduce(viol[:, :], mask[:, :], AX.X, ALU.max).then_inc(sem("viol"), 1)
                    v.wait_ge(sem("viol_sum"), 1)
                    v.tensor_scalar(flag[:, :], ps[0][0:1, 0:1], 1.0, None, ALU.min).then_inc(sem("flag"), 1)

                @block.tensor
                def _(t):
                    t.wait_ge(sem("consts"), 11)
                    t.wait_ge(sem("viol"), 1)
                    t.matmul(ps[0][0:1, 0:1], viol[:, :], ones[0:SP_P, 0:1], start=True, stop=True).then_inc(sem("viol_sum"), 1)

            with nc.Block() as block:
                @block.sync
                def _(sp):
                    sp.dma_start(s_pm[:, :], src.rearrange("(p w) -> p w", w=SP_W)).then_inc(sem("spm"), 16)
                    sp.wait_ge(sem("spm"), 16)

                @block.vector
                def _(v):
                    unordered = v.value_load(flag[0:1, 0:1], min_val=0, max_val=1)
                    with v.If(unordered > 0):
                        link(v, "ord2", v.memset(bcur[:, :], 0.0))
                        link(v, "ord2", v.memset(base[:, :], -1.0))
                        link(v, "ord2", v.memset(rank[:, :], 0.0))
                        done = tallies["ord2"]
                        per = 7
                        with v.Fori(0, NT) as b:
                            n = b * per + done
                            v.tensor_scalar(mask[:, :], b_f[:, 0:SP_W], bcur[:, :], None, ALU.is_equal).then_inc(sem("ord2"), 1)
                            v.wait_ge(sem("ord2"), n + 1)
                            v.tensor_tensor_scan(scan[:, :], onesr[:, :], mask[:, :], 0.0, ALU.mult, ALU.add).then_inc(sem("ord2"), 1)
                            v.wait_ge(sem("ord2"), n + 2)
                            v.tensor_copy(viol[:, :], scan[:, SP_W - 1:SP_W]).then_inc(sem("ord_tot"), 1)
                            v.wait_ge(sem("ord_sum"), b + 1)
                            v.tensor_tensor(shift[:, :], ps[0][0:SP_P, 0:1], base[:, :], ALU.add).then_inc(sem("ord2"), 1)
                            v.wait_ge(sem("ord2"), n + 3)
                            v.scalar_tensor_tensor(scan[:, :], scan[:, :], shift[:, :], mask[:, :], ALU.add, ALU.mult).then_inc(sem("ord2"), 1)
                            v.wait_ge(sem("ord2"), n + 4)
                            v.tensor_tensor(rank[:, :], rank[:, :], scan[:, :], ALU.add).then_inc(sem("ord2"), 1)
                            v.tensor_tensor(base[:, :], base[:, :], ps[1][0:SP_P, 0:1], ALU.add).then_inc(sem("ord2"), 1)
                            v.tensor_scalar(bcur[:, :], bcur[:, :], 1.0, None, ALU.add).then_inc(sem("ord2"), 1)
                            v.wait_ge(sem("ord2"), n + per)
                        v.tensor_copy(rank_i[:, :], rank[:, :]).then_inc(sem("ranked"), 1)

                @block.tensor
                def _(t):
                    unordered = t.value_load(flag[0:1, 0:1], min_val=0, max_val=1)
                    with t.If(unordered > 0):
                        with t.Fori(0, NT) as b:
                            t.wait_ge(sem("ord_tot"), b + 1)
                            t.matmul(ps[0][0:SP_P, 0:1], tri[0:SP_P, 0:SP_P], viol[:, :], start=True, stop=True)
                            t.matmul(ps[1][0:SP_P, 0:1], ones[0:SP_P, 0:SP_P], viol[:, :], start=True, stop=True).then_inc(sem("ord_sum"), 1)

                @block.gpsimd
                def _(pool):
                    unordered = pool.value_load(flag[0:1, 0:1], min_val=0, max_val=1)
                    with pool.If(unordered > 0):
                        pool.wait_ge(sem("ranked"), 1)
                        pool.wait_ge(sem("spm"), 16)
                        with pool.Fori(0, SP_W) as j:
                            pool.tensor_copy(b_i[:, 0:1], rank_i[:, bass.ds(j, 1)]).then_inc(sem("ord_col"), 1)
                            pool.tensor_copy(b_i[:, 1:2], d_pm[:, bass.ds(j, 1)]).then_inc(sem("ord_col"), 1)
                            pool.tensor_copy(b_i[:, 2:3], s_pm[:, bass.ds(j, 1)]).then_inc(sem("ord_col"), 1)
                            pool.wait_ge(sem("ord_col"), j * 3 + 3)
                            pool.nop(nofuse=True)
                            pool.indirect_dma_start(e_dst, bass.IndirectOffsetOnAxis(ap=b_i[:, 0:1], axis=0),
                                                    b_i[:, 1:2], None).then_inc(sem("ord_dma"), 16)
                            pool.indirect_dma_start(e_src, bass.IndirectOffsetOnAxis(ap=b_i[:, 0:1], axis=0),
                                                    b_i[:, 2:3], None).then_inc(sem("ord_dma2"), 16)
                            pool.wait_ge(sem("ord_dma"), j * 16 + 16)
                            pool.wait_ge(sem("ord_dma2"), j * 16 + 16)

        with ExitStack() as ph:
            ctx_name[0] = "prep"
            first = sb(ph, "first", [1, ET], I32)
            first_b = sb(ph, "first_b", [1, ET], I32)
            tb = sb(ph, "tb", [1, ET])
            iota_t = sb(ph, "iota_t", [1, ET])
            tb_all = sb(ph, "tb_all", [P, ET])
            junk = sb(ph, "junk", [P, ET])
            s_no = sb(ph, "s_no", [P, SG])
            cnt = sb(ph, "cnt", [P, SG])
            t_i = sb(ph, "t_i", [P, SG], I32)
            b_s = sb(ph, "b_s", [P, SG])
            b_128 = sb(ph, "b_128", [P, SG])
            off_i = sb(ph, "off_i", [P, SG], I32)
            rows_i = sb(ph, "rows_i", [P, 2, SG, P], I32)
            rows_f = sb(ph, "rows_f", [P, 2, SG, P])
            iota_b = sb(ph, "iota_b", [P, P], BF16)
            ones_b = sb(ph, "ones_b", [P, 1], BF16)
            iota_k = sb(ph, "iota_k", [P, NT])
            onehot = [sb(ph, f"onehot{i}", [P, 9, P], BF16) for i in range(2)]
            cnt_n = sb(ph, "cnt_n", [P, SG * P])
            cnt_t = sb(ph, "cnt_t", [P, SG, P])
            bind = sb(ph, "bind", [P, SG, NT])
            stat = sb(ph, "stat", [P, NT, 6])
            mv = sb(ph, "mv", [P, NT, 2])
            rstd = sb(ph, "rstd", [P, NT])
            deg = sb(ph, "deg", [P, NT])
            ps = banks(ph, 6)
            cnt_ps = ph.enter_context(nc.psum_tensor("cnt_ps", [P, 1024], F32))
            H2 = ET // 2
            GRP = [(0, 9), (9, SPI)]
            with nc.Block() as block:
                @block.sync
                def _(sp):
                    with nc.allow_non_contiguous_dma("one word per row of edges"):
                        sp.dma_start(first[:, :], e_dst_rows[:, 0:1].rearrange("t o -> o t")).then_inc(sem("first"), 16)
                    for c in range(NT // XCH):
                        lo, n = c * XCH, XCH - (c == NT // XCH - 1)
                        sp.dma_start(node[:, lo:lo + n, :],
                                     x[lo * P:(lo + n) * P, :].rearrange("(t p) d -> p t d", p=P)).then_inc(sem("x_in"), 16)
                    sp.wait_ge(sem("tail0"), 1)
                    sp.dma_start(node[0:TAIL, NT - 1, :], x[(NT - 1) * P:N, :]).then_inc(sem("x_in"), 16)
                    sp.wait_ge(sem("off_i"), 1)
                    with nc.allow_non_contiguous_dma("small"):
                        sp.dma_start(off_d.rearrange("(g p) -> p g", p=P), off_i[:, :]).then_inc(sem("off_d"), 16)
                    sp.wait_ge(sem("off_d"), 16)
                    sp.dma_start(offs[:, :].rearrange("o (i k) -> o i k", k=OFFROW)[:, :, 0:SPI],
                                 off_d[0:STEPS].rearrange("(o i k) -> o i k", o=1, k=SPI)).then_inc(sem("offs"), 16)
                    sp.dma_start(w_qkv[:, :, :], wqkv.rearrange("(c p) n -> p c n", p=P)).then_inc(sem("weights"), 16)
                    sp.dma_start(w_proj[:, :, :], wproj.rearrange("(c p) n -> p c n", p=P)).then_inc(sem("weights"), 16)
                    for i, (w, b) in enumerate(((gw1, gb1), (gw2, gb2))):
                        sp.dma_start(w_g[i][:, :, :], w.rearrange("(c p) n -> p c n", p=P)).then_inc(sem("weights"), 16)
                        sp.dma_start(b_g[i][:, :], b[None, :].to_broadcast([P, D])).then_inc(sem("weights"), 16)
                    sp.dma_start(b_proj[:, :], bproj[None, :].to_broadcast([P, D])).then_inc(sem("weights"), 16)
                    with nc.allow_non_contiguous_dma("small"):
                        sp.dma_start(w_r[:, :, :], wr.rearrange("(c p) n -> p c n", p=P)).then_inc(sem("weights"), 16)
                        sp.dma_start(b_r[:, :], br[None, :].to_broadcast([P, NX])).then_inc(sem("weights"), 16)
                    sp.wait_ge(sem("offs"), 16)
                    sp.wait_ge(sem("weights"), 9 * 16)
                    for c in range(NT // XCH):
                        sp.wait_ge(sem("scaled"), (c + 1) * XCH)
                        sp.dma_start(table[0][c * XCH * P:(c + 1) * XCH * P, :].rearrange("(t p) d -> p t d", p=P),
                                     accv[:, c * XCH:(c + 1) * XCH, :]).then_inc(sem("tab0"), 16)
                    sp.wait_ge(sem("tab0"), NT // XCH * 16)

                @block.gpsimd
                def _(pool):
                    pool.iota(iota_t[:, :], pattern=[[1, ET]], base=0, channel_multiplier=0,
                              allow_small_or_imprecise_dtypes=True).then_inc(sem("prep_c"), 1)
                    pool.iota(s_no[:, :], pattern=[[P, SG]], base=0, channel_multiplier=1,
                              allow_small_or_imprecise_dtypes=True).then_inc(sem("prep_c"), 1)
                    pool.iota(iota_k[:, :], pattern=[[1, NT]], base=0, channel_multiplier=0,
                              allow_small_or_imprecise_dtypes=True).then_inc(sem("prep_c"), 1)
                    pool.memset(ones_b[:, :], 1.0).then_inc(sem("prep_c"), 1)
                    pool.memset(cnt_n[:, :], 0.0).then_inc(sem("prep_c"), 1)
                    pool.memset(acc[:, NT * D:BLOCKS * D], 0.0).then_inc(sem("prep_c"), 1)
                    pool.wait_ge(sem("t_i"), 1)
                    for g in range(SG):
                        at = bass.IndirectOffsetOnAxis(ap=t_i[:, g:g + 1], axis=0)
                        pool.indirect_dma_start(rows_i[:, 0, g, :], None, e_dst_rows, at).then_inc(sem("rows_i"), 16)
                    for g in range(SG):
                        at = bass.IndirectOffsetOnAxis(ap=t_i[:, g:g + 1], axis=0)
                        pool.indirect_dma_start(rows_i[:, 1, g, :], None, e_src_rows, at).then_inc(sem("rows_i"), 16)

                @block.vector
                def _(v):
                    v.memset(node[:, NT - 1, :], 0.0).then_inc(sem("tail0"), 1)
                    v.tensor_copy(iota_b[:, :], iota_n[:, :]).then_inc(sem("iota_b"), 1)
                    v.wait_ge(sem("first"), 16)
                    v.wait_ge(sem("prep_c"), 6)
                    link(v, "prp", v.tensor_scalar(first_b[:, :], first[:, :], 7, None, ALU.arith_shift_right))
                    link(v, "prp", v.tensor_scalar(tb[:, :], first_b[:, :], float(NT - 1), None, ALU.min))
                    v.tensor_tensor(tb[:, :], tb[:, :], iota_t[:, :], ALU.add).then_inc(sem("tb"), 1)
                    v.wait_ge(sem("tb_all"), 1)
                    v.tensor_copy(tb_all[:, 0:H2], ps[0][:, 0:H2]).then_inc(sem("prp"), 1)
                    tallies["prp"] += 1
                    link(v, "prp", v.tensor_copy(tb_all[:, H2:ET], ps[1][:, 0:ET - H2]))
                    for g in range(SG):
                        link(v, "prp", v.tensor_scalar(junk[:, :], tb_all[:, :], s_no[:, g:g + 1], 0.0, ALU.is_le, ALU.add,
                                                       accum_out=cnt[:, g:g + 1]))
                    v.tensor_scalar(t_i[:, :], cnt[:, :], -1.0, None, ALU.add).then_inc(sem("t_i"), 1)
                    link(v, "prp", v.scalar_tensor_tensor(b_s[:, :], s_no[:, :], 1.0, cnt[:, :], ALU.add, ALU.subtract))
                    v.tensor_scalar(off_i[:, :], b_s[:, :], float(D), None, ALU.mult).then_inc(sem("off_i"), 1)
                    link(v, "prp", v.tensor_scalar(b_128[:, :], b_s[:, :], float(P), None, ALU.mult))
                    for g in range(SG):
                        v.tensor_scalar(bind[:, g, :], iota_k[:, :], b_s[:, g:g + 1], None, ALU.is_equal).then_inc(sem("bind"), 1)
                    v.wait_ge(sem("rows_i"), 2 * SG * 16)
                    for g in range(SG):
                        v.tensor_scalar(rows_f[:, 0, g, :], rows_i[:, 0, g, :], b_128[:, g:g + 1], None,
                                        ALU.subtract).then_inc(sem("rows_f"), 1)
                    for g in range(SG):
                        v.tensor_copy(rows_f[:, 1, g, :], rows_i[:, 1, g, :]).then_inc(sem("rows_f"), 1)
                    v.wait_ge(sem("dloc"), 2)

                    def one_hots(i, is_first):
                        for h, (a, b) in enumerate(GRP):
                            if not is_first:
                                v.wait_ge(sem("counted"), i * 2 + h - 1)
                            v.tensor_tensor(onehot[h][:, 0:b - a, :], iota_b[:, None, :].to_broadcast([P, b - a, P]),
                                            dloc[:, bass.ds(i * SPI + a, b - a), None].to_broadcast([P, b - a, P]),
                                            ALU.is_equal).then_inc(sem("onehot"), 1)
                    one_hots(0, True)
                    with v.Fori(1, NT) as i:
                        one_hots(i, False)
                    v.wait_ge(sem("x_in"), (NT // XCH + 1) * 16)
                    with v.Fori(0, NT) as t:
                        v.bn_stats(stat[:, bass.ds(t, 1), :].rearrange("p o s -> p (o s)"),
                                   node[:, bass.ds(t, 1), :].rearrange("p o d -> p (o d)")).then_inc(sem("stat"), 1)
                    v.wait_ge(sem("stat"), NT)
                    for t in range(NT):
                        v.bn_aggr(mv[:, t, :], stat[:, t, :]).then_inc(sem("mv"), 1)
                    v.wait_ge(sem("mv"), NT)
                    v.tensor_scalar(rstd[:, :], mv[:, :, 1], LN_EPS, None, ALU.add).then_inc(sem("var"), 1)
                    v.wait_ge(sem("std"), 1)
                    link(v, "prp", v.reciprocal(rstd[:, :], rstd[:, :]))
                    with v.Fori(0, NT) as t:
                        row = node[:, bass.ds(t, 1), :].rearrange("p o d -> p (o d)")
                        v.tensor_scalar(row, row, mv[:, bass.ds(t, 1), 0], rstd[:, bass.ds(t, 1)],
                                        ALU.subtract, ALU.mult).then_inc(sem("normed"), 1)
                    v.wait_ge(sem("counted"), 2 * NT)
                    v.tensor_copy(cnt_n[:, 0:512], cnt_ps[:, 0:512]).then_inc(sem("cnt_n"), 1)
                    v.tensor_copy(cnt_n[:, 512:STEPS], cnt_ps[:, 512:STEPS]).then_inc(sem("cnt_n"), 1)
                    for j in range(2):
                        n = min(4, SG - 4 * j)
                        v.wait_ge(sem("cnt_tp"), j + 1)
                        v.tensor_copy(cnt_t[:, 4 * j:4 * j + n, :].rearrange("p g n -> p (g n)"),
                                      ps[j][:, 0:n * P]).then_inc(sem("cnt_t"), 1)
                    v.wait_ge(sem("deg"), 1)
                    v.tensor_scalar(deg[:, :], ps[2][:, 0:NT], 1.0, None, ALU.add).then_inc(sem("deg1"), 1)
                    v.wait_ge(sem("std"), 2)
                    v.reciprocal(dis[:, :], deg[:, :]).then_inc(sem("dis"), 1)

                @block.tensor
                def _(t):
                    t.wait_ge(sem("tb"), 1)
                    t.matmul(ps[0][:, 0:H2], ones[0:1, :], tb[:, 0:H2], start=True, stop=True)
                    t.matmul(ps[1][:, 0:ET - H2], ones[0:1, :], tb[:, H2:ET], start=True, stop=True).then_inc(sem("tb_all"), 1)
                    for which in range(2):
                        for g in range(SG):
                            t.wait_ge(sem("rows_f"), which * SG + g + 1)
                            ins = t.transpose(ps[2 + 2 * which + g // 4][:, g % 4 * P:g % 4 * P + P],
                                              rows_f[:, which, g, :], ident[:, :])
                            if g % 4 == 3 or g == SG - 1:
                                ins.then_inc(sem("rows_t"), 1)

                    def counts(i):
                        for h, (a, b) in enumerate(GRP):
                            t.wait_ge(sem("onehot"), i * 2 + h + 1)
                            for k in range(a, b):
                                ins = t.matmul(cnt_ps[:, bass.ds(i * SPI + k, 1)], onehot[h][:, k - a, :], ones_b[:, :],
                                               start=True, stop=True)
                            ins.then_inc(sem("counted"), 1)
                    with t.Fori(0, NT) as i:
                        counts(i)
                    t.wait_ge(sem("cnt_n"), 2)
                    for g in range(SG):
                        ins = t.transpose(ps[g // 4][:, g % 4 * P:g % 4 * P + P], cnt_n[:, g * P:(g + 1) * P], ident[:, :])
                        if g % 4 == 3 or g == SG - 1:
                            ins.then_inc(sem("cnt_tp"), 1)
                    t.wait_ge(sem("cnt_t"), 2)
                    t.wait_ge(sem("bind"), SG)
                    t.wait_ge(sem("dloc"), 2)
                    for g in range(SG):
                        ins = t.matmul(ps[2][:, 0:NT], cnt_t[:, g, :], bind[:, g, :], start=(g == 0), stop=(g == SG - 1))
                    ins.then_inc(sem("deg"), 1)

                @block.scalar
                def _(a):
                    for j in range(2):
                        n = min(4, SG - 4 * j) * P
                        a.wait_ge(sem("rows_t"), j + 1)
                        a.activation(dloc[:, j * 512:j * 512 + n], ps[2 + j][:, 0:n], ACT.Copy).then_inc(sem("dloc"), 1)
                    for j in range(2):
                        n = min(4, SG - 4 * j) * P
                        a.wait_ge(sem("rows_t"), j + 3)
                        a.activation(srcs[:, j * 512:j * 512 + n], ps[4 + j][:, 0:n], ACT.Copy).then_inc(sem("srcs"), 1)
                    a.wait_ge(sem("zeroed"), 1)
                    for z in range(ZDMAS):
                        a.dma_start(slots_x[z * P * ZROWS:(z + 1) * P * ZROWS, :].rearrange("(p r) d -> p (r d)", r=ZROWS),
                                    zero[:, :]).then_inc(sem("cleared"), 16)
                    a.wait_ge(sem("var"), 1)
                    a.activation(rstd[:, :], rstd[:, :], ACT.Sqrt).then_inc(sem("std"), 1)
                    a.wait_ge(sem("deg1"), 1)
                    a.activation(deg[:, :], deg[:, :], ACT.Sqrt).then_inc(sem("std"), 1)
                    a.wait_ge(sem("dis"), 1)
                    a.wait_ge(sem("normed"), NT)
                    with a.Fori(0, NT) as t:
                        a.activation(accv[:, bass.ds(t, 1), :].rearrange("p o d -> p (o d)"),
                                     node[:, bass.ds(t, 1), :].rearrange("p o d -> p (o d)"), ACT.Copy,
                                     scale=dis[:, bass.ds(t, 1)]).then_inc(sem("scaled"), 1)

        def turn(layer, i):
            return i + layer * NT

        def step_gathers(pool, layer, rows, i, is_first):
            for part, (a, b) in enumerate(QSTAGE):
                pool.wait_ge(sem("staged"), turn(layer, i) * len(QSTAGE) + part + 1)
                for k in range(a, b):
                    if not is_first:
                        pool.wait_ge(sem("summed"), turn(layer, i) * SPI + k + 1 - SPI)
                    pool.nop(nofuse=True)
                    pool.indirect_dma_start(rows[:, k, :], None, table[layer],
                                            bass.IndirectOffsetOnAxis(ap=stage[:, k:k + 1], axis=0)
                                            ).then_inc(sem(f"slot_{k}"), 16)

        def stage_indices(a, layer, i, is_first):
            for lo, hi in QSTAGE:
                if not is_first:
                    a.wait_ge(sem("summed"), turn(layer, i) * SPI + hi - SPI)
                a.activation(stage[:, lo:hi], srcs[:, bass.ds(i * SPI + lo, hi - lo)], ACT.Copy
                             ).then_inc(sem("staged"), 1)

        def step_select(v, layer, i, k, is_first):
            if not is_first:
                v.wait_ge(sem("summed"), turn(layer, i) * SPI + k + 1 - SPI)
            v.tensor_scalar(sel[:, k, :], iota_n[:, :], dloc[:, bass.ds(i * SPI + k, 1)], None,
                            ALU.is_equal).then_inc(sem("selected"), 1)

        def step_add(v, layer, i, k, off, is_first):
            v.wait_ge(sem("summed"), turn(layer, i) * SPI + k + 1)
            if not (is_first and k == 0):
                v.wait_ge(sem("added"), turn(layer, i) * SPI + k)
            to = acc[:, bass.ds(off, D)]
            v.tensor_tensor(to, to, step_ps[k % PSB][:, 0:D], ALU.add).then_inc(sem("added"), 1)

        def step_sum(t, layer, i, k, is_first):
            t.wait_ge(sem("selected"), turn(layer, i) * SPI + k + 1)
            t.wait_ge(sem(f"slot_{k}"), turn(layer, i) * 16 + 16)
            last = k - PSB if k >= PSB else max(j for j in range(SPI) if j % PSB == k % PSB) - SPI
            if not (is_first and k < PSB):
                t.wait_ge(sem("added"), turn(layer, i) * SPI + last + 1)
            t.matmul(step_ps[k % PSB][:, 0:D], sel[:, k, :], rows[:, k, :], start=True, stop=True
                     ).then_inc(sem("summed"), 1)

        def offsets(v, i):
            _, regs = nc.values_load_multi_w_load_instructions(
                offs[0:1, bass.ds(i * OFFROW, SPI)], engines=(DVE_ENGINE,), min_val=0, max_val=(BLOCKS - 1) * D,
                skip_runtime_bounds_check_because="the table holds blocks below BLOCKS")
            return regs

        def dense(ap):
            return ap.rearrange("p o d -> p (o d)")

        def tile(buf, t):
            return dense(buf[:, bass.ds(t, 1), :])

        with ExitStack() as ph:
            ctx_name[0] = "l0"
            stage = sb(ph, "stage0", [P, SPI], I32)
            rows = sb(ph, "rows0", [P, SPI, D])
            sel = sb(ph, "sel0", [P, SPI, P])
            xc = sb(ph, "xc0", [P, D])
            xt = sb(ph, "xt0", [P, KC, P])
            eq = sb(ph, "eq", [P, 2 * D])
            qk = sb(ph, "qk", [P, D])
            vv = sb(ph, "vv", [P, D])
            bk = banks(ph, 8)
            step_ps, ps_t, ps_q, ps_v, ps_c, ps_k = bk[0:3], bk[3], bk[4], bk[5], bk[6], bk[7]
            with nc.Block() as block:
                @block.gpsimd
                def _(pool):
                    step_gathers(pool, 0, rows, 0, True)
                    with pool.Fori(1, NT) as i:
                        step_gathers(pool, 0, rows, i, False)

                @block.scalar
                def _(a):
                    def one(i, is_first):
                        stage_indices(a, 0, i, is_first)
                        if not is_first:
                            a.wait_ge(sem("m_xt_ps"), i)
                        a.activation(xc[:, :], tile(node, i), ACT.Copy).then_inc(sem("m_xc"), 1)
                        a.wait_ge(sem("m_xt_ps"), i + 1)
                        a.activation(xt[:, :, :].rearrange("p c n -> p (c n)"), ps_t[:, 0:KC * P], ACT.Copy
                                     ).then_inc(sem("m_xt"), 1)
                        a.wait_ge(sem("m_qkv"), i + 1)
                        if not is_first:
                            a.wait_ge(sem("m_k"), i)
                        a.activation(eq[:, :], ps_q[:, :], ACT.Exp).then_inc(sem("m_exp"), 1)
                        if not is_first:
                            a.wait_ge(sem("m_kv"), i)
                        a.activation(vv[:, :], ps_v[:, 0:D], ACT.Copy).then_inc(sem("m_v"), 1)
                    one(0, True)
                    with a.Fori(1, NT) as i:
                        one(i, False)

                @block.vector
                def _(v):
                    def one(i, is_first):
                        off = offsets(v, i)
                        step_select(v, 0, i, 0, is_first)
                        for k in range(SPI):
                            if k + 1 < SPI:
                                step_select(v, 0, i, k + 1, is_first)
                            step_add(v, 0, i, k, off[k], is_first)
                            if k == 8:
                                v.wait_ge(sem("m_exp"), i + 1)
                                v.tensor_scalar(eq[:, :], eq[:, :], 1.0, None, ALU.min).then_inc(sem("m_min"), 1)
                                v.wait_ge(sem("m_min"), i + 1)
                                v.wait_ge(sem("m_xt_ps"), i + 1)
                                v.scalar_tensor_tensor(tile(node, i), ps_q[:, 0:D], 0.0, eq[:, 0:D],
                                                       ALU.max, ALU.add).then_inc(sem("m_q"), 1)
                                if not is_first:
                                    v.wait_ge(sem("m_kv"), i)
                                v.scalar_tensor_tensor(qk[:, :], ps_q[:, D:2 * D], 0.0, eq[:, D:2 * D],
                                                       ALU.max, ALU.add).then_inc(sem("m_k"), 1)
                    one(0, True)
                    with v.Fori(1, NT) as i:
                        one(i, False)
                    v.wait_ge(sem("m_closed"), 1)
                    for c in range(KC):
                        v.tensor_tensor(ctx_q[:, c, 0:P].rearrange("p (h d) -> p h d", d=HD),
                                        ps_c[:, c * P:(c + 1) * P].rearrange("p (h d) -> p h d", d=HD),
                                        hmask[:, c, 4 * c:4 * c + 4, None].to_broadcast([P, 4, HD]), ALU.mult
                                        ).then_inc(sem("ctx"), 1)
                        v.tensor_scalar(ks_h[:, c, :], hmask[:, c, :], ps_k[:, c:c + 1], None, ALU.mult
                                        ).then_inc(sem("ctx"), 1)

                @block.tensor
                def _(t):
                    t.wait_ge(sem("zeroed"), 1)
                    t.matmul(ps_c[:, 0:D], zero[:, 0:P], zero[:, 0:D], start=True, stop=False, skip_group_check=True)
                    t.matmul(ps_k[:, 0:KC], zero[:, 0:P], zero[:, 0:KC], start=True, stop=False, skip_group_check=True)

                    def one(i, is_first):
                        for k in range(SPI):
                            step_sum(t, 0, i, k, is_first)
                            if k == 0:
                                if not is_first:
                                    t.wait_ge(sem("m_xt"), i)
                                t.wait_ge(sem("m_xc"), i + 1)
                                for c in range(KC):
                                    ins = t.transpose(ps_t[:, c * P:(c + 1) * P], xc[:, c * P:(c + 1) * P], ident[:, :])
                                ins.then_inc(sem("m_xt_ps"), 1)
                            if k == 3:
                                t.wait_ge(sem("m_xt"), i + 1)
                                if not is_first:
                                    t.wait_ge(sem("m_k"), i)
                                    t.wait_ge(sem("m_v"), i)
                                for lo, n, to in ((0, 2 * D, ps_q), (2 * D, D, ps_v)):
                                    for c in range(KC):
                                        ins = t.matmul(to[:, 0:n], xt[:, c, :], w_qkv[:, c, lo:lo + n],
                                                       start=(c == 0), stop=(c == KC - 1))
                                ins.then_inc(sem("m_qkv"), 1)
                            if k == 13:
                                t.wait_ge(sem("m_k"), i + 1)
                                t.wait_ge(sem("m_v"), i + 1)
                                for c in range(KC):
                                    t.matmul(ps_c[:, c * P:(c + 1) * P], vv[:, c * P:(c + 1) * P], qk[:, c * P:(c + 1) * P],
                                             start=False, stop=False, skip_group_check=True)
                                    ins = t.matmul(ps_k[:, c:c + 1], qk[:, c * P:(c + 1) * P], valid[:, bass.ds(i, 1)],
                                                   start=False, stop=False, skip_group_check=True)
                                ins.then_inc(sem("m_kv"), 1)
                    one(0, True)
                    with t.Fori(1, NT) as i:
                        one(i, False)
                    t.matmul(ps_c[:, 0:D], zero[:, 0:P], zero[:, 0:D], start=False, stop=True, skip_group_check=True)
                    t.matmul(ps_k[:, 0:KC], zero[:, 0:P], zero[:, 0:KC], start=False, stop=True, skip_group_check=True
                             ).then_inc(sem("m_closed"), 1)

        def conv_scalar(a, layer):
            def one(t, is_first):
                if not is_first:
                    a.wait_ge(sem("c_t"), turn(layer, t))
                a.activation(sc[:, :], tile(accv, t), ACT.Copy, scale=dis[:, bass.ds(t, 1)]).then_inc(sem("c_sc"), 1)
                a.wait_ge(sem("c_t"), turn(layer, t) + 1)
                if not is_first:
                    a.wait_ge(sem("c_m"), turn(layer, t))
                a.activation(aggt[:, :, :].rearrange("p c n -> p (c n)"), ps_t[:, 0:KC * P], ACT.Copy
                             ).then_inc(sem("c_at"), 1)
                a.wait_ge(sem("c_z"), turn(layer, t) + 1)
                a.activation(ez[:, :], zz[:, :], ACT.Exp).then_inc(sem("c_e"), 1)
            one(0, True)
            with a.Fori(1, NT) as t:
                one(t, False)

        def conv_tensor(t_eng, layer, t, is_first):
            t_eng.wait_ge(sem("c_sc"), turn(layer, t) + 1)
            if not is_first:
                t_eng.wait_ge(sem("c_at"), turn(layer, t))
            for c in range(KC):
                ins = t_eng.transpose(ps_t[:, c * P:(c + 1) * P], sc[:, c * P:(c + 1) * P], ident[:, :])
            ins.then_inc(sem("c_t"), 1)
            t_eng.wait_ge(sem("c_at"), turn(layer, t) + 1)
            if not is_first:
                t_eng.wait_ge(sem("c_z"), turn(layer, t))
            for c in range(KC):
                ins = t_eng.matmul(ps_z[:, 0:D], aggt[:, c, :], w_g[layer][:, c, :], start=(c == 0), stop=(c == KC - 1))
            ins.then_inc(sem("c_m"), 1)

        def conv_vector(v, layer, hh, t, done):
            v.wait_ge(sem("c_m"), turn(layer, t) + 1)
            v.tensor_tensor(zz[:, :], ps_z[:, 0:D], b_g[layer][:, :], ALU.add).then_inc(sem("c_z"), 1)
            v.wait_ge(sem("c_e"), turn(layer, t) + 1)
            v.tensor_scalar(ez[:, :], ez[:, :], 1.0, -1.0, ALU.min, ALU.add).then_inc(sem("c_k"), 1)
            v.wait_ge(sem("c_k"), turn(layer, t) + 1)
            done(v.scalar_tensor_tensor(hh, zz[:, :], 0.0, ez[:, :], ALU.max, ALU.add))

        with ExitStack() as ph:
            ctx_name[0] = "c0"
            aggt = sb(ph, "aggt0", [P, KC, P])
            sc = sb(ph, "sc0", [P, D])
            zz = sb(ph, "zz0", [P, D])
            ez = sb(ph, "ez0", [P, D])
            hh = sb(ph, "hh0", [P, D])
            bk = banks(ph, 4)
            ps_t, ps_z, ps_m = bk[0], bk[1], bk[2]
            with nc.Block() as block:
                @block.sync
                def _(sp):
                    with sp.Fori(0, NT) as t:
                        sp.wait_ge(sem("c_s0"), t + 1)
                        sp.dma_start(table[1][bass.ds(t * P, P), :], tile(accv, t)).then_inc(sem("tab1"), 16)
                    sp.wait_ge(sem("tab1"), NT * 16)

                @block.tensor
                def _(t):
                    t.wait_ge(sem("ctx"), 2 * KC)
                    for c in range(KC):
                        ins = t.matmul(ps_m[:, c * D:(c + 1) * D], ctx_q[:, c, 0:P], w_proj[:, c, :], start=True, stop=True)
                    ins.then_inc(sem("ctx_w"), 1)
                    conv_tensor(t, 0, 0, True)
                    with t.Fori(1, NT) as i:
                        conv_tensor(t, 0, i, False)

                @block.scalar
                def _(a):
                    a.wait_ge(sem("ctx_w"), 1)
                    a.activation(ctx_q[:, :, :].rearrange("p c o -> p (c o)"), ps_m[:, :], ACT.Copy).then_inc(sem("ctx_s"), 1)
                    conv_scalar(a, 0)

                @block.vector
                def _(v):
                    with v.Fori(0, NT) as t:
                        conv_vector(v, 0, hh[:, :], t, lambda ins: ins.then_inc(sem("c_h0"), 1))
                        v.wait_ge(sem("c_h0"), t + 1)
                        v.tensor_scalar(tile(accv, t), hh[:, :], dis[:, bass.ds(t, 1)], None, ALU.mult).then_inc(sem("c_s0"), 1)

        with ExitStack() as ph:
            ctx_name[0] = "l1"
            stage = sb(ph, "stage1", [P, SPI], I32)
            rows = sb(ph, "rows1", [P, SPI, D])
            sel = sb(ph, "sel1", [P, SPI, P])
            qc = sb(ph, "qc", [P, D])
            qt = sb(ph, "qt", [P, KC, P])
            qdt = sb(ph, "qdt", [P, KC, P])
            qd = sb(ph, "qd", [P, D])
            xb = sb(ph, "xb", [P, D])
            den = sb(ph, "den", [P, HEADS])
            mixb = sb(ph, "mixb", [P, D])
            bk = banks(ph, 7)
            step_ps, ps_t, ps_d, ps_t2, ps_o = bk[0:3], bk[3], bk[4], bk[5], bk[6]
            with nc.Block() as block:
                @block.sync
                def _(sp):
                    def one(i, is_first, n):
                        if not is_first:
                            sp.wait_ge(sem("a_xadd"), i)
                        sp.dma_start(xb[0:n, :], x[bass.ds(i * P, n), :]).then_inc(sem("a_x"), 16)
                    one(0, True, P)
                    with sp.Fori(1, NT - 1) as i:
                        one(i, False, P)
                    sp.wait_ge(sem("a_xzero"), 1)
                    sp.dma_start(xb[0:TAIL, :], x[(NT - 1) * P:N, :]).then_inc(sem("a_x"), 16)
                    sp.wait_ge(sem("a_x"), NT * 16)

                @block.gpsimd
                def _(pool):
                    step_gathers(pool, 1, rows, 0, True)
                    with pool.Fori(1, NT) as i:
                        step_gathers(pool, 1, rows, i, False)

                @block.scalar
                def _(a):
                    def one(i, is_first):
                        stage_indices(a, 1, i, is_first)
                        if not is_first:
                            a.wait_ge(sem("a_t"), i)
                        a.activation(qc[:, :], tile(node, i), ACT.Copy).then_inc(sem("a_qc"), 1)
                        a.wait_ge(sem("a_t"), i + 1)
                        a.activation(qt[:, :, :].rearrange("p c n -> p (c n)"), ps_t[:, 0:KC * P], ACT.Copy
                                     ).then_inc(sem("a_qt"), 1)
                        a.wait_ge(sem("a_t2"), i + 1)
                        a.activation(qdt[:, :, :].rearrange("p c n -> p (c n)"), ps_t2[:, 0:KC * P], ACT.Copy
                                     ).then_inc(sem("a_qdt"), 1)
                        a.wait_ge(sem("a_o"), i + 1)
                        if not is_first:
                            a.wait_ge(sem("a_node"), i)
                        a.activation(mixb[:, :], ps_o[:, 0:D], ACT.Copy).then_inc(sem("a_mix"), 1)
                    one(0, True)
                    with a.Fori(1, NT) as i:
                        one(i, False)
                    a.wait_ge(sem("cleared"), ZDMAS * 16)

                @block.vector
                def _(v):
                    def one(i, is_first, is_last):
                        off = offsets(v, i)
                        if is_last:
                            v.wait_ge(sem("a_xadd"), NT - 1)
                            v.memset(xb[:, :], 0.0).then_inc(sem("a_xzero"), 1)
                        step_select(v, 1, i, 0, is_first)
                        for k in range(SPI):
                            if k + 1 < SPI:
                                step_select(v, 1, i, k + 1, is_first)
                            step_add(v, 1, i, k, off[k], is_first)
                            if k == 5:
                                v.wait_ge(sem("a_den"), i + 1)
                                v.tensor_scalar(den[:, :], ps_d[:, 0:HEADS], DEN_MIN, None, ALU.max).then_inc(sem("a_d1"), 1)
                                v.wait_ge(sem("a_d1"), i + 1)
                                v.reciprocal(den[:, :], den[:, :]).then_inc(sem("a_d2"), 1)
                                v.wait_ge(sem("a_d2"), i + 1)
                                if not is_first:
                                    v.wait_ge(sem("a_t2"), i)
                                v.tensor_tensor(qd[:, :].rearrange("p (h d) -> p h d", d=HD),
                                                tile(node, i).rearrange("p (h d) -> p h d", d=HD),
                                                den[:, :, None].to_broadcast([P, HEADS, HD]), ALU.mult
                                                ).then_inc(sem("a_qd"), 1)
                            if k == 14:
                                v.wait_ge(sem("a_x"), i * 16 + 16)
                                v.wait_ge(sem("a_qd"), i + 1)
                                v.wait_ge(sem("a_t"), i + 1)
                                v.tensor_tensor(tile(node, i), xb[:, :], b_proj[:, :], ALU.add).then_inc(sem("a_xadd"), 1)
                                v.wait_ge(sem("a_xadd"), i + 1)
                                v.wait_ge(sem("a_mix"), i + 1)
                                v.tensor_tensor(tile(node, i), tile(node, i), mixb[:, :], ALU.add).then_inc(sem("a_node"), 1)
                    one(0, True, False)
                    with v.Fori(1, NT - 1) as i:
                        one(i, False, False)
                    one(NT - 1, False, True)

                @block.tensor
                def _(t):
                    def one(i, is_first):
                        for k in range(SPI):
                            step_sum(t, 1, i, k, is_first)
                            if k == 0:
                                if not is_first:
                                    t.wait_ge(sem("a_qt"), i)
                                t.wait_ge(sem("a_qc"), i + 1)
                                for c in range(KC):
                                    ins = t.transpose(ps_t[:, c * P:(c + 1) * P], qc[:, c * P:(c + 1) * P], ident[:, :])
                                ins.then_inc(sem("a_t"), 1)
                            if k == 3:
                                t.wait_ge(sem("a_qt"), i + 1)
                                if not is_first:
                                    t.wait_ge(sem("a_d1"), i)
                                for c in range(KC):
                                    ins = t.matmul(ps_d[:, 0:HEADS], qt[:, c, :], ks_h[:, c, :], start=(c == 0), stop=(c == KC - 1))
                                ins.then_inc(sem("a_den"), 1)
                            if k == 8:
                                t.wait_ge(sem("a_qd"), i + 1)
                                if not is_first:
                                    t.wait_ge(sem("a_qdt"), i)
                                for c in range(KC):
                                    ins = t.transpose(ps_t2[:, c * P:(c + 1) * P], qd[:, c * P:(c + 1) * P], ident[:, :])
                                ins.then_inc(sem("a_t2"), 1)
                            if k == 11:
                                t.wait_ge(sem("a_qdt"), i + 1)
                                if not is_first:
                                    t.wait_ge(sem("a_mix"), i)
                                for c in range(KC):
                                    ins = t.matmul(ps_o[:, 0:D], qdt[:, c, :], ctx_q[:, c, :], start=(c == 0), stop=(c == KC - 1))
                                ins.then_inc(sem("a_o"), 1)
                    one(0, True)
                    with t.Fori(1, NT) as i:
                        one(i, False)
        steps_ctx.close()

        with ExitStack() as ph:
            ctx_name[0] = "route"
            aggt = sb(ph, "aggt1", [P, KC, P])
            sc = sb(ph, "sc1", [P, D])
            zz = sb(ph, "zz1", [P, D])
            ez = sb(ph, "ez1", [P, D])
            hh = sb(ph, "hh1", [P, D])
            stat = sb(ph, "statf", [P, 2, NT, 6])
            mv = sb(ph, "mvf", [P, 2, NT, 2])
            rstd = sb(ph, "rstdf", [P, 2, NT])
            xrc = sb(ph, "xrc", [P, D])
            xtt = sb(ph, "xtt", [P, KC, P])
            lg = sb(ph, "lg", [P, NT, NX])
            tri = sb(ph, "trif", [P, P])
            rev = sb(ph, "rev", [P, NX])
            keep = sb(ph, "keep", [P, NX, NT])
            dumpp = sb(ph, "dumpp", [P, 2, NT])
            starts = sb(ph, "starts", [1, FT])
            ea, eb, ec = (sb(ph, f"route_{n}", [P, NT, NX]) for n in "abc")
            oh = [sb(ph, f"oh{i}", [P, NT, NX]) for i in range(2)]
            top = sb(ph, "top", [P, 2, NT])
            small = sb(ph, "small", [P, NT])
            tot = sb(ph, "tot", [P, NX, NT])
            incl = sb(ph, "incl", [P, NX, NT])
            n_f = sb(ph, "n_f", [P, NX])
            n_i = sb(ph, "n_i", [P, NX], I32)
            st = sb(ph, "st", [P, NX])
            one8 = sb(ph, "one8", [P, NX])
            ge = sb(ph, "ge", [1, FT, NX])
            which = sb(ph, "which", [1, FT])
            bk = banks(ph, 5)
            ps_t, ps_z, ps_l, ps_a, ps_b = bk
            with nc.Block() as block:
                @block.gpsimd
                def _(pool):
                    pool.iota(rev[:, :], pattern=[[-1, NX]], base=NX, channel_multiplier=0,
                              allow_small_or_imprecise_dtypes=True).then_inc(sem("f_c"), 1)
                    pool.iota(starts[:, :], pattern=[[TS, FT]], base=0, channel_multiplier=0,
                              allow_small_or_imprecise_dtypes=True).then_inc(sem("f_c"), 1)
                    pool.memset(keep[:, :, :], 1.0).then_inc(sem("f_c"), 1)
                    pool.memset(one8[:, :], 1.0).then_inc(sem("f_c"), 1)
                    pool.iota(dumpp[:, :, :], pattern=[[P, 2], [0, NT]], base=DUMP, channel_multiplier=1,
                              allow_small_or_imprecise_dtypes=True).then_inc(sem("f_c"), 1)
                    pool.affine_select(out=tri[:, :], in_=ones[:, :], compare_op=ALU.is_gt, fill=0.0, base=0,
                                       pattern=[[1, P]], channel_multiplier=-1).then_inc(sem("f_c"), 1)
                    pool.wait_ge(sem("f_c"), 6)
                    pool.affine_select(out=keep[:, :, :], in_=keep[:, :, :], compare_op=ALU.not_equal, fill=0.0, base=0,
                                       pattern=[[0, NX], [1, NT]], channel_multiplier=0).then_inc(sem("f_c"), 1)
                    pool.affine_select(out=dumpp[:, :, :], in_=dumpp[:, :, :], compare_op=ALU.is_ge, fill=0.0, base=-N,
                                       pattern=[[0, 2], [P, NT]], channel_multiplier=1).then_inc(sem("f_c"), 1)
                    pool.wait_ge(sem("f_pos"), 2)
                    for t in range(NT):
                        pool.wait_ge(sem("f_xn2"), t + 1)
                        for j in range(2):
                            pool.indirect_dma_start(slots_x, bass.IndirectOffsetOnAxis(ap=pos_i[:, j, t:t + 1], axis=0),
                                                    accv[:, t, :], None).then_inc(sem(f"f_sc{j}"), 16)
                    for j in range(2):
                        pool.wait_ge(sem(f"f_sc{j}"), NT * 16)

                @block.scalar
                def _(a):
                    conv_scalar(a, 1)
                    a.wait_ge(sem("f_var"), 1)
                    a.activation(rstd[:, 0, :], rstd[:, 0, :], ACT.Sqrt).then_inc(sem("f_std"), 1)
                    def route_copies(t, is_first):
                        a.wait_ge(sem("f_xt"), t + 1)
                        if not is_first:
                            a.wait_ge(sem("f_t"), t)
                        a.activation(xrc[:, :], tile(accv, t), ACT.Copy).then_inc(sem("f_xrc"), 1)
                        a.wait_ge(sem("f_t"), t + 1)
                        if not is_first:
                            a.wait_ge(sem("f_l"), t)
                        a.activation(xtt[:, :, :].rearrange("p c n -> p (c n)"), ps_a[:, 0:KC * P], ACT.Copy
                                     ).then_inc(sem("f_xtt"), 1)
                    route_copies(0, True)
                    with a.Fori(1, NT) as t:
                        route_copies(t, False)
                    a.wait_ge(sem("f_var"), 2)
                    a.activation(rstd[:, 1, :], rstd[:, 1, :], ACT.Sqrt).then_inc(sem("f_std"), 1)
                    a.wait_ge(sem("f_lmax"), 1)
                    a.activation(ea[:, :, :], ea[:, :, :], ACT.Exp).then_inc(sem("f_exp"), 1)

                @block.tensor
                def _(t):
                    conv_tensor(t, 1, 0, True)
                    with t.Fori(1, NT) as i:
                        conv_tensor(t, 1, i, False)

                    def route(i, is_first):
                        t.wait_ge(sem("f_xrc"), i + 1)
                        if not is_first:
                            t.wait_ge(sem("f_xtt"), i)
                        for c in range(KC):
                            ins = t.transpose(ps_a[:, c * P:(c + 1) * P], xrc[:, c * P:(c + 1) * P], ident[:, :])
                        ins.then_inc(sem("f_t"), 1)
                        t.wait_ge(sem("f_xtt"), i + 1)
                        for c in range(KC):
                            ins = t.matmul(ps_l[:, bass.ds(i * NX, NX)], xtt[:, c, :], w_r[:, c, :], start=(c == 0), stop=(c == KC - 1))
                        ins.then_inc(sem("f_l"), 1)
                    route(0, True)
                    with t.Fori(1, NT) as i:
                        route(i, False)
                    t.wait_ge(sem("f_m"), 1)
                    t.wait_ge(sem("f_c"), 6)
                    m = ec[:, :, :].rearrange("p t e -> p (t e)")
                    t.matmul(ps_a[:, 0:NT * NX], tri[:, :], m, start=True, stop=True)
                    t.matmul(ps_b[:, 0:NT * NX], ones[:, :], m, start=True, stop=True).then_inc(sem("f_cnt"), 1)

                @block.vector
                def _(v):
                    def b8(ap):
                        return ap[:, :, None].to_broadcast([P, NT, NX])

                    def b49(ap):
                        return ap[:, None, :].to_broadcast([P, NT, NX])
                    with v.Fori(0, NT) as t:
                        conv_vector(v, 1, hh[:, :], t, lambda ins: ins.then_inc(sem("f_h"), 1))
                        v.wait_ge(sem("f_h"), t + 1)
                        v.tensor_tensor(tile(node, t), tile(node, t), hh[:, :], ALU.add).then_inc(sem("f_x2"), 1)
                        v.wait_ge(sem("f_x2"), t + 1)
                        v.bn_stats(dense(stat[:, 0, bass.ds(t, 1), :]), tile(node, t)).then_inc(sem("f_s1"), 1)
                    v.wait_ge(sem("f_s1"), NT)
                    for t in range(NT):
                        v.bn_aggr(mv[:, 0, t, :], stat[:, 0, t, :]).then_inc(sem("f_s1"), 1)
                    v.wait_ge(sem("f_s1"), 2 * NT)
                    v.tensor_scalar(rstd[:, 0, :], mv[:, 0, :, 1], LN_EPS, None, ALU.add).then_inc(sem("f_var"), 1)
                    v.wait_ge(sem("f_std"), 1)
                    link(v, "f_v", v.reciprocal(rstd[:, 0, :], rstd[:, 0, :]))
                    with v.Fori(0, NT) as t:
                        v.tensor_scalar(tile(accv, t), tile(node, t), mv[:, 0, bass.ds(t, 1), 0], rstd[:, 0, bass.ds(t, 1)],
                                        ALU.subtract, ALU.mult).then_inc(sem("f_xt"), 1)
                        v.wait_ge(sem("f_xt"), t + 1)
                        v.bn_stats(dense(stat[:, 1, bass.ds(t, 1), :]), tile(accv, t)).then_inc(sem("f_s2"), 1)
                    v.wait_ge(sem("f_s2"), NT)
                    for t in range(NT):
                        v.bn_aggr(mv[:, 1, t, :], stat[:, 1, t, :]).then_inc(sem("f_s2"), 1)
                    v.wait_ge(sem("f_s2"), 2 * NT)
                    v.tensor_scalar(rstd[:, 1, :], mv[:, 1, :, 1], LN_EPS, None, ALU.add).then_inc(sem("f_var"), 1)
                    v.wait_ge(sem("f_l"), NT)
                    link(v, "f_v", v.tensor_tensor(lg[:, :, :], ps_l[:, 0:NT * NX].rearrange("p (t e) -> p t e", e=NX),
                                                   b49(b_r[:, :]), ALU.add))
                    link(v, "f_v", v.tensor_reduce(small[:, :], lg[:, :, :], AX.X, ALU.max))
                    v.tensor_tensor(ea[:, :, :], lg[:, :, :], b8(small[:, :]), ALU.subtract).then_inc(sem("f_lmax"), 1)
                    v.wait_ge(sem("f_std"), 2)
                    link(v, "f_v", v.reciprocal(rstd[:, 1, :], rstd[:, 1, :]))
                    v.wait_ge(sem("f_exp"), 1)
                    link(v, "f_v", v.tensor_reduce(small[:, :], ea[:, :, :], AX.X, ALU.add))
                    link(v, "f_v", v.reciprocal(small[:, :], small[:, :]))
                    link(v, "f_v", v.tensor_tensor(ea[:, :, :], ea[:, :, :], b8(small[:, :]), ALU.mult))
                    v.wait_ge(sem("f_c"), 8)
                    for j in range(2):
                        link(v, "f_v", v.tensor_reduce(top[:, j, :], ea[:, :, :], AX.X, ALU.max))
                        link(v, "f_v", v.tensor_tensor(eb[:, :, :], ea[:, :, :], b8(top[:, j, :]), ALU.is_equal))
                        link(v, "f_v", v.tensor_tensor(eb[:, :, :], eb[:, :, :], b49(rev[:, :]), ALU.mult))
                        link(v, "f_v", v.tensor_reduce(small[:, :], eb[:, :, :], AX.X, ALU.max))
                        link(v, "f_v", v.tensor_tensor(oh[j][:, :, :], eb[:, :, :], b8(small[:, :]), ALU.is_equal))
                        if j == 0:
                            link(v, "f_v", v.scalar_tensor_tensor(
                                ea[:, :, :].rearrange("p t e -> p (t e)"), oh[0][:, :, :].rearrange("p t e -> p (t e)"), -4.0,
                                ea[:, :, :].rearrange("p t e -> p (t e)"), ALU.mult, ALU.add))
                    link(v, "f_v", v.tensor_tensor(small[:, :], top[:, 0, :], top[:, 1, :], ALU.add))
                    link(v, "f_v", v.reciprocal(small[:, :], small[:, :]))
                    for j in range(2):
                        v.tensor_tensor(wts[:, j, :], top[:, j, :], small[:, :], ALU.mult).then_inc(sem("f_w"), 1)
                    link(v, "f_v", v.tensor_tensor(ec[:, :, :], oh[0][:, :, :], oh[1][:, :, :], ALU.add))
                    v.tensor_tensor(ec[:, :, :], ec[:, :, :], b8(valid[:, :]), ALU.mult).then_inc(sem("f_m"), 1)
                    v.wait_ge(sem("f_cnt"), 1)
                    link(v, "f_v", v.tensor_copy(tot[:, :, :], ps_b[:, 0:NT * NX].rearrange("p (t e) -> p e t", e=NX)))
                    flat = "p e t -> p (e t)"
                    link(v, "f_v", v.tensor_tensor_scan(incl[:, :, :].rearrange(flat), keep[:, :, :].rearrange(flat),
                                                        tot[:, :, :].rearrange(flat), 0.0, ALU.mult, ALU.add))
                    link(v, "f_v", v.tensor_scalar(n_f[:, :], incl[:, :, NT - 1], float(TS - 1), None, ALU.add))
                    link(v, "f_v", v.tensor_copy(n_i[:, :], n_f[:, :]))
                    link(v, "f_v", v.tensor_scalar(n_i[:, :], n_i[:, :], -TS, None, ALU.bitwise_and))
                    link(v, "f_v", v.tensor_copy(n_f[:, :], n_i[:, :]))
                    link(v, "f_v", v.tensor_tensor_scan(st[:, :], one8[:, :], n_f[:, :], 0.0, ALU.mult, ALU.add))
                    link(v, "f_v", v.tensor_tensor(st[:, :], st[:, :], n_f[:, :], ALU.subtract))
                    link(v, "f_v", v.tensor_tensor(ge[:, :, :], st[0:1, None, :].to_broadcast([1, FT, NX]),
                                                   starts[:, :, None].to_broadcast([1, FT, NX]), ALU.is_le))
                    link(v, "f_v", v.tensor_reduce(which[:, :], ge[:, :, :], AX.X, ALU.add))
                    v.tensor_scalar(which_i[:, :], which[:, :], float(P), float(-P), ALU.mult, ALU.add).then_inc(sem("f_which"), 1)
                    link(v, "f_v", v.tensor_tensor(incl[:, :, :], incl[:, :, :], tot[:, :, :], ALU.subtract))
                    link(v, "f_v", v.tensor_tensor(incl[:, :, :], incl[:, :, :], st[:, :, None].to_broadcast([P, NX, NT]), ALU.add))
                    link(v, "f_v", v.tensor_tensor(ea[:, :, :], ps_a[:, 0:NT * NX].rearrange("p (t e) -> p t e", e=NX),
                                                   incl[:, :, :].rearrange("p e t -> p t e"), ALU.add))
                    for j in range(2):
                        link(v, "f_v", v.tensor_tensor(eb[:, :, :], ea[:, :, :], oh[j][:, :, :], ALU.mult))
                        link(v, "f_v", v.tensor_reduce(small[:, :], eb[:, :, :], AX.X, ALU.add))
                        link(v, "f_v", v.tensor_tensor(small[:, :], small[:, :], valid[:, :], ALU.mult))
                        v.tensor_tensor(pos_i[:, j, :], small[:, :], dumpp[:, j, :], ALU.add).then_inc(sem("f_pos"), 1)
                        v.wait_ge(sem("f_pos"), j + 1)
                    v.wait_ge(sem("f_t"), NT)
                    with v.Fori(0, NT) as t:
                        v.tensor_scalar(tile(accv, t), tile(accv, t), mv[:, 1, bass.ds(t, 1), 0], rstd[:, 1, bass.ds(t, 1)],
                                        ALU.subtract, ALU.mult).then_inc(sem("f_xn2"), 1)

        with ExitStack() as ph:
            ctx_name[0] = "ffn"
            wb = [sb(ph, f"wb{i}", [P, PACK]) for i in range(2)]
            xr = [sb(ph, f"xr{i}", [P, 2, D]) for i in range(2)]
            xe = sb(ph, "xe", [P, KC, TS])
            ht = [sb(ph, f"ht{i}", [P, HC, TS]) for i in range(2)]
            ys = [sb(ph, f"ys{i}", [P, 2, D]) for i in range(2)]
            bk = banks(ph, 6)
            ps_x, ps_h, ps_y = bk[0], bk[1:5], bk[5]
            x_tiles = slots_x[0:FT * TS, :].rearrange("(n h p) d -> n p h d", h=2, p=P)
            y_tiles = slots_y.rearrange("(n h p) d -> n p h d", h=2, p=P)

            def pairs(eng, body):
                body(0, 0, True)
                body(1, 1, True)
                with eng.Fori(1, FT // 2) as n:
                    body(n * 2, 0, False)
                    body(n * 2 + 1, 1, False)

            with nc.Block() as block:
                @block.sync
                def _(sp):
                    def one(n, q, is_first):
                        row = sp.value_load(which_i[0:1, bass.ds(n, 1)], min_val=0, max_val=(NX - 1) * P)
                        if not is_first:
                            sp.wait_ge(sem("e_y"), n - 1)
                            sp.wait_ge(sem("e_ys"), n - 1)
                        sp.dma_start(wb[q][:, :], experts[bass.ds(row, P), :]).then_inc(sem(f"load_{q}"), 16)
                        sp.dma_start(xr[q][:, :, :], x_tiles[bass.ds(n, 1), :, :, :].rearrange("o p h d -> (o p) h d")
                                     ).then_inc(sem(f"load_{2 + q}"), 16)
                    pairs(sp, one)

                @block.scalar
                def _(a):
                    def one(n, q, is_first):
                        half = (n if isinstance(n, int) else n) - q
                        a.wait_ge(sem(f"load_{q}"), half * 8 + 16)
                        a.wait_ge(sem("e_t"), n + 1)
                        if not (is_first and q == 0):
                            a.wait_ge(sem("e_h"), n * HC)
                        for c in range(KC):
                            a.activation(xe[:, c, :], ps_x[:, c * TS:(c + 1) * TS], ACT.Identity,
                                         scale=wb[q][:, O_G + c:O_G + c + 1], bias=wb[q][:, O_B + c:O_B + c + 1]
                                         ).then_inc(sem("e_xe"), 1)
                        if not is_first:
                            a.wait_ge(sem("e_y"), n - 1)
                        for m in range(HC):
                            a.wait_ge(sem("e_h"), n * HC + m + 1)
                            a.activation(ht[q][:, m, :], ps_h[m % 4][:, 0:TS], ACT.Gelu,
                                         bias=wb[q][:, O_B1 + m:O_B1 + m + 1]).then_inc(sem("e_g"), 1)
                    pairs(a, one)

                @block.vector
                def _(v):
                    def one(n, q, is_first):
                        v.wait_ge(sem("e_y"), n + 1)
                        if not is_first:
                            v.wait_ge(sem(f"e_st{q}"), (n - q) * 8)
                        v.tensor_tensor(ys[q][:, :, :], ps_y[:, :].rearrange("p (h d) -> p h d", h=2),
                                        wb[q][:, None, O_B2:O_B2 + D].to_broadcast([P, 2, D]), ALU.add
                                        ).then_inc(sem("e_ys"), 1)
                    pairs(v, one)

                @block.gpsimd
                def _(pool):
                    def one(n, q, is_first):
                        pool.wait_ge(sem("e_ys"), n + 1)
                        pool.nop(nofuse=True)
                        pool.dma_start(y_tiles[bass.ds(n, 1), :, :, :].rearrange("o p h d -> (o p) h d"), ys[q][:, :, :]
                                       ).then_inc(sem(f"e_st{q}"), 16)
                    pairs(pool, one)
                    for q in range(2):
                        pool.wait_ge(sem(f"e_st{q}"), FT * 8)

                @block.tensor
                def _(t):
                    def transposes(n, q, is_first):
                        t.wait_ge(sem(f"load_{2 + q}"), (n - q) * 8 + 16)
                        if not (is_first and q == 0):
                            t.wait_ge(sem("e_xe"), n * KC)
                        for h in range(2):
                            for c in range(KC):
                                ins = t.transpose(ps_x[:, c * TS + h * P:c * TS + (h + 1) * P],
                                                  xr[q][:, h, c * P:(c + 1) * P], ident[:, :])
                        ins.then_inc(sem("e_t"), 1)

                    def hidden(n, q, is_first):
                        t.wait_ge(sem("e_xe"), n * KC + KC)
                        t.wait_ge(sem(f"load_{q}"), (n - q) * 8 + 16)
                        for m in range(HC):
                            if not (is_first and q == 0 and m < 4):
                                t.wait_ge(sem("e_g"), n * HC + m - 3)
                            for c in range(KC):
                                ins = t.matmul(ps_h[m % 4][:, 0:TS], wb[q][:, c * HID + m * P:c * HID + (m + 1) * P],
                                               xe[:, c, :], start=(c == 0), stop=(c == KC - 1))
                            ins.then_inc(sem("e_h"), 1)
                            if m == HC - 1:
                                pass
                        return ins

                    def output(n, q, is_first):
                        if not (is_first and q == 0):
                            t.wait_ge(sem("e_ys"), n)
                        for h in range(2):
                            for m in range(HC):
                                if h == 0:
                                    t.wait_ge(sem("e_g"), n * HC + m + 1)
                                ins = t.matmul(ps_y[:, h * D:(h + 1) * D], ht[q][:, m, h * P:(h + 1) * P],
                                               wb[q][:, O_W2 + m * D:O_W2 + (m + 1) * D], start=(m == 0), stop=(m == HC - 1))
                        ins.then_inc(sem("e_y"), 1)

                    def one(n, q, is_first, is_last=False):
                        hidden(n, q, is_first)
                        if not is_last:
                            transposes(n + 1, 1 - q, is_first)
                        output(n, q, is_first)

                    transposes(0, 0, True)
                    one(0, 0, True)
                    hidden(1, 1, True)
                    transposes(2, 0, False)
                    output(1, 1, True)
                    with t.Fori(1, FT // 2 - 1) as n:
                        one(n * 2, 0, False)
                        one(n * 2 + 1, 1, False)
                    one(FT - 2, 0, False)
                    one(FT - 1, 1, False, True)

        with ExitStack() as ph:
            ctx_name[0] = "comb"
            GB = 4
            yg = sb(ph, "yg", [P, GB, 2, D])
            ob = sb(ph, "ob", [P, GB, D])
            with nc.Block() as block:
                @block.gpsimd
                def _(pool):
                    for t in range(NT):
                        if t >= GB:
                            pool.wait_ge(sem("o_2"), t - GB + 1)
                        for j in range(2):
                            idx = pos_i[:, j, t:t + 1] if t < NT - 1 else pos_i[0:TAIL, j, t:t + 1]
                            n = P if t < NT - 1 else TAIL
                            pool.indirect_dma_start(yg[0:n, t % GB, j, :], None, slots_y,
                                                    bass.IndirectOffsetOnAxis(ap=idx, axis=0)
                                                    ).then_inc(sem(f"slot_{t % GB * 2 + j}"), 16)

                @block.vector
                def _(v):
                    for t in range(NT):
                        n = P if t < NT - 1 else TAIL
                        g = t % GB
                        if t >= GB:
                            v.wait_ge(sem(f"load_{g}"), FT * 8 + t // GB * 16)
                        v.wait_ge(sem(f"slot_{g * 2}"), (turn(2, 0) + t // GB + 1) * 16)
                        v.scalar_tensor_tensor(ob[0:n, g, :], yg[0:n, g, 0, :], wts[0:n, 0, t:t + 1], node[0:n, t, :],
                                               ALU.mult, ALU.add).then_inc(sem("o_1"), 1)
                        v.wait_ge(sem("o_1"), t + 1)
                        v.wait_ge(sem(f"slot_{g * 2 + 1}"), (turn(2, 0) + t // GB + 1) * 16)
                        v.scalar_tensor_tensor(ob[0:n, g, :], yg[0:n, g, 1, :], wts[0:n, 1, t:t + 1], ob[0:n, g, :],
                                               ALU.mult, ALU.add).then_inc(sem("o_2"), 1)

                @block.sync
                def _(sp):
                    for t in range(NT):
                        n = P if t < NT - 1 else TAIL
                        sp.wait_ge(sem("o_2"), t + 1)
                        sp.dma_start(out[t * P:t * P + n, :], ob[0:n, t % GB, :]).then_inc(sem(f"load_{t % GB}"), 16)
                    for g in range(GB):
                        sp.wait_ge(sem(f"load_{g}"), FT * 8 + len(range(g, NT, GB)) * 16)


def _layout(inputs):
    import numpy as np
    f = {k: np.ascontiguousarray(v) for k, v in inputs.items()}
    rows = [
        f["L0_ffn_W1"].reshape(NX, KC, P, HID).transpose(0, 2, 1, 3).reshape(NX * P, KC * HID),
        f["L0_ffn_W2"].reshape(NX, HC, P, D).transpose(0, 2, 1, 3).reshape(NX * P, HC * D),
        f["L0_ffn_b1"].reshape(NX, HC, P).transpose(0, 2, 1).reshape(NX * P, HC),
        f["L0_ffn_ln_g"].reshape(NX, KC, P).transpose(0, 2, 1).reshape(NX * P, KC),
        f["L0_ffn_ln_b"].reshape(NX, KC, P).transpose(0, 2, 1).reshape(NX * P, KC),
        np.repeat(f["L0_ffn_b2"], P, axis=0),
    ]
    return {
        "x": f["x"], "src": f["src"], "dst": f["dst"],
        "wqkv": np.concatenate([f["L0_mix_Wq"].T, f["L0_mix_Wkv"].T], axis=1),
        "wproj": np.ascontiguousarray(f["L0_mix_Wproj"].T), "bproj": f["L0_mix_bproj"],
        "gw1": f["L0_gnn_W1"], "gb1": f["L0_gnn_b1"], "gw2": f["L0_gnn_W2"], "gb2": f["L0_gnn_b2"],
        "wr": f["L0_ffn_Wr"], "br": f["L0_ffn_br"],
        "experts": np.concatenate(rows, axis=1),
    }


def kernel(**inputs):
    import numpy as np
    import concourse.bacc as bacc
    from concourse.bass_utils import run_bass_kernel_spmd

    arrays = _layout(inputs)
    nc = bacc.Bacc("TRN2", target_bir_lowering=False, num_devices=1)
    args = [nc.dram_tensor(name, a.shape, mybir.dt.from_np(a.dtype), kind="ExternalInput").ap()
            for name, a in arrays.items()]
    out = nc.dram_tensor("out", (N, D), F32, kind="ExternalOutput").ap()
    gps_layer(nc, *args, out)
    r = run_bass_kernel_spmd(nc, [arrays], core_ids=[0])
    return r.results[0]["out"]
```

```python
import concourse.bass as bass
from concourse import mybir
from contextlib import ExitStack

F32 = mybir.dt.float32
F32R = mybir.dt.float32r
I32 = mybir.dt.int32
BF16 = mybir.dt.bfloat16
ALU = mybir.AluOpType
ACT = mybir.ActivationFunctionType
AX = mybir.AxisListType
DVE_ENGINE = mybir.EngineType.DVE
SP_ENGINE = mybir.EngineType.SP

P = 128
N, D, E = 6250, 256, 100000
NT = -(-N // P)
TAIL = N - (NT - 1) * P
ET = -(-E // P)
EPAD = ET * P - E
PAD_DST = 1 << 14
SPI = 17
STEPS = NT * SPI
assert STEPS >= ET + NT - 1
BLOCKS = NT + STEPS - (ET + NT - 1)
PAIRS = BLOCKS // 2
assert BLOCKS % 2 == 0 and PAIRS % 2 == 0
SG = -(-STEPS // P)
OFFROW = 20
HEADS, HD = 8, 32
NX, HID = 8, 1024
KC = D // P
HC = HID // P
TS = 256
FT = (2 * N + NX * (TS - 1)) // TS
DUMP = FT * TS
ZROWS = 4
ZDMAS = -(-(DUMP + 2 * P) // (P * ZROWS))
SLOTS = ZDMAS * P * ZROWS
WIDE = KC * HID + HC * D
O_W2 = KC * HID
SPLIT = 2 * -(-NX * WIDE // (2 * NT))
SMALL = HC + 2 * KC + D
O_B1 = 0
O_G = O_B1 + HC
O_B = O_G + KC
O_B2 = O_B + KC
SP_P, SP_W = 125, 800
assert SP_P * SP_W == E
XCH = 7
LN_EPS = 1e-5
DEN_MIN = 1e-6
QSTAGE = [(0, 6), (6, 12), (12, SPI)]
AHEAD = 6
PSB = 3


def gps_layer(nc, x, src, dst, wqkv, wproj, bproj, gw1, gb1, gw2, gb2, wr, br, wide, vectors, out):
    whole = ExitStack()
    sems = {}

    def sem(name):
        if name not in sems:
            sems[name] = nc.alloc_semaphore(name=name)
        return sems[name]

    def retire(*kept):
        done = [n for n in sems if n not in kept]
        nc.clear_and_free_semaphores([sems.pop(n) for n in done])
        for n in done:
            tallies.pop(n, None)
        nc.all_engine_barrier()

    def dram(name, shape, dt):
        return nc.dram_tensor(name, shape, dt, kind="Internal").ap()

    def sb(ctx, name, shape, dt=F32):
        return ctx.enter_context(nc.sbuf_tensor(name, shape, dt))

    def banks(ctx, n):
        return [ctx.enter_context(nc.psum_tensor(f"{ctx_name[0]}_bank{i}", [P, 512], F32)) for i in range(n)]

    ctx_name = ["p"]
    tallies = {}

    def link(eng, s, ins):
        tallies[s] = tallies.get(s, 0) + 1
        ins.then_inc(sem(s), 1)
        eng.wait_ge(sem(s), tallies[s])

    e_dst = dram("edges_dst", [ET * P, 1], I32)
    e_src = dram("edges_src", [ET * P, 1], I32)
    off_d = dram("step_offsets", [SG * P], I32)
    table = [dram(f"rows_layer{i}", [n * P, D], F32) for i, n in enumerate((NT, BLOCKS))]
    slots_x = dram("slots_x", [SLOTS, D], F32)
    w_hi = dram("w_hi", [P, NT * SPLIT], F32)
    w_lo = dram("w_lo", [P, NT * SPLIT], F32)
    slots_y = dram("slots_y", [FT * TS, D], F32)
    e_dst_rows = e_dst.rearrange("(t p) o -> t (p o)", p=P)
    e_src_rows = e_src.rearrange("(t p) o -> t (p o)", p=P)

    with whole, nc.allow_non_contiguous_dma("a few columns of one word"):
        node = sb(whole, "node", [P, BLOCKS, D])
        ident = sb(whole, "ident", [P, P])
        ones = sb(whole, "ones", [P, P])
        dis = sb(whole, "dis", [P, BLOCKS])
        valid = sb(whole, "valid", [P, NT])
        w_qkv = sb(whole, "w_qkv", [P, KC, 3 * D])
        w_proj = sb(whole, "w_proj", [P, KC, D])
        w_g = [sb(whole, f"w_g{i}", [P, KC, D]) for i in range(2)]
        b_g = [sb(whole, f"b_g{i}", [P, D]) for i in range(2)]
        b_proj = sb(whole, "b_proj", [P, D])
        w_r = sb(whole, "w_r", [P, KC, NX])
        b_r = sb(whole, "b_r", [P, NX])
        pos_i = sb(whole, "pos_i", [P, 2, NT], I32)
        wts = sb(whole, "wts", [P, 2, NT])

        which_i = sb(whole, "which_i", [1, FT], I32)

        acc_ctx = ExitStack()
        acc = sb(acc_ctx, "acc", [P, BLOCKS * D])
        accv = acc[:, :].rearrange("p (t d) -> p t d", d=D)
        steps_ctx = ExitStack()
        iota_n = sb(steps_ctx, "iota_n", [P, P])
        dloc = sb(steps_ctx, "dloc", [P, SG * P])
        srcs = sb(steps_ctx, "srcs", [P, SG * P], I32)
        offs = sb(steps_ctx, "offs", [1, NT * OFFROW], I32)
        ctx_q = sb(steps_ctx, "ctx_q", [P, KC, D])
        ks_h = sb(steps_ctx, "ks_h", [P, KC, HEADS])
        hmask = sb(steps_ctx, "hmask", [P, KC, HEADS])
        zero = sb(steps_ctx, "zero", [P, ZROWS * D])

        with ExitStack() as ph:
            ctx_name[0] = "order"
            d_pm = sb(ph, "d_pm", [SP_P, SP_W + 1], I32)
            s_pm = sb(ph, "s_pm", [SP_P, SP_W], I32)
            b_i = sb(ph, "b_i", [SP_P, SP_W + 1], I32)
            b_f = sb(ph, "b_f", [SP_P, SP_W + 1])
            mask = sb(ph, "mask", [SP_P, SP_W])
            scan = sb(ph, "scan", [SP_P, SP_W])
            onesr = sb(ph, "onesr", [SP_P, SP_W])
            rank = sb(ph, "rank", [SP_P, SP_W])
            rank_i = sb(ph, "rank_i", [SP_P, SP_W], I32)
            tri = sb(ph, "tri", [P, P])
            bcur = sb(ph, "bcur", [SP_P, 1])
            base = sb(ph, "base", [SP_P, 1])
            shift = sb(ph, "shift", [SP_P, 1])
            viol = sb(ph, "viol", [SP_P, 1])
            flag = sb(ph, "flag", [1, 1], I32)
            padd = sb(ph, "padd", [1, EPAD], I32)
            pads = sb(ph, "pads", [1, EPAD], I32)
            ps = banks(ph, 2)
            with nc.Block() as block:
                @block.sync
                def _(sp):
                    sp.dma_start(e_dst[0:E, :].rearrange("(a b) o -> a (b o)", a=32),
                                 dst.rearrange("(a b) -> a b", a=32)).then_inc(sem("copy_d"), 16)
                    sp.dma_start(e_src[0:E, :].rearrange("(a b) o -> a (b o)", a=32),
                                 src.rearrange("(a b) -> a b", a=32)).then_inc(sem("copy_s"), 16)
                    sp.dma_start(d_pm[:, 0:SP_W], dst.rearrange("(p w) -> p w", w=SP_W)).then_inc(sem("dpm"), 16)
                    sp.wait_ge(sem("edge_mem"), 3)
                    sp.dma_start(d_pm[0:SP_P - 1, SP_W:SP_W + 1],
                                 dst.rearrange("(p w) -> p w", w=SP_W)[1:SP_P, 0:1]).then_inc(sem("dpm_next"), 16)
                    sp.dma_start(e_dst[E:ET * P, :].rearrange("n o -> o n"), padd[:, :]).then_inc(sem("pad_d"), 16)
                    sp.dma_start(e_src[E:ET * P, :].rearrange("n o -> o n"), pads[:, :]).then_inc(sem("pad_s"), 16)
                    for s in ("copy_d", "copy_s", "pad_d", "pad_s"):
                        sp.wait_ge(sem(s), 16)

                @block.gpsimd
                def _(pool):
                    pool.memset(ones[:, :], 1.0).then_inc(sem("consts"), 1)
                    pool.memset(ident[:, :], 0.0).then_inc(sem("consts"), 1)
                    pool.memset(onesr[:, :], 1.0).then_inc(sem("consts"), 1)
                    pool.memset(valid[:, :], 1.0).then_inc(sem("consts"), 1)
                    pool.memset(hmask[:, :, :], 1.0).then_inc(sem("consts"), 1)
                    pool.iota(iota_n[:, :], pattern=[[1, P]], base=0, channel_multiplier=0,
                              allow_small_or_imprecise_dtypes=True).then_inc(sem("consts"), 1)
                    pool.wait_ge(sem("consts"), 6)
                    pool.affine_select(out=ident[:, :], in_=ident[:, :], compare_op=ALU.not_equal, fill=1.0, base=0,
                                       pattern=[[-1, P]], channel_multiplier=1).then_inc(sem("consts"), 1)
                    pool.affine_select(out=tri[:, :], in_=ones[:, :], compare_op=ALU.is_gt, fill=0.0, base=0,
                                       pattern=[[1, P]], channel_multiplier=-1).then_inc(sem("consts"), 1)
                    pool.affine_select(out=valid[:, :], in_=valid[:, :], compare_op=ALU.is_gt, fill=0.0, base=N,
                                       pattern=[[-P, NT]], channel_multiplier=-1).then_inc(sem("consts"), 1)
                    pool.affine_select(out=hmask[:, :, :], in_=hmask[:, :, :], compare_op=ALU.is_ge, fill=0.0, base=0,
                                       pattern=[[P, KC], [-HD, HEADS]], channel_multiplier=1).then_inc(sem("consts"), 1)
                    pool.wait_ge(sem("consts"), 10)
                    pool.affine_select(out=hmask[:, :, :], in_=hmask[:, :, :], compare_op=ALU.is_gt, fill=0.0, base=HD,
                                       pattern=[[-P, KC], [HD, HEADS]], channel_multiplier=-1).then_inc(sem("consts"), 1)

                @block.vector
                def _(v):
                    v.memset(padd[:, :], PAD_DST).then_inc(sem("edge_mem"), 1)
                    v.memset(pads[:, :], 0).then_inc(sem("edge_mem"), 1)
                    v.memset(d_pm[:, SP_W:SP_W + 1], PAD_DST).then_inc(sem("edge_mem"), 1)
                    v.memset(zero[:, :], 0.0).then_inc(sem("zeroed"), 1)
                    v.wait_ge(sem("dpm"), 16)
                    v.wait_ge(sem("dpm_next"), 16)
                    link(v, "ord", v.tensor_scalar(b_i[:, :], d_pm[:, :], 7, None, ALU.arith_shift_right))
                    link(v, "ord", v.tensor_scalar(b_f[:, :], b_i[:, :], float(NT - 1), None, ALU.min))
                    link(v, "ord", v.tensor_tensor(mask[:, :], b_f[:, 0:SP_W], b_f[:, 1:SP_W + 1], ALU.is_gt))
                    v.tensor_reduce(viol[:, :], mask[:, :], AX.X, ALU.max).then_inc(sem("viol"), 1)
                    v.wait_ge(sem("viol_sum"), 1)
                    v.tensor_scalar(flag[:, :], ps[0][0:1, 0:1], 1.0, None, ALU.min).then_inc(sem("flag"), 1)

                @block.tensor
                def _(t):
                    t.wait_ge(sem("consts"), 11)
                    t.wait_ge(sem("viol"), 1)
                    t.matmul(ps[0][0:1, 0:1], viol[:, :], ones[0:SP_P, 0:1], start=True, stop=True).then_inc(sem("viol_sum"), 1)

            with nc.Block() as block:
                @block.sync
                def _(sp):
                    sp.dma_start(s_pm[:, :], src.rearrange("(p w) -> p w", w=SP_W)).then_inc(sem("spm"), 16)
                    sp.wait_ge(sem("spm"), 16)

                @block.vector
                def _(v):
                    unordered = v.value_load(flag[0:1, 0:1], min_val=0, max_val=1)
                    with v.If(unordered > 0):
                        link(v, "ord2", v.memset(bcur[:, :], 0.0))
                        link(v, "ord2", v.memset(base[:, :], -1.0))
                        link(v, "ord2", v.memset(rank[:, :], 0.0))
                        done = tallies["ord2"]
                        per = 7
                        with v.Fori(0, NT) as b:
                            n = b * per + done
                            v.tensor_scalar(mask[:, :], b_f[:, 0:SP_W], bcur[:, :], None, ALU.is_equal).then_inc(sem("ord2"), 1)
                            v.wait_ge(sem("ord2"), n + 1)
                            v.tensor_tensor_scan(scan[:, :], onesr[:, :], mask[:, :], 0.0, ALU.mult, ALU.add).then_inc(sem("ord2"), 1)
                            v.wait_ge(sem("ord2"), n + 2)
                            v.tensor_copy(viol[:, :], scan[:, SP_W - 1:SP_W]).then_inc(sem("ord_tot"), 1)
                            v.wait_ge(sem("ord_sum"), b + 1)
                            v.tensor_tensor(shift[:, :], ps[0][0:SP_P, 0:1], base[:, :], ALU.add).then_inc(sem("ord2"), 1)
                            v.wait_ge(sem("ord2"), n + 3)
                            v.scalar_tensor_tensor(scan[:, :], scan[:, :], shift[:, :], mask[:, :], ALU.add, ALU.mult).then_inc(sem("ord2"), 1)
                            v.wait_ge(sem("ord2"), n + 4)
                            v.tensor_tensor(rank[:, :], rank[:, :], scan[:, :], ALU.add).then_inc(sem("ord2"), 1)
                            v.tensor_tensor(base[:, :], base[:, :], ps[1][0:SP_P, 0:1], ALU.add).then_inc(sem("ord2"), 1)
                            v.tensor_scalar(bcur[:, :], bcur[:, :], 1.0, None, ALU.add).then_inc(sem("ord2"), 1)
                            v.wait_ge(sem("ord2"), n + per)
                        v.tensor_copy(rank_i[:, :], rank[:, :]).then_inc(sem("ranked"), 1)

                @block.tensor
                def _(t):
                    unordered = t.value_load(flag[0:1, 0:1], min_val=0, max_val=1)
                    with t.If(unordered > 0):
                        with t.Fori(0, NT) as b:
                            t.wait_ge(sem("ord_tot"), b + 1)
                            t.matmul(ps[0][0:SP_P, 0:1], tri[0:SP_P, 0:SP_P], viol[:, :], start=True, stop=True)
                            t.matmul(ps[1][0:SP_P, 0:1], ones[0:SP_P, 0:SP_P], viol[:, :], start=True, stop=True).then_inc(sem("ord_sum"), 1)

                @block.gpsimd
                def _(pool):
                    unordered = pool.value_load(flag[0:1, 0:1], min_val=0, max_val=1)
                    with pool.If(unordered > 0):
                        pool.wait_ge(sem("ranked"), 1)
                        pool.wait_ge(sem("spm"), 16)
                        with pool.Fori(0, SP_W) as j:
                            pool.tensor_copy(b_i[:, 0:1], rank_i[:, bass.ds(j, 1)]).then_inc(sem("ord_col"), 1)
                            pool.tensor_copy(b_i[:, 1:2], d_pm[:, bass.ds(j, 1)]).then_inc(sem("ord_col"), 1)
                            pool.tensor_copy(b_i[:, 2:3], s_pm[:, bass.ds(j, 1)]).then_inc(sem("ord_col"), 1)
                            pool.wait_ge(sem("ord_col"), j * 3 + 3)
                            pool.nop(nofuse=True)
                            pool.indirect_dma_start(e_dst, bass.IndirectOffsetOnAxis(ap=b_i[:, 0:1], axis=0),
                                                    b_i[:, 1:2], None).then_inc(sem("ord_dma"), 16)
                            pool.indirect_dma_start(e_src, bass.IndirectOffsetOnAxis(ap=b_i[:, 0:1], axis=0),
                                                    b_i[:, 2:3], None).then_inc(sem("ord_dma2"), 16)
                            pool.wait_ge(sem("ord_dma"), j * 16 + 16)
                            pool.wait_ge(sem("ord_dma2"), j * 16 + 16)

        with ExitStack() as ph:
            ctx_name[0] = "prep"
            first = sb(ph, "first", [1, ET], I32)
            first_b = sb(ph, "first_b", [1, ET], I32)
            tb = sb(ph, "tb", [1, ET])
            iota_t = sb(ph, "iota_t", [1, ET])
            tb_all = sb(ph, "tb_all", [P, ET])
            junk = sb(ph, "junk", [P, ET])
            s_no = sb(ph, "s_no", [P, SG])
            cnt = sb(ph, "cnt", [P, SG])
            t_i = sb(ph, "t_i", [P, SG], I32)
            b_s = sb(ph, "b_s", [P, SG])
            b_128 = sb(ph, "b_128", [P, SG])
            off_i = sb(ph, "off_i", [P, SG], I32)
            rows_i = sb(ph, "rows_i", [P, 2, SG, P], I32)
            rows_f = sb(ph, "rows_f", [P, 2, SG, P])
            iota_b = sb(ph, "iota_b", [P, P], BF16)
            ones_b = sb(ph, "ones_b", [P, 1], BF16)
            iota_k = sb(ph, "iota_k", [P, NT])
            onehot = [sb(ph, f"onehot{i}", [P, 9, P], BF16) for i in range(2)]
            cnt_n = sb(ph, "cnt_n", [P, SG * P])
            cnt_t = sb(ph, "cnt_t", [P, SG, P])
            bind = sb(ph, "bind", [P, SG, NT])
            stat = sb(ph, "stat", [P, NT, 6])
            mv = sb(ph, "mv", [P, NT, 2])
            rstd = sb(ph, "rstd", [P, NT])
            deg = sb(ph, "deg", [P, NT])
            ps = banks(ph, 6)
            cnt_ps = ph.enter_context(nc.psum_tensor("cnt_ps", [P, 1024], F32))
            H2 = ET // 2
            GRP = [(0, 9), (9, SPI)]
            with nc.Block() as block:
                @block.sync
                def _(sp):
                    with nc.allow_non_contiguous_dma("one word per row of edges"):
                        sp.dma_start(first[:, :], e_dst_rows[:, 0:1].rearrange("t o -> o t")).then_inc(sem("first"), 16)
                    for c in range(NT // XCH):
                        lo, n = c * XCH, XCH - (c == NT // XCH - 1)
                        sp.dma_start(node[:, lo:lo + n, :],
                                     x[lo * P:(lo + n) * P, :].rearrange("(t p) d -> p t d", p=P)).then_inc(sem("x_in"), 16)
                    sp.wait_ge(sem("tail0"), 1)
                    sp.dma_start(node[0:TAIL, NT - 1, :], x[(NT - 1) * P:N, :]).then_inc(sem("x_in"), 16)
                    sp.wait_ge(sem("off_i"), 1)
                    with nc.allow_non_contiguous_dma("small"):
                        sp.dma_start(off_d.rearrange("(g p) -> p g", p=P), off_i[:, :]).then_inc(sem("off_d"), 16)
                    sp.wait_ge(sem("off_d"), 16)
                    sp.dma_start(offs[:, :].rearrange("o (i k) -> o i k", k=OFFROW)[:, :, 0:SPI],
                                 off_d[0:STEPS].rearrange("(o i k) -> o i k", o=1, k=SPI)).then_inc(sem("offs"), 16)
                    sp.dma_start(w_qkv[:, :, :], wqkv.rearrange("(c p) n -> p c n", p=P)).then_inc(sem("weights"), 16)
                    sp.dma_start(w_proj[:, :, :], wproj.rearrange("(c p) n -> p c n", p=P)).then_inc(sem("weights"), 16)
                    for i, (w, b) in enumerate(((gw1, gb1), (gw2, gb2))):
                        sp.dma_start(w_g[i][:, :, :], w.rearrange("(c p) n -> p c n", p=P)).then_inc(sem("weights"), 16)
                        sp.dma_start(b_g[i][:, :], b[None, :].to_broadcast([P, D])).then_inc(sem("weights"), 16)
                    sp.dma_start(b_proj[:, :], bproj[None, :].to_broadcast([P, D])).then_inc(sem("weights"), 16)
                    with nc.allow_non_contiguous_dma("small"):
                        sp.dma_start(w_r[:, :, :], wr.rearrange("(c p) n -> p c n", p=P)).then_inc(sem("weights"), 16)
                        sp.dma_start(b_r[:, :], br[None, :].to_broadcast([P, NX])).then_inc(sem("weights"), 16)
                    sp.wait_ge(sem("offs"), 16)
                    sp.wait_ge(sem("weights"), 9 * 16)
                    for c in range(NT // XCH):
                        sp.wait_ge(sem("scaled"), (c + 1) * XCH)
                        sp.dma_start(table[0][c * XCH * P:(c + 1) * XCH * P, :].rearrange("(t p) d -> p t d", p=P),
                                     accv[:, c * XCH:(c + 1) * XCH, :]).then_inc(sem("tab0"), 16)
                    sp.wait_ge(sem("tab0"), NT // XCH * 16)

                @block.gpsimd
                def _(pool):
                    pool.iota(iota_t[:, :], pattern=[[1, ET]], base=0, channel_multiplier=0,
                              allow_small_or_imprecise_dtypes=True).then_inc(sem("prep_c"), 1)
                    pool.iota(s_no[:, :], pattern=[[P, SG]], base=0, channel_multiplier=1,
                              allow_small_or_imprecise_dtypes=True).then_inc(sem("prep_c"), 1)
                    pool.iota(iota_k[:, :], pattern=[[1, NT]], base=0, channel_multiplier=0,
                              allow_small_or_imprecise_dtypes=True).then_inc(sem("prep_c"), 1)
                    pool.memset(ones_b[:, :], 1.0).then_inc(sem("prep_c"), 1)
                    pool.memset(cnt_n[:, :], 0.0).then_inc(sem("prep_c"), 1)
                    pool.memset(acc[:, NT * D:BLOCKS * D], 0.0).then_inc(sem("prep_c"), 1)
                    pool.wait_ge(sem("t_i"), 1)
                    for g in range(SG):
                        at = bass.IndirectOffsetOnAxis(ap=t_i[:, g:g + 1], axis=0)
                        pool.indirect_dma_start(rows_i[:, 0, g, :], None, e_dst_rows, at).then_inc(sem("rows_i"), 16)
                    for g in range(SG):
                        at = bass.IndirectOffsetOnAxis(ap=t_i[:, g:g + 1], axis=0)
                        pool.indirect_dma_start(rows_i[:, 1, g, :], None, e_src_rows, at).then_inc(sem("rows_i"), 16)

                @block.vector
                def _(v):
                    v.memset(dis[:, NT:BLOCKS], 0.0)
                    v.memset(node[:, NT - 1:BLOCKS, :], 0.0).then_inc(sem("tail0"), 1)
                    v.tensor_copy(iota_b[:, :], iota_n[:, :]).then_inc(sem("iota_b"), 1)
                    v.wait_ge(sem("first"), 16)
                    v.wait_ge(sem("prep_c"), 6)
                    link(v, "prp", v.tensor_scalar(first_b[:, :], first[:, :], 7, None, ALU.arith_shift_right))
                    link(v, "prp", v.tensor_scalar(tb[:, :], first_b[:, :], float(NT - 1), None, ALU.min))
                    v.tensor_tensor(tb[:, :], tb[:, :], iota_t[:, :], ALU.add).then_inc(sem("tb"), 1)
                    v.wait_ge(sem("tb_all"), 1)
                    v.tensor_copy(tb_all[:, 0:H2], ps[0][:, 0:H2]).then_inc(sem("prp"), 1)
                    tallies["prp"] += 1
                    link(v, "prp", v.tensor_copy(tb_all[:, H2:ET], ps[1][:, 0:ET - H2]))
                    for g in range(SG):
                        link(v, "prp", v.tensor_scalar(junk[:, :], tb_all[:, :], s_no[:, g:g + 1], 0.0, ALU.is_le, ALU.add,
                                                       accum_out=cnt[:, g:g + 1]))
                    v.tensor_scalar(t_i[:, :], cnt[:, :], -1.0, None, ALU.add).then_inc(sem("t_i"), 1)
                    link(v, "prp", v.scalar_tensor_tensor(b_s[:, :], s_no[:, :], 1.0, cnt[:, :], ALU.add, ALU.subtract))
                    v.tensor_scalar(off_i[:, :], b_s[:, :], float(D), None, ALU.mult).then_inc(sem("off_i"), 1)
                    link(v, "prp", v.tensor_scalar(b_128[:, :], b_s[:, :], float(P), None, ALU.mult))
                    for g in range(SG):
                        v.tensor_scalar(bind[:, g, :], iota_k[:, :], b_s[:, g:g + 1], None, ALU.is_equal).then_inc(sem("bind"), 1)
                    v.wait_ge(sem("rows_i"), 2 * SG * 16)
                    for g in range(SG):
                        v.tensor_scalar(rows_f[:, 0, g, :], rows_i[:, 0, g, :], b_128[:, g:g + 1], None,
                                        ALU.subtract).then_inc(sem("rows_f"), 1)
                    for g in range(SG):
                        v.tensor_copy(rows_f[:, 1, g, :], rows_i[:, 1, g, :]).then_inc(sem("rows_f"), 1)
                    v.wait_ge(sem("dloc"), 2)

                    def one_hots(i, is_first):
                        for h, (a, b) in enumerate(GRP):
                            if not is_first:
                                v.wait_ge(sem("counted"), i * 2 + h - 1)
                            v.tensor_tensor(onehot[h][:, 0:b - a, :], iota_b[:, None, :].to_broadcast([P, b - a, P]),
                                            dloc[:, bass.ds(i * SPI + a, b - a), None].to_broadcast([P, b - a, P]),
                                            ALU.is_equal).then_inc(sem("onehot"), 1)
                    one_hots(0, True)
                    with v.Fori(1, NT) as i:
                        one_hots(i, False)
                    v.wait_ge(sem("x_in"), (NT // XCH + 1) * 16)
                    with v.Fori(0, NT) as t:
                        v.bn_stats(stat[:, bass.ds(t, 1), :].rearrange("p o s -> p (o s)"),
                                   node[:, bass.ds(t, 1), :].rearrange("p o d -> p (o d)")).then_inc(sem("stat"), 1)
                    v.wait_ge(sem("stat"), NT)
                    for t in range(NT):
                        v.bn_aggr(mv[:, t, :], stat[:, t, :]).then_inc(sem("mv"), 1)
                    v.wait_ge(sem("mv"), NT)
                    v.tensor_scalar(rstd[:, :], mv[:, :, 1], LN_EPS, None, ALU.add).then_inc(sem("var"), 1)
                    v.wait_ge(sem("std"), 1)
                    link(v, "prp", v.reciprocal(rstd[:, :], rstd[:, :]))
                    with v.Fori(0, NT) as t:
                        row = node[:, bass.ds(t, 1), :].rearrange("p o d -> p (o d)")
                        v.tensor_scalar(row, row, mv[:, bass.ds(t, 1), 0], rstd[:, bass.ds(t, 1)],
                                        ALU.subtract, ALU.mult).then_inc(sem("normed"), 1)
                    v.wait_ge(sem("counted"), 2 * NT)
                    v.tensor_copy(cnt_n[:, 0:512], cnt_ps[:, 0:512]).then_inc(sem("cnt_n"), 1)
                    v.tensor_copy(cnt_n[:, 512:STEPS], cnt_ps[:, 512:STEPS]).then_inc(sem("cnt_n"), 1)
                    for j in range(2):
                        n = min(4, SG - 4 * j)
                        v.wait_ge(sem("cnt_tp"), j + 1)
                        v.tensor_copy(cnt_t[:, 4 * j:4 * j + n, :].rearrange("p g n -> p (g n)"),
                                      ps[j][:, 0:n * P]).then_inc(sem("cnt_t"), 1)
                    v.wait_ge(sem("deg"), 1)
                    v.tensor_scalar(deg[:, :], ps[2][:, 0:NT], 1.0, None, ALU.add).then_inc(sem("deg1"), 1)
                    v.wait_ge(sem("std"), 2)
                    v.reciprocal(dis[:, 0:NT], deg[:, :]).then_inc(sem("dis"), 1)

                @block.tensor
                def _(t):
                    t.wait_ge(sem("tb"), 1)
                    t.matmul(ps[0][:, 0:H2], ones[0:1, :], tb[:, 0:H2], start=True, stop=True)
                    t.matmul(ps[1][:, 0:ET - H2], ones[0:1, :], tb[:, H2:ET], start=True, stop=True).then_inc(sem("tb_all"), 1)
                    for which in range(2):
                        for g in range(SG):
                            t.wait_ge(sem("rows_f"), which * SG + g + 1)
                            ins = t.transpose(ps[2 + 2 * which + g // 4][:, g % 4 * P:g % 4 * P + P],
                                              rows_f[:, which, g, :], ident[:, :])
                            if g % 4 == 3 or g == SG - 1:
                                ins.then_inc(sem("rows_t"), 1)

                    def counts(i):
                        for h, (a, b) in enumerate(GRP):
                            t.wait_ge(sem("onehot"), i * 2 + h + 1)
                            for k in range(a, b):
                                ins = t.matmul(cnt_ps[:, bass.ds(i * SPI + k, 1)], onehot[h][:, k - a, :], ones_b[:, :],
                                               start=True, stop=True)
                            ins.then_inc(sem("counted"), 1)
                    with t.Fori(0, NT) as i:
                        counts(i)
                    t.wait_ge(sem("cnt_n"), 2)
                    for g in range(SG):
                        ins = t.transpose(ps[g // 4][:, g % 4 * P:g % 4 * P + P], cnt_n[:, g * P:(g + 1) * P], ident[:, :])
                        if g % 4 == 3 or g == SG - 1:
                            ins.then_inc(sem("cnt_tp"), 1)
                    t.wait_ge(sem("cnt_t"), 2)
                    t.wait_ge(sem("bind"), SG)
                    t.wait_ge(sem("dloc"), 2)
                    for g in range(SG):
                        ins = t.matmul(ps[2][:, 0:NT], cnt_t[:, g, :], bind[:, g, :], start=(g == 0), stop=(g == SG - 1))
                    ins.then_inc(sem("deg"), 1)

                @block.scalar
                def _(a):
                    for j in range(2):
                        n = min(4, SG - 4 * j) * P
                        a.wait_ge(sem("rows_t"), j + 1)
                        a.activation(dloc[:, j * 512:j * 512 + n], ps[2 + j][:, 0:n], ACT.Copy).then_inc(sem("dloc"), 1)
                    for j in range(2):
                        n = min(4, SG - 4 * j) * P
                        a.wait_ge(sem("rows_t"), j + 3)
                        a.activation(srcs[:, j * 512:j * 512 + n], ps[4 + j][:, 0:n], ACT.Copy).then_inc(sem("srcs"), 1)
                    a.wait_ge(sem("zeroed"), 1)
                    for z in range(ZDMAS):
                        a.dma_start(slots_x[z * P * ZROWS:(z + 1) * P * ZROWS, :].rearrange("(p r) d -> p (r d)", r=ZROWS),
                                    zero[:, :]).then_inc(sem("cleared"), 16)
                    a.wait_ge(sem("var"), 1)
                    a.activation(rstd[:, :], rstd[:, :], ACT.Sqrt).then_inc(sem("std"), 1)
                    a.wait_ge(sem("deg1"), 1)
                    a.activation(deg[:, :], deg[:, :], ACT.Sqrt).then_inc(sem("std"), 1)
                    a.wait_ge(sem("dis"), 1)
                    a.wait_ge(sem("normed"), NT)
                    with a.Fori(0, NT) as t:
                        a.activation(accv[:, bass.ds(t, 1), :].rearrange("p o d -> p (o d)"),
                                     node[:, bass.ds(t, 1), :].rearrange("p o d -> p (o d)"), ACT.Copy,
                                     scale=dis[:, bass.ds(t, 1)]).then_inc(sem("scaled"), 1)

        retire("cleared", "zeroed")

        def turn(layer, i):
            return i + layer * NT

        def step_gathers(pool, layer, rows, i, is_first):
            for part, (a, b) in enumerate(QSTAGE):
                pool.wait_ge(sem("staged"), turn(layer, i) * len(QSTAGE) + part + 1)
                for k in range(a, b):
                    if not is_first:
                        pool.wait_ge(sem("summed"), turn(layer, i) * SPI + k + 1 - SPI)
                    pool.nop(nofuse=True)
                    pool.indirect_dma_start(rows[:, k, :], None, table[layer],
                                            bass.IndirectOffsetOnAxis(ap=stage[:, k:k + 1], axis=0)
                                            ).then_inc(sem(f"slot_{k}"), 16)

        def stage_indices(a, layer, i, part, is_first=False):
            lo, hi = QSTAGE[part]
            if not is_first:
                a.wait_ge(sem("summed"), turn(layer, i) * SPI + hi - SPI)
            a.activation(stage[:, lo:hi], srcs[:, bass.ds(i * SPI + lo, hi - lo)], ACT.Copy
                         ).then_inc(sem("staged"), 1)

        def step_select(v, layer, i, k, is_first):
            if not is_first:
                v.wait_ge(sem("summed"), turn(layer, i) * SPI + k + 1 - SPI)
            v.tensor_scalar(sel[:, k, :], iota_n[:, :], dloc[:, bass.ds(i * SPI + k, 1)], None,
                            ALU.is_equal).then_inc(sem("selected"), 1)

        def select_ahead(v, layer, i, k, is_first, is_last):
            if k + AHEAD < SPI:
                step_select(v, layer, i, k + AHEAD, is_first)
            elif not is_last:
                step_select(v, layer, i + 1, k + AHEAD - SPI, False)

        def step_add(v, layer, i, k, off, is_first):
            v.wait_ge(sem("summed"), turn(layer, i) * SPI + k + 1)
            if not (is_first and k == 0):
                v.wait_ge(sem("added"), turn(layer, i) * SPI + k)
            to = acc[:, bass.ds(off, D)]
            v.tensor_tensor(to, to, step_ps[k % PSB][:, 0:D], ALU.add).then_inc(sem("added"), 1)

        def step_sum(t, layer, i, k, is_first):
            t.wait_ge(sem("selected"), turn(layer, i) * SPI + k + 1)
            t.wait_ge(sem(f"slot_{k}"), turn(layer, i) * 16 + 16)
            last = k - PSB if k >= PSB else max(j for j in range(SPI) if j % PSB == k % PSB) - SPI
            if not (is_first and k < PSB):
                t.wait_ge(sem("added"), turn(layer, i) * SPI + last + 1)
            t.matmul(step_ps[k % PSB][:, 0:D], sel[:, k, :], rows[:, k, :], start=True, stop=True
                     ).then_inc(sem("summed"), 1)

        def offsets(v, i):
            _, regs = nc.values_load_multi_w_load_instructions(
                offs[0:1, bass.ds(i * OFFROW, SPI)], engines=(DVE_ENGINE,), min_val=0, max_val=(BLOCKS - 1) * D,
                skip_runtime_bounds_check_because="the table holds blocks below BLOCKS")
            return regs

        def dense(ap):
            return ap.rearrange("p o d -> p (o d)")

        def tile(buf, t):
            return dense(buf[:, bass.ds(t, 1), :])

        with ExitStack() as ph:
            ctx_name[0] = "l0"
            stage = sb(ph, "stage0", [P, SPI], I32)
            rows = sb(ph, "rows0", [P, SPI, D])
            sel = sb(ph, "sel0", [P, SPI, P])
            xc = sb(ph, "xc0", [P, D])
            xt = sb(ph, "xt0", [P, KC, P])
            eq = sb(ph, "eq", [P, 2 * D])
            qk = sb(ph, "qk", [P, D])
            vv = sb(ph, "vv", [P, D])
            bk = banks(ph, 8)
            step_ps, ps_t, ps_q, ps_v, ps_c, ps_k = bk[0:3], bk[3], bk[4], bk[5], bk[6], bk[7]
            with nc.Block() as block:
                @block.gpsimd
                def _(pool):
                    step_gathers(pool, 0, rows, 0, True)
                    with pool.Fori(1, NT) as i:
                        step_gathers(pool, 0, rows, i, False)

                @block.scalar
                def _(a):
                    for part in range(len(QSTAGE)):
                        stage_indices(a, 0, 0, part, True)

                    def one(i, is_first, is_last=False):
                        if not is_first:
                            a.wait_ge(sem("m_xt_ps"), i)
                        a.activation(xc[:, :], tile(node, i), ACT.Copy).then_inc(sem("m_xc"), 1)
                        a.wait_ge(sem("m_xt_ps"), i + 1)
                        a.activation(xt[:, :, :].rearrange("p c n -> p (c n)"), ps_t[:, 0:KC * P], ACT.Copy
                                     ).then_inc(sem("m_xt"), 1)
                        a.wait_ge(sem("m_qkv"), i + 1)
                        if not is_first:
                            a.wait_ge(sem("m_k"), i)
                        a.activation(eq[:, :], ps_q[:, :], ACT.Exp).then_inc(sem("m_exp"), 1)
                        if not is_last:
                            stage_indices(a, 0, i + 1, 0)
                        if not is_first:
                            a.wait_ge(sem("m_kv"), i)
                        a.activation(vv[:, :], ps_v[:, 0:D], ACT.Copy).then_inc(sem("m_v"), 1)
                        if not is_last:
                            stage_indices(a, 0, i + 1, 1)
                            stage_indices(a, 0, i + 1, 2)
                    one(0, True)
                    with a.Fori(1, NT - 1) as i:
                        one(i, False)
                    one(NT - 1, False, True)

                @block.vector
                def _(v):
                    def one(i, is_first, is_last):
                        off = offsets(v, i)
                        if is_first:
                            for k in range(AHEAD):
                                step_select(v, 0, 0, k, True)
                        for k in range(SPI):
                            select_ahead(v, 0, i, k, is_first, is_last)
                            step_add(v, 0, i, k, off[k], is_first)
                            if k == 8:
                                v.wait_ge(sem("m_exp"), i + 1)
                                v.tensor_scalar(eq[:, :], eq[:, :], 1.0, None, ALU.min).then_inc(sem("m_min"), 1)
                                v.wait_ge(sem("m_min"), i + 1)
                                v.wait_ge(sem("m_xt_ps"), i + 1)
                                v.scalar_tensor_tensor(tile(node, i), ps_q[:, 0:D], 0.0, eq[:, 0:D],
                                                       ALU.max, ALU.add).then_inc(sem("m_q"), 1)
                                if not is_first:
                                    v.wait_ge(sem("m_kv"), i)
                                v.scalar_tensor_tensor(qk[:, :], ps_q[:, D:2 * D], 0.0, eq[:, D:2 * D],
                                                       ALU.max, ALU.add).then_inc(sem("m_k"), 1)
                    one(0, True, False)
                    with v.Fori(1, NT - 1) as i:
                        one(i, False, False)
                    one(NT - 1, False, True)
                    v.wait_ge(sem("m_closed"), 1)
                    for c in range(KC):
                        v.tensor_tensor(ctx_q[:, c, 0:P].rearrange("p (h d) -> p h d", d=HD),
                                        ps_c[:, c * P:(c + 1) * P].rearrange("p (h d) -> p h d", d=HD),
                                        hmask[:, c, 4 * c:4 * c + 4, None].to_broadcast([P, 4, HD]), ALU.mult
                                        ).then_inc(sem("ctx"), 1)
                        v.tensor_scalar(ks_h[:, c, :], hmask[:, c, :], ps_k[:, c:c + 1], None, ALU.mult
                                        ).then_inc(sem("ctx"), 1)

                @block.tensor
                def _(t):
                    t.wait_ge(sem("zeroed"), 1)
                    t.matmul(ps_c[:, 0:D], zero[:, 0:P], zero[:, 0:D], start=True, stop=False, skip_group_check=True)
                    t.matmul(ps_k[:, 0:KC], zero[:, 0:P], zero[:, 0:KC], start=True, stop=False, skip_group_check=True)

                    def one(i, is_first):
                        for k in range(SPI):
                            step_sum(t, 0, i, k, is_first)
                            if k == 0:
                                if not is_first:
                                    t.wait_ge(sem("m_xt"), i)
                                t.wait_ge(sem("m_xc"), i + 1)
                                for c in range(KC):
                                    ins = t.transpose(ps_t[:, c * P:(c + 1) * P], xc[:, c * P:(c + 1) * P], ident[:, :])
                                ins.then_inc(sem("m_xt_ps"), 1)
                            if k == 3:
                                t.wait_ge(sem("m_xt"), i + 1)
                                if not is_first:
                                    t.wait_ge(sem("m_k"), i)
                                    t.wait_ge(sem("m_v"), i)
                                for lo, n, to in ((0, 2 * D, ps_q), (2 * D, D, ps_v)):
                                    for c in range(KC):
                                        ins = t.matmul(to[:, 0:n], xt[:, c, :], w_qkv[:, c, lo:lo + n],
                                                       start=(c == 0), stop=(c == KC - 1))
                                ins.then_inc(sem("m_qkv"), 1)
                            if k == 13:
                                t.wait_ge(sem("m_k"), i + 1)
                                t.wait_ge(sem("m_v"), i + 1)
                                for c in range(KC):
                                    t.matmul(ps_c[:, c * P:(c + 1) * P], vv[:, c * P:(c + 1) * P], qk[:, c * P:(c + 1) * P],
                                             start=False, stop=False, skip_group_check=True)
                                    ins = t.matmul(ps_k[:, c:c + 1], qk[:, c * P:(c + 1) * P], valid[:, bass.ds(i, 1)],
                                                   start=False, stop=False, skip_group_check=True)
                                ins.then_inc(sem("m_kv"), 1)
                    one(0, True)
                    with t.Fori(1, NT) as i:
                        one(i, False)
                    t.matmul(ps_c[:, 0:D], zero[:, 0:P], zero[:, 0:D], start=False, stop=True, skip_group_check=True)
                    t.matmul(ps_k[:, 0:KC], zero[:, 0:P], zero[:, 0:KC], start=False, stop=True, skip_group_check=True
                             ).then_inc(sem("m_closed"), 1)

        LAG = 2

        def slots(eng, body, lag=LAG):
            def peeled(n):
                body(n, n % 2, lambda d: 0 <= n - d < PAIRS)
            for n in range(4):
                peeled(n)
            with eng.Fori(2, PAIRS // 2 - 1) as turn_no:
                for q in range(2):
                    body(turn_no * 2 + q, q, lambda d: True)
            for n in range(PAIRS - 2, PAIRS + lag):
                peeled(n)

        def later(eng, name, count, n, d):
            if not isinstance(n, int) or n - d >= 0:
                eng.wait_ge(sem(name), count)

        def pair(buf, n):
            return buf[:, bass.ds(n * 2, 2), :]

        def flat2(ap):
            return ap.rearrange("p h d -> p (h d)")

        def conv_scalar(a, layer):
            def scale(n, q):
                later(a, f"c_t{layer}", n - 1, n, 2)
                for h in range(2):
                    a.activation(sc[q][:, h, :], tile(accv, n * 2 + h), ACT.Copy, scale=dis[:, bass.ds(n * 2 + h, 1)]
                                 ).then_inc(sem(f"c_sc{layer}"), 1)

            def body(n, q, has):
                if has(0):
                    a.wait_ge(sem(f"c_t{layer}"), n + 1)
                    later(a, f"c_m{layer}", n - 1, n, 2)
                    a.activation(aggt[q][:, :], ps_t[q][:, :], ACT.Copy).then_inc(sem(f"c_at{layer}"), 1)
                if has(2):
                    a.wait_ge(sem(f"c_z{layer}"), n - 1)
                    later(a, f"c_h{layer}", n - 3, n, 4)
                    a.activation(ez[q][:, :], zz[q][:, :], ACT.Exp).then_inc(sem(f"c_e{layer}"), 1)
                if has(-1):
                    scale(n + 1, 1 - q)
            scale(0, 0)
            slots(a, body)

        def conv_tensor(t, layer):
            def body(n, q, has):
                if has(0):
                    t.wait_ge(sem(f"c_sc{layer}"), n * 2 + 2)
                    later(t, f"c_at{layer}", n - 1, n, 2)
                    for j in range(2 * KC):
                        ins = t.transpose(ps_t[q][:, j * P:(j + 1) * P], flat2(sc[q][:, :, :])[:, j * P:(j + 1) * P], ident[:, :])
                    ins.then_inc(sem(f"c_t{layer}"), 1)
                if has(1):
                    t.wait_ge(sem(f"c_at{layer}"), n)
                    later(t, f"c_z{layer}", n - 2, n, 3)
                    for h in range(2):
                        for c in range(KC):
                            j = h * KC + c
                            ins = t.matmul(ps_z[1 - q][:, h * D:(h + 1) * D], aggt[1 - q][:, j * P:(j + 1) * P],
                                           w_g[layer][:, c, :], start=(c == 0), stop=(c == KC - 1))
                    ins.then_inc(sem(f"c_m{layer}"), 1)
            slots(t, body)

        def conv_vector(v, layer, n, q, has):
            if has(1):
                v.wait_ge(sem(f"c_m{layer}"), n)
                later(v, f"c_e{layer}", n - 2, n, 3)
                later(v, f"c_h{layer}", n - 2, n, 3)
                v.tensor_tensor(zz[1 - q][:, :].rearrange("p (h d) -> p h d", h=2),
                                ps_z[1 - q][:, :].rearrange("p (h d) -> p h d", h=2),
                                b_g[layer][:, None, :].to_broadcast([P, 2, D]), ALU.add).then_inc(sem(f"c_z{layer}"), 1)
            if has(2):
                v.wait_ge(sem(f"c_e{layer}"), n - 1)
                v.tensor_scalar(ez[q][:, :], ez[q][:, :], 1.0, -1.0, ALU.min, ALU.add).then_inc(sem(f"c_k{layer}"), 1)
                v.wait_ge(sem(f"c_k{layer}"), n - 1)
                later(v, f"c_u{layer}", n - 3, n, 4)
                v.scalar_tensor_tensor(hh[q][:, :], zz[q][:, :], 0.0, ez[q][:, :], ALU.max, ALU.add
                                       ).then_inc(sem(f"c_h{layer}"), 1)

        def conv_buffers(ph, layer):
            two = range(2)
            return ([sb(ph, f"sc{layer}_{q}", [P, 2, D]) for q in two],
                    [sb(ph, f"aggt{layer}_{q}", [P, 2 * D]) for q in two],
                    [sb(ph, f"zz{layer}_{q}", [P, 2 * D]) for q in two],
                    [sb(ph, f"ez{layer}_{q}", [P, 2 * D]) for q in two],
                    [sb(ph, f"hh{layer}_{q}", [P, 2 * D]) for q in two])

        with ExitStack() as ph:
            ctx_name[0] = "c0"
            sc, aggt, zz, ez, hh = conv_buffers(ph, 0)
            bk = banks(ph, 5)
            ps_t, ps_z, ps_m = bk[0:2], bk[2:4], bk[4]
            with nc.Block() as block:
                @block.sync
                def _(sp):
                    def body(n, q, has):
                        if has(2):
                            sp.wait_ge(sem("c_u0"), n - 1)
                            sp.dma_start(table[1][bass.ds((n - 2) * 2 * P, 2 * P), :].rearrange("(h p) d -> p h d", p=P),
                                         pair(accv, n - 2)).then_inc(sem("tab1"), 16)
                    slots(sp, body)
                    sp.wait_ge(sem("tab1"), PAIRS * 16)

                @block.gpsimd
                def _(pool):
                    def body(n, q, has):
                        if has(2):
                            pool.wait_ge(sem("c_h0"), n - 1)
                            pool.tensor_tensor(pair(accv, n - 2), hh[q][:, :].rearrange("p (h d) -> p h d", h=2),
                                               dis[:, bass.ds((n - 2) * 2, 2), None].to_broadcast([P, 2, D]), ALU.mult
                                               ).then_inc(sem("c_u0"), 1)
                    slots(pool, body)

                @block.tensor
                def _(t):
                    t.wait_ge(sem("ctx"), 2 * KC)
                    for c in range(KC):
                        ins = t.matmul(ps_m[:, c * D:(c + 1) * D], ctx_q[:, c, 0:P], w_proj[:, c, :], start=True, stop=True)
                    ins.then_inc(sem("ctx_w"), 1)
                    conv_tensor(t, 0)

                @block.scalar
                def _(a):
                    a.wait_ge(sem("ctx_w"), 1)
                    a.activation(ctx_q[:, :, :].rearrange("p c o -> p (c o)"), ps_m[:, :], ACT.Copy).then_inc(sem("ctx_s"), 1)
                    conv_scalar(a, 0)

                @block.vector
                def _(v):
                    slots(v, lambda n, q, has: conv_vector(v, 0, n, q, has))

        with ExitStack() as ph:
            ctx_name[0] = "l1"
            stage = sb(ph, "stage1", [P, SPI], I32)
            rows = sb(ph, "rows1", [P, SPI, D])
            sel = sb(ph, "sel1", [P, SPI, P])
            qc = sb(ph, "qc", [P, D])
            qt = sb(ph, "qt", [P, KC, P])
            qdt = sb(ph, "qdt", [P, KC, P])
            qd = sb(ph, "qd", [P, D])
            xb = sb(ph, "xb", [P, D])
            den = sb(ph, "den", [P, HEADS])
            mixb = sb(ph, "mixb", [P, D])
            wraw = sb(ph, "wraw", [P, SPLIT])
            whi = sb(ph, "whi", [P, SPLIT], F32R)
            wlo = sb(ph, "wlo", [P, SPLIT], F32R)
            bk = banks(ph, 7)
            step_ps, ps_t, ps_d, ps_t2, ps_o = bk[0:3], bk[3], bk[4], bk[5], bk[6]
            with nc.Block() as block:
                @block.sync
                def _(sp):
                    def one(i, is_first, n):
                        if not is_first:
                            sp.wait_ge(sem("a_xadd"), i)
                        sp.dma_start(xb[0:n, :], x[bass.ds(i * P, n), :]).then_inc(sem("a_x"), 16)
                        split_in(i, is_first)
                        split_out(i)

                    def split_in(i, is_first):
                        if not is_first:
                            sp.wait_ge(sem("w_lo"), i)
                        sp.dma_start(wraw[:, :], wide[:, bass.ds(i * SPLIT, SPLIT)]).then_inc(sem("w_raw"), 16)

                    def split_out(i):
                        sp.wait_ge(sem("w_lo"), i + 1)
                        sp.dma_start(w_hi[:, bass.ds(i * SPLIT, SPLIT)], whi[:, :].bitcast(F32)).then_inc(sem("w_st"), 16)
                        sp.dma_start(w_lo[:, bass.ds(i * SPLIT, SPLIT)], wlo[:, :].bitcast(F32)).then_inc(sem("w_st"), 16)
                    one(0, True, P)
                    with sp.Fori(1, NT - 1) as i:
                        one(i, False, P)
                    split_in(NT - 1, False)
                    split_out(NT - 1)
                    sp.wait_ge(sem("a_xzero"), 1)
                    sp.dma_start(xb[0:TAIL, :], x[(NT - 1) * P:N, :]).then_inc(sem("a_x"), 16)
                    sp.wait_ge(sem("a_x"), NT * 16)
                    sp.wait_ge(sem("w_st"), NT * 32)

                @block.gpsimd
                def _(pool):
                    step_gathers(pool, 1, rows, 0, True)
                    with pool.Fori(1, NT) as i:
                        step_gathers(pool, 1, rows, i, False)

                @block.scalar
                def _(a):
                    for part in range(len(QSTAGE)):
                        stage_indices(a, 1, 0, part, True)

                    def one(i, is_first, is_last=False):
                        if not is_first:
                            a.wait_ge(sem("a_t"), i)
                        a.activation(qc[:, :], tile(node, i), ACT.Copy).then_inc(sem("a_qc"), 1)
                        a.wait_ge(sem("a_t"), i + 1)
                        a.activation(qt[:, :, :].rearrange("p c n -> p (c n)"), ps_t[:, 0:KC * P], ACT.Copy
                                     ).then_inc(sem("a_qt"), 1)
                        if not is_last:
                            stage_indices(a, 1, i + 1, 0)
                        a.wait_ge(sem("w_raw"), i * 16 + 16)
                        if not is_first:
                            a.wait_ge(sem("w_st"), i * 32)
                        a.activation(whi[:, :], wraw[:, :], ACT.Copy).then_inc(sem("w_hi"), 1)
                        a.wait_ge(sem("a_t2"), i + 1)
                        a.activation(qdt[:, :, :].rearrange("p c n -> p (c n)"), ps_t2[:, 0:KC * P], ACT.Copy
                                     ).then_inc(sem("a_qdt"), 1)
                        a.wait_ge(sem("a_o"), i + 1)
                        if not is_first:
                            a.wait_ge(sem("a_node"), i)
                        a.activation(mixb[:, :], ps_o[:, 0:D], ACT.Copy).then_inc(sem("a_mix"), 1)
                        if not is_last:
                            stage_indices(a, 1, i + 1, 1)
                            stage_indices(a, 1, i + 1, 2)
                    one(0, True)
                    with a.Fori(1, NT - 1) as i:
                        one(i, False)
                    one(NT - 1, False, True)
                    a.wait_ge(sem("cleared"), ZDMAS * 16)

                @block.vector
                def _(v):
                    def one(i, is_first, is_last):
                        off = offsets(v, i)
                        if is_last:
                            v.wait_ge(sem("a_xadd"), NT - 1)
                            v.memset(xb[:, :], 0.0).then_inc(sem("a_xzero"), 1)
                        if is_first:
                            for k in range(AHEAD):
                                step_select(v, 1, 0, k, True)
                        for k in range(SPI):
                            select_ahead(v, 1, i, k, is_first, is_last)
                            step_add(v, 1, i, k, off[k], is_first)
                            if k == 5:
                                v.wait_ge(sem("a_den"), i + 1)
                                v.tensor_scalar(den[:, :], ps_d[:, 0:HEADS], DEN_MIN, None, ALU.max).then_inc(sem("a_d1"), 1)
                                v.wait_ge(sem("a_d1"), i + 1)
                                v.reciprocal(den[:, :], den[:, :]).then_inc(sem("a_d2"), 1)
                                v.wait_ge(sem("a_d2"), i + 1)
                                if not is_first:
                                    v.wait_ge(sem("a_t2"), i)
                                v.tensor_tensor(qd[:, :].rearrange("p (h d) -> p h d", d=HD),
                                                tile(node, i).rearrange("p (h d) -> p h d", d=HD),
                                                den[:, :, None].to_broadcast([P, HEADS, HD]), ALU.mult
                                                ).then_inc(sem("a_qd"), 1)
                            if k == 11:
                                v.wait_ge(sem("w_hi"), i + 1)
                                v.tensor_tensor(wlo[:, :], wraw[:, :], whi[:, :].bitcast(F32), ALU.subtract
                                                ).then_inc(sem("w_lo"), 1)
                            if k == 15:
                                v.wait_ge(sem("a_x"), i * 16 + 16)
                                v.wait_ge(sem("a_qd"), i + 1)
                                v.wait_ge(sem("a_t"), i + 1)
                                v.tensor_tensor(tile(node, i), xb[:, :], b_proj[:, :], ALU.add).then_inc(sem("a_xadd"), 1)
                                v.wait_ge(sem("a_xadd"), i + 1)
                                v.wait_ge(sem("a_mix"), i + 1)
                                v.tensor_tensor(tile(node, i), tile(node, i), mixb[:, :], ALU.add).then_inc(sem("a_node"), 1)
                    one(0, True, False)
                    with v.Fori(1, NT - 1) as i:
                        one(i, False, False)
                    one(NT - 1, False, True)

                @block.tensor
                def _(t):
                    def one(i, is_first):
                        for k in range(SPI):
                            step_sum(t, 1, i, k, is_first)
                            if k == 0:
                                if not is_first:
                                    t.wait_ge(sem("a_qt"), i)
                                t.wait_ge(sem("a_qc"), i + 1)
                                for c in range(KC):
                                    ins = t.transpose(ps_t[:, c * P:(c + 1) * P], qc[:, c * P:(c + 1) * P], ident[:, :])
                                ins.then_inc(sem("a_t"), 1)
                            if k == 3:
                                t.wait_ge(sem("a_qt"), i + 1)
                                if not is_first:
                                    t.wait_ge(sem("a_d1"), i)
                                for c in range(KC):
                                    ins = t.matmul(ps_d[:, 0:HEADS], qt[:, c, :], ks_h[:, c, :], start=(c == 0), stop=(c == KC - 1))
                                ins.then_inc(sem("a_den"), 1)
                            if k == 8:
                                t.wait_ge(sem("a_qd"), i + 1)
                                if not is_first:
                                    t.wait_ge(sem("a_qdt"), i)
                                for c in range(KC):
                                    ins = t.transpose(ps_t2[:, c * P:(c + 1) * P], qd[:, c * P:(c + 1) * P], ident[:, :])
                                ins.then_inc(sem("a_t2"), 1)
                            if k == 11:
                                t.wait_ge(sem("a_qdt"), i + 1)
                                if not is_first:
                                    t.wait_ge(sem("a_mix"), i)
                                for c in range(KC):
                                    ins = t.matmul(ps_o[:, 0:D], qdt[:, c, :], ctx_q[:, c, :], start=(c == 0), stop=(c == KC - 1))
                                ins.then_inc(sem("a_o"), 1)
                    one(0, True)
                    with t.Fori(1, NT) as i:
                        one(i, False)
        steps_ctx.close()

        with ExitStack() as ph:
            ctx_name[0] = "route"
            sc, aggt, zz, ez, hh = conv_buffers(ph, 1)
            stat = sb(ph, "statf", [P, 2, BLOCKS, 6])
            mv = sb(ph, "mvf", [P, 2, BLOCKS, 2])
            rstd = sb(ph, "rstdf", [P, 2, BLOCKS])
            nmr = sb(ph, "nmr", [P, BLOCKS])
            lg = sb(ph, "lg", [P, NT, NX])
            tri = sb(ph, "trif", [P, P])
            rev = sb(ph, "rev", [P, NX])
            keep = sb(ph, "keep", [P, NX, NT])
            dumpp = sb(ph, "dumpp", [P, 2, NT])
            starts = sb(ph, "starts", [1, FT])
            ea, eb, ec = (sb(ph, f"route_{n}", [P, NT, NX]) for n in "abc")
            oh = [sb(ph, f"oh{i}", [P, NT, NX]) for i in range(2)]
            top = sb(ph, "top", [P, 2, NT])
            small = sb(ph, "small", [P, NT])
            tot = sb(ph, "tot", [P, NX, NT])
            incl = sb(ph, "incl", [P, NX, NT])
            n_f = sb(ph, "n_f", [P, NX])
            n_i = sb(ph, "n_i", [P, NX], I32)
            st = sb(ph, "st", [P, NX])
            one8 = sb(ph, "one8", [P, NX])
            ge = sb(ph, "ge", [1, FT, NX])
            which = sb(ph, "which", [1, FT])
            bk = banks(ph, 7)
            ps_t, ps_z, ps_l, ps_a, ps_b = bk[0:2], bk[2:4], bk[4], bk[5], bk[6]
            with nc.Block() as block:
                @block.gpsimd
                def _(pool):
                    pool.iota(rev[:, :], pattern=[[-1, NX]], base=NX, channel_multiplier=0,
                              allow_small_or_imprecise_dtypes=True).then_inc(sem("f_c"), 1)
                    pool.iota(starts[:, :], pattern=[[TS, FT]], base=0, channel_multiplier=0,
                              allow_small_or_imprecise_dtypes=True).then_inc(sem("f_c"), 1)
                    pool.memset(keep[:, :, :], 1.0).then_inc(sem("f_c"), 1)
                    pool.memset(one8[:, :], 1.0).then_inc(sem("f_c"), 1)
                    pool.iota(dumpp[:, :, :], pattern=[[P, 2], [0, NT]], base=DUMP, channel_multiplier=1,
                              allow_small_or_imprecise_dtypes=True).then_inc(sem("f_c"), 1)
                    pool.affine_select(out=tri[:, :], in_=ones[:, :], compare_op=ALU.is_gt, fill=0.0, base=0,
                                       pattern=[[1, P]], channel_multiplier=-1).then_inc(sem("f_c"), 1)
                    pool.wait_ge(sem("f_c"), 6)
                    pool.affine_select(out=keep[:, :, :], in_=keep[:, :, :], compare_op=ALU.not_equal, fill=0.0, base=0,
                                       pattern=[[0, NX], [1, NT]], channel_multiplier=0).then_inc(sem("f_c"), 1)
                    pool.affine_select(out=dumpp[:, :, :], in_=dumpp[:, :, :], compare_op=ALU.is_ge, fill=0.0, base=-N,
                                       pattern=[[0, 2], [P, NT]], channel_multiplier=1).then_inc(sem("f_c"), 1)
                    def body(n, q, has):
                        if has(2):
                            pool.wait_ge(sem("c_h1"), n - 1)
                            pool.tensor_tensor(pair(node, n - 2), pair(node, n - 2),
                                               hh[q][:, :].rearrange("p (h d) -> p h d", h=2), ALU.add
                                               ).then_inc(sem("c_u1"), 1)
                    slots(pool, body)
                    pool.wait_ge(sem("f_pos"), 2)
                    for t in range(NT):
                        pool.wait_ge(sem("f_xn2"), t + 1)
                        for j in range(2):
                            pool.indirect_dma_start(slots_x, bass.IndirectOffsetOnAxis(ap=pos_i[:, j, t:t + 1], axis=0),
                                                    accv[:, t, :], None).then_inc(sem(f"f_sc{j}"), 16)
                    for j in range(2):
                        pool.wait_ge(sem(f"f_sc{j}"), NT * 16)

                @block.scalar
                def _(a):
                    conv_scalar(a, 1)
                    a.wait_ge(sem("f_var"), 1)
                    a.activation(rstd[:, 0, :], rstd[:, 0, :], ACT.Sqrt).then_inc(sem("f_std"), 1)
                    a.wait_ge(sem("f_nmr"), 1)

                    def norm(n, q):
                        later(a, "f_t", n - 1, n, 2)
                        later(a, "f_cp", n - 1, n, 2)
                        for h in range(2):
                            a.activation(sc[q][:, h, :], tile(node, n * 2 + h), ACT.Identity,
                                         scale=rstd[:, 0, bass.ds(n * 2 + h, 1)], bias=nmr[:, bass.ds(n * 2 + h, 1)]
                                         ).then_inc(sem("f_xt"), 1)

                    def body(n, q, has):
                        if has(0):
                            a.wait_ge(sem("f_t"), n + 1)
                            later(a, "f_l", n - 1, n, 2)
                            a.activation(aggt[q][:, :], ps_t[q][:, :], ACT.Copy).then_inc(sem("f_at"), 1)
                        if has(-1):
                            norm(n + 1, 1 - q)
                    norm(0, 0)
                    slots(a, body, 1)
                    a.wait_ge(sem("f_var"), 2)
                    a.activation(rstd[:, 1, :], rstd[:, 1, :], ACT.Sqrt).then_inc(sem("f_std"), 1)
                    a.wait_ge(sem("f_lmax"), 1)
                    a.activation(ea[:, :, :], ea[:, :, :], ACT.Exp).then_inc(sem("f_exp"), 1)

                @block.tensor
                def _(t):
                    conv_tensor(t, 1)

                    def body(n, q, has):
                        if has(0):
                            t.wait_ge(sem("f_xt"), n * 2 + 2)
                            later(t, "f_at", n - 1, n, 2)
                            for j in range(2 * KC):
                                ins = t.transpose(ps_t[q][:, j * P:(j + 1) * P], flat2(sc[q][:, :, :])[:, j * P:(j + 1) * P], ident[:, :])
                            ins.then_inc(sem("f_t"), 1)
                        if has(1):
                            t.wait_ge(sem("f_at"), n)
                            for h in range(2):
                                for c in range(KC):
                                    j = h * KC + c
                                    ins = t.matmul(ps_l[:, bass.ds((n * 2 - 2 + h) * NX, NX)], aggt[1 - q][:, j * P:(j + 1) * P],
                                                   w_r[:, c, :], start=(c == 0), stop=(c == KC - 1))
                            ins.then_inc(sem("f_l"), 1)
                    slots(t, body, 1)
                    t.wait_ge(sem("f_m"), 1)
                    t.wait_ge(sem("f_c"), 6)
                    m = ec[:, :, :].rearrange("p t e -> p (t e)")
                    t.matmul(ps_a[:, 0:NT * NX], tri[:, :], m, start=True, stop=True)
                    t.matmul(ps_b[:, 0:NT * NX], ones[:, :], m, start=True, stop=True).then_inc(sem("f_cnt"), 1)

                @block.vector
                def _(v):
                    def b8(ap):
                        return ap[:, :, None].to_broadcast([P, NT, NX])

                    def b49(ap):
                        return ap[:, None, :].to_broadcast([P, NT, NX])

                    def stats(which, n, of):
                        for h in range(2):
                            v.bn_stats(dense(stat[:, which, bass.ds(n * 2 + h, 1), :]), of(h)).then_inc(sem(f"f_s{which}"), 1)

                    def aggregate(which):
                        v.wait_ge(sem(f"f_s{which}"), BLOCKS)
                        for t in range(BLOCKS):
                            v.bn_aggr(mv[:, which, t, :], stat[:, which, t, :]).then_inc(sem(f"f_a{which}"), 1)
                        v.wait_ge(sem(f"f_a{which}"), BLOCKS)

                    def body(n, q, has):
                        conv_vector(v, 1, n, q, has)
                        if has(3):
                            v.wait_ge(sem("c_u1"), n - 2)
                            stats(0, n - 3, lambda h: tile(node, (n - 3) * 2 + h))
                    slots(v, body, 3)
                    aggregate(0)
                    v.tensor_scalar(rstd[:, 0, :], mv[:, 0, :, 1], LN_EPS, None, ALU.add).then_inc(sem("f_var"), 1)
                    v.wait_ge(sem("f_std"), 1)
                    link(v, "f_v", v.reciprocal(rstd[:, 0, :], rstd[:, 0, :]))
                    v.scalar_tensor_tensor(nmr[:, :], mv[:, 0, :, 0], -1.0, rstd[:, 0, :], ALU.mult, ALU.mult
                                           ).then_inc(sem("f_nmr"), 1)

                    def second(n, q, has):
                        if has(0):
                            v.wait_ge(sem("f_xt"), n * 2 + 2)
                            stats(1, n, lambda h: sc[q][:, h, :])
                            v.tensor_copy(pair(accv, n), sc[q][:, :, :]).then_inc(sem("f_cp"), 1)
                    slots(v, second, 1)
                    aggregate(1)
                    v.tensor_scalar(rstd[:, 1, :], mv[:, 1, :, 1], LN_EPS, None, ALU.add).then_inc(sem("f_var"), 1)
                    v.wait_ge(sem("f_l"), PAIRS)
                    link(v, "f_v", v.tensor_tensor(lg[:, :, :], ps_l[:, 0:NT * NX].rearrange("p (t e) -> p t e", e=NX),
                                                   b49(b_r[:, :]), ALU.add))
                    link(v, "f_v", v.tensor_reduce(small[:, :], lg[:, :, :], AX.X, ALU.max))
                    v.tensor_tensor(ea[:, :, :], lg[:, :, :], b8(small[:, :]), ALU.subtract).then_inc(sem("f_lmax"), 1)
                    v.wait_ge(sem("f_std"), 2)
                    link(v, "f_v", v.reciprocal(rstd[:, 1, :], rstd[:, 1, :]))
                    v.wait_ge(sem("f_exp"), 1)
                    link(v, "f_v", v.tensor_reduce(small[:, :], ea[:, :, :], AX.X, ALU.add))
                    link(v, "f_v", v.reciprocal(small[:, :], small[:, :]))
                    link(v, "f_v", v.tensor_tensor(ea[:, :, :], ea[:, :, :], b8(small[:, :]), ALU.mult))
                    v.wait_ge(sem("f_c"), 8)
                    for j in range(2):
                        link(v, "f_v", v.tensor_reduce(top[:, j, :], ea[:, :, :], AX.X, ALU.max))
                        link(v, "f_v", v.tensor_tensor(eb[:, :, :], ea[:, :, :], b8(top[:, j, :]), ALU.is_equal))
                        link(v, "f_v", v.tensor_tensor(eb[:, :, :], eb[:, :, :], b49(rev[:, :]), ALU.mult))
                        link(v, "f_v", v.tensor_reduce(small[:, :], eb[:, :, :], AX.X, ALU.max))
                        link(v, "f_v", v.tensor_tensor(oh[j][:, :, :], eb[:, :, :], b8(small[:, :]), ALU.is_equal))
                        if j == 0:
                            link(v, "f_v", v.scalar_tensor_tensor(
                                ea[:, :, :].rearrange("p t e -> p (t e)"), oh[0][:, :, :].rearrange("p t e -> p (t e)"), -4.0,
                                ea[:, :, :].rearrange("p t e -> p (t e)"), ALU.mult, ALU.add))
                    link(v, "f_v", v.tensor_tensor(small[:, :], top[:, 0, :], top[:, 1, :], ALU.add))
                    link(v, "f_v", v.reciprocal(small[:, :], small[:, :]))
                    for j in range(2):
                        v.tensor_tensor(wts[:, j, :], top[:, j, :], small[:, :], ALU.mult).then_inc(sem("f_w"), 1)
                    link(v, "f_v", v.tensor_tensor(ec[:, :, :], oh[0][:, :, :], oh[1][:, :, :], ALU.add))
                    v.tensor_tensor(ec[:, :, :], ec[:, :, :], b8(valid[:, :]), ALU.mult).then_inc(sem("f_m"), 1)
                    v.wait_ge(sem("f_cnt"), 1)
                    link(v, "f_v", v.tensor_copy(tot[:, :, :], ps_b[:, 0:NT * NX].rearrange("p (t e) -> p e t", e=NX)))
                    flat = "p e t -> p (e t)"
                    link(v, "f_v", v.tensor_tensor_scan(incl[:, :, :].rearrange(flat), keep[:, :, :].rearrange(flat),
                                                        tot[:, :, :].rearrange(flat), 0.0, ALU.mult, ALU.add))
                    link(v, "f_v", v.tensor_scalar(n_f[:, :], incl[:, :, NT - 1], float(TS - 1), None, ALU.add))
                    link(v, "f_v", v.tensor_copy(n_i[:, :], n_f[:, :]))
                    link(v, "f_v", v.tensor_scalar(n_i[:, :], n_i[:, :], -TS, None, ALU.bitwise_and))
                    link(v, "f_v", v.tensor_copy(n_f[:, :], n_i[:, :]))
                    link(v, "f_v", v.tensor_tensor_scan(st[:, :], one8[:, :], n_f[:, :], 0.0, ALU.mult, ALU.add))
                    link(v, "f_v", v.tensor_tensor(st[:, :], st[:, :], n_f[:, :], ALU.subtract))
                    link(v, "f_v", v.tensor_tensor(ge[:, :, :], st[0:1, None, :].to_broadcast([1, FT, NX]),
                                                   starts[:, :, None].to_broadcast([1, FT, NX]), ALU.is_le))
                    link(v, "f_v", v.tensor_reduce(which[:, :], ge[:, :, :], AX.X, ALU.add))
                    v.tensor_scalar(which_i[:, :], which[:, :], 1.0, float(-1), ALU.mult, ALU.add).then_inc(sem("f_which"), 1)
                    link(v, "f_v", v.tensor_tensor(incl[:, :, :], incl[:, :, :], tot[:, :, :], ALU.subtract))
                    link(v, "f_v", v.tensor_tensor(incl[:, :, :], incl[:, :, :], st[:, :, None].to_broadcast([P, NX, NT]), ALU.add))
                    link(v, "f_v", v.tensor_tensor(ea[:, :, :], ps_a[:, 0:NT * NX].rearrange("p (t e) -> p t e", e=NX),
                                                   incl[:, :, :].rearrange("p e t -> p t e"), ALU.add))
                    for j in range(2):
                        link(v, "f_v", v.tensor_tensor(eb[:, :, :], ea[:, :, :], oh[j][:, :, :], ALU.mult))
                        link(v, "f_v", v.tensor_reduce(small[:, :], eb[:, :, :], AX.X, ALU.add))
                        link(v, "f_v", v.tensor_tensor(small[:, :], small[:, :], valid[:, :], ALU.mult))
                        v.tensor_tensor(pos_i[:, j, :], small[:, :], dumpp[:, j, :], ALU.add).then_inc(sem("f_pos"), 1)
                        v.wait_ge(sem("f_pos"), j + 1)
                    v.wait_ge(sem("f_cp"), PAIRS)
                    with v.Fori(0, NT) as t:
                        v.tensor_scalar(tile(accv, t), tile(accv, t), mv[:, 1, bass.ds(t, 1), 0], rstd[:, 1, bass.ds(t, 1)],
                                        ALU.subtract, ALU.mult).then_inc(sem("f_xn2"), 1)

        acc_ctx.close()

        with ExitStack() as ph:
            ctx_name[0] = "ffn"
            wh = [sb(ph, f"wh{i}", [P, WIDE], F32R) for i in range(2)]
            wl = [sb(ph, f"wl{i}", [P, WIDE], F32R) for i in range(2)]
            vec = [sb(ph, f"vec{i}", [P, SMALL]) for i in range(2)]
            xr = [sb(ph, f"xr{i}", [P, 2, D]) for i in range(2)]
            xe = sb(ph, "xe", [P, KC, TS])
            xh = sb(ph, "xh", [P, KC, TS], F32R)
            xl = sb(ph, "xl", [P, KC, TS], F32R)
            hr = sb(ph, "hr", [P, 4, TS])
            hh = [sb(ph, f"hhi{i}", [P, HC, TS], F32R) for i in range(2)]
            hl = [sb(ph, f"hlo{i}", [P, HC, TS], F32R) for i in range(2)]
            ys = [sb(ph, f"ys{i}", [P, 2, D]) for i in range(2)]
            bk = banks(ph, 6)
            ps_x, ps_h, ps_y = bk[0], bk[1:5], bk[5]
            x_tiles = slots_x[0:FT * TS, :].rearrange("(n h p) d -> n p h d", h=2, p=P)
            y_tiles = slots_y.rearrange("(n h p) d -> n p h d", h=2, p=P)

            def pairs(eng, body):
                body(0, 0, True, False)
                body(1, 1, True, False)
                with eng.Fori(1, FT // 2 - 1) as n:
                    body(n * 2, 0, False, False)
                    body(n * 2 + 1, 1, False, False)
                body(FT - 2, 0, False, False)
                body(FT - 1, 1, False, True)

            def three(t, to, a, b, first, last):
                t.matmul(to, a[0], b[0], start=first, stop=False)
                t.matmul(to, a[0], b[1], start=False, stop=False)
                return t.matmul(to, a[1], b[0], start=False, stop=last)

            with nc.Block() as block:
                @block.sync
                def _(sp):
                    def first_half(q, e):
                        for to, of in ((wh[q], w_hi), (wl[q], w_lo)):
                            sp.dma_start(to[:, 0:O_W2].bitcast(F32), of[:, bass.ds(e * WIDE, O_W2)]
                                         ).then_inc(sem(f"load_{q}"), 16)
                        sp.dma_start(vec[q][:, 0:O_B2], vectors[:, bass.ds(e * SMALL, O_B2)]).then_inc(sem(f"load_{q}"), 16)

                    def second_half(q, e):
                        for to, of in ((wh[q], w_hi), (wl[q], w_lo)):
                            sp.dma_start(to[:, O_W2:WIDE].bitcast(F32), of[:, bass.ds(e * WIDE + O_W2, WIDE - O_W2)]
                                         ).then_inc(sem(f"load_{2 + q}"), 16)
                        sp.dma_start(vec[q][:, O_B2:SMALL], vectors[:, bass.ds(e * SMALL + O_B2, D)]
                                     ).then_inc(sem(f"load_{2 + q}"), 16)

                    def one(n, q, is_first, is_last):
                        if not is_first:
                            sp.wait_ge(sem("e_t"), n - 1)
                        sp.dma_start(xr[q][:, :, :], x_tiles[bass.ds(n, 1), :, :, :].rearrange("o p h d -> (o p) h d")
                                     ).then_inc(sem(f"load_x{q}"), 16)
                        e = sp.value_load(which_i[0:1, bass.ds(n, 1)], min_val=0, max_val=NX - 1)
                        if is_first:
                            first_half(q, e)
                            second_half(q, e)
                        else:
                            was = sp.value_load(which_i[0:1, bass.ds(n - 2, 1)], min_val=0, max_val=NX - 1)
                            sp.wait_ge(sem("e_g"), n * HC - HC)
                            sp.nop(nofuse=True)
                            with sp.If(e - was > 0):
                                first_half(q, e)
                                sp.wait_ge(sem("e_y"), n - 1)
                                sp.wait_ge(sem("e_ys"), n - 1)
                                second_half(q, e)
                            with sp.Else():
                                sp.sem_inc(sem(f"load_{q}"), 48)
                                sp.wait_ge(sem("e_y"), n - 1)
                                sp.nop(nofuse=True)
                                sp.sem_inc(sem(f"load_{2 + q}"), 48)
                    pairs(sp, one)

                @block.scalar
                def _(a):
                    def scaled(n, q, is_first):
                        a.wait_ge(sem(f"load_{q}"), (n - q) * 24 + 48)
                        a.wait_ge(sem("e_t"), n + 1)
                        if not (is_first and q == 0):
                            a.wait_ge(sem("e_xs"), n * 2)
                        for c in range(KC):
                            a.activation(xe[:, c, :], ps_x[:, c * TS:(c + 1) * TS], ACT.Identity,
                                         scale=vec[q][:, O_G + c:O_G + c + 1], bias=vec[q][:, O_B + c:O_B + c + 1]
                                         ).then_inc(sem("e_xe"), 1)

                    def one(n, q, is_first, is_last):
                        for m in range(HC):
                            a.wait_ge(sem("e_h"), n * HC + m + 1)
                            if not (is_first and q == 0 and m < 4):
                                a.wait_ge(sem("e_hs"), (n * HC + m - 3) * 2)
                            a.activation(hr[:, m % 4, :], ps_h[m % 4][:, 0:TS], ACT.Gelu,
                                         bias=vec[q][:, O_B1 + m:O_B1 + m + 1]).then_inc(sem("e_g"), 1)
                        if not is_last:
                            scaled(n + 1, 1 - q, is_first and q == 0)
                    scaled(0, 0, True)
                    pairs(a, one)

                @block.vector
                def _(v):
                    def split_x(n, q, is_first):
                        v.wait_ge(sem("e_xe"), n * KC + KC)
                        if not (is_first and q == 0):
                            v.wait_ge(sem("e_h"), n * HC)
                        v.tensor_copy(xh[:, :, :], xe[:, :, :]).then_inc(sem("e_xs"), 1)
                        v.wait_ge(sem("e_xs"), n * 2 + 1)
                        v.tensor_tensor(xl[:, :, :], xe[:, :, :], xh[:, :, :].bitcast(F32), ALU.subtract).then_inc(sem("e_xs"), 1)

                    def one(n, q, is_first, is_last):
                        if not is_first:
                            v.wait_ge(sem("e_y"), n - 1)
                        for m in range(HC):
                            v.wait_ge(sem("e_g"), n * HC + m + 1)
                            v.tensor_copy(hh[q][:, m, :], hr[:, m % 4, :]).then_inc(sem("e_hs"), 1)
                            v.wait_ge(sem("e_hs"), (n * HC + m) * 2 + 1)
                            v.tensor_tensor(hl[q][:, m, :], hr[:, m % 4, :], hh[q][:, m, :].bitcast(F32), ALU.subtract
                                            ).then_inc(sem("e_hs"), 1)
                        if not is_last:
                            split_x(n + 1, 1 - q, False)
                        v.wait_ge(sem("e_y"), n + 1)
                        v.wait_ge(sem(f"load_{2 + q}"), (n - q) * 24 + 48)
                        if not is_first:
                            v.wait_ge(sem(f"e_st{q}"), (n - q) * 8)
                        v.tensor_tensor(ys[q][:, :, :], ps_y[:, :].rearrange("p (h d) -> p h d", h=2),
                                        vec[q][:, None, O_B2:O_B2 + D].to_broadcast([P, 2, D]), ALU.add
                                        ).then_inc(sem("e_ys"), 1)
                    split_x(0, 0, True)
                    pairs(v, one)

                @block.gpsimd
                def _(pool):
                    def one(n, q, is_first, is_last):
                        pool.wait_ge(sem("e_ys"), n + 1)
                        pool.nop(nofuse=True)
                        pool.dma_start(y_tiles[bass.ds(n, 1), :, :, :].rearrange("o p h d -> (o p) h d"), ys[q][:, :, :]
                                       ).then_inc(sem(f"e_st{q}"), 16)
                    pairs(pool, one)
                    for q in range(2):
                        pool.wait_ge(sem(f"e_st{q}"), FT * 8)

                @block.tensor
                def _(t):
                    def transposes(n, q, is_first):
                        t.wait_ge(sem(f"load_x{q}"), (n - q) * 8 + 16)
                        if not is_first:
                            t.wait_ge(sem("e_xe"), n * KC)
                        for h in range(2):
                            for c in range(KC):
                                ins = t.transpose(ps_x[:, c * TS + h * P:c * TS + (h + 1) * P],
                                                  xr[q][:, h, c * P:(c + 1) * P], ident[:, :])
                        ins.then_inc(sem("e_t"), 1)

                    def one(n, q, is_first, is_last):
                        t.wait_ge(sem("e_xs"), n * 2 + 2)
                        t.wait_ge(sem(f"load_{q}"), (n - q) * 24 + 48)
                        for m in range(HC):
                            if not (is_first and q == 0 and m < 4):
                                t.wait_ge(sem("e_g"), n * HC + m - 3)
                            for c in range(KC):
                                at = slice(c * HID + m * P, c * HID + (m + 1) * P)
                                ins = three(t, ps_h[m % 4][:, 0:TS], (wh[q][:, at], wl[q][:, at]),
                                            (xh[:, c, :], xl[:, c, :]), c == 0, c == KC - 1)
                            ins.then_inc(sem("e_h"), 1)
                        if not is_last:
                            transposes(n + 1, 1 - q, False)
                        t.wait_ge(sem(f"load_{2 + q}"), (n - q) * 24 + 48)
                        if not (is_first and q == 0):
                            t.wait_ge(sem("e_ys"), n)
                        for h in range(2):
                            for m in range(HC):
                                if h == 0:
                                    t.wait_ge(sem("e_hs"), (n * HC + m) * 2 + 2)
                                at = slice(O_W2 + m * D, O_W2 + (m + 1) * D)
                                ins = three(t, ps_y[:, h * D:(h + 1) * D],
                                            (hh[q][:, m, h * P:(h + 1) * P], hl[q][:, m, h * P:(h + 1) * P]),
                                            (wh[q][:, at], wl[q][:, at]), m == 0, m == HC - 1)
                        ins.then_inc(sem("e_y"), 1)
                    transposes(0, 0, True)
                    pairs(t, one)

        with ExitStack() as ph:
            ctx_name[0] = "comb"
            GB = 4
            LOADED = [FT * 24] * GB
            yg = sb(ph, "yg", [P, GB, 2, D])
            ob = sb(ph, "ob", [P, GB, D])
            with nc.Block() as block:
                @block.gpsimd
                def _(pool):
                    for t in range(NT):
                        if t >= GB:
                            pool.wait_ge(sem("o_2"), t - GB + 1)
                        for j in range(2):
                            idx = pos_i[:, j, t:t + 1] if t < NT - 1 else pos_i[0:TAIL, j, t:t + 1]
                            n = P if t < NT - 1 else TAIL
                            pool.indirect_dma_start(yg[0:n, t % GB, j, :], None, slots_y,
                                                    bass.IndirectOffsetOnAxis(ap=idx, axis=0)
                                                    ).then_inc(sem(f"slot_{t % GB * 2 + j}"), 16)

                @block.vector
                def _(v):
                    for t in range(NT):
                        n = P if t < NT - 1 else TAIL
                        g = t % GB
                        if t >= GB:
                            v.wait_ge(sem(f"load_{g}"), LOADED[g] + t // GB * 16)
                        v.wait_ge(sem(f"slot_{g * 2}"), (turn(2, 0) + t // GB + 1) * 16)
                        v.scalar_tensor_tensor(ob[0:n, g, :], yg[0:n, g, 0, :], wts[0:n, 0, t:t + 1], node[0:n, t, :],
                                               ALU.mult, ALU.add).then_inc(sem("o_1"), 1)
                        v.wait_ge(sem("o_1"), t + 1)
                        v.wait_ge(sem(f"slot_{g * 2 + 1}"), (turn(2, 0) + t // GB + 1) * 16)
                        v.scalar_tensor_tensor(ob[0:n, g, :], yg[0:n, g, 1, :], wts[0:n, 1, t:t + 1], ob[0:n, g, :],
                                               ALU.mult, ALU.add).then_inc(sem("o_2"), 1)

                @block.sync
                def _(sp):
                    for t in range(NT):
                        n = P if t < NT - 1 else TAIL
                        sp.wait_ge(sem("o_2"), t + 1)
                        sp.dma_start(out[t * P:t * P + n, :], ob[0:n, t % GB, :]).then_inc(sem(f"load_{t % GB}"), 16)
                    for g in range(GB):
                        sp.wait_ge(sem(f"load_{g}"), LOADED[g] + len(range(g, NT, GB)) * 16)


def _layout(inputs):
    import numpy as np
    f = {k: np.ascontiguousarray(v) for k, v in inputs.items()}
    wide = np.concatenate([
        f["L0_ffn_W1"].reshape(NX, KC, P, HID).transpose(2, 0, 1, 3).reshape(P, NX, KC * HID),
        f["L0_ffn_W2"].reshape(NX, HC, P, D).transpose(2, 0, 1, 3).reshape(P, NX, HC * D),
    ], axis=2).reshape(P, NX * WIDE)
    vectors = np.concatenate([
        f["L0_ffn_b1"].reshape(NX, HC, P).transpose(2, 0, 1),
        f["L0_ffn_ln_g"].reshape(NX, KC, P).transpose(2, 0, 1),
        f["L0_ffn_ln_b"].reshape(NX, KC, P).transpose(2, 0, 1),
        np.repeat(f["L0_ffn_b2"][None], P, axis=0),
    ], axis=2).reshape(P, NX * SMALL)
    return {
        "x": f["x"], "src": f["src"], "dst": f["dst"],
        "wqkv": np.concatenate([f["L0_mix_Wq"].T, f["L0_mix_Wkv"].T], axis=1),
        "wproj": np.ascontiguousarray(f["L0_mix_Wproj"].T), "bproj": f["L0_mix_bproj"],
        "gw1": f["L0_gnn_W1"], "gb1": f["L0_gnn_b1"], "gw2": f["L0_gnn_W2"], "gb2": f["L0_gnn_b2"],
        "wr": f["L0_ffn_Wr"], "br": f["L0_ffn_br"],
        "wide": np.pad(wide, ((0, 0), (0, NT * SPLIT - NX * WIDE))), "vectors": vectors,
    }


def kernel(**inputs):
    import numpy as np
    import concourse.bacc as bacc
    from concourse.bass_utils import run_bass_kernel_spmd

    arrays = _layout(inputs)
    nc = bacc.Bacc("TRN2", target_bir_lowering=False, num_devices=1)
    args = [nc.dram_tensor(name, a.shape, mybir.dt.from_np(a.dtype), kind="ExternalInput").ap()
            for name, a in arrays.items()]
    out = nc.dram_tensor("out", (N, D), F32, kind="ExternalOutput").ap()
    gps_layer(nc, *args, out)
    r = run_bass_kernel_spmd(nc, [arrays], core_ids=[0])
    return r.results[0]["out"]
```

```python
import concourse.bass as bass
from concourse import mybir
from contextlib import ExitStack

F32 = mybir.dt.float32
F32R = mybir.dt.float32r
I32 = mybir.dt.int32
BF16 = mybir.dt.bfloat16
ALU = mybir.AluOpType
ACT = mybir.ActivationFunctionType
AX = mybir.AxisListType
DVE_ENGINE = mybir.EngineType.DVE

P = 128
N, D, E = 6250, 256, 100000
NT = -(-N // P)
TAIL = N - (NT - 1) * P
ET = -(-E // P)
EPAD = ET * P - E
PAD_DST = 1 << 14
SPI = 17
STEPS = NT * SPI
assert STEPS >= ET + NT - 1
BLOCKS = NT + STEPS - (ET + NT - 1)
PAIRS = BLOCKS // 2
assert BLOCKS % 2 == 0 and PAIRS % 2 == 0
SG = -(-STEPS // P)
OFFROW = 20
HEADS, HD = 8, 32
NX, HID = 8, 1024
KC = D // P
HC = HID // P
TS = 256
FT = (2 * N + NX * (TS - 1)) // TS
SC = FT * TS // P
DUMP = FT * TS
WIDE = KC * HID + HC * D
O_W2 = KC * HID
SPLIT = 2 * -(-NX * WIDE // (2 * NT))
SMALL = HC + 2 * KC + D
O_B1 = 0
O_G = O_B1 + HC
O_B = O_G + KC
O_B2 = O_B + KC
SP_P, SP_W = 125, 800
assert SP_P * SP_W == E
XCH = 7
XIN = NT // XCH
assert NT % XCH == 0
LN_EPS = 1e-5
DEN_MIN = 1e-6
QSTAGE = [(0, 6), (6, 12), (12, SPI)]
AHEAD = 6
PSB = 3


def gps_layer(nc, x, src, dst, wqkv, wproj, bproj, gw1, gb1, gw2, gb2, wr, br, wide, vectors, out):
    whole = ExitStack()
    sems = {}

    def sem(name):
        if name not in sems:
            sems[name] = nc.alloc_semaphore(name=name)
        return sems[name]

    def retire(*kept):
        done = [n for n in sems if n not in kept]
        nc.clear_and_free_semaphores([sems.pop(n) for n in done])
        for n in done:
            tallies.pop(n, None)
        nc.all_engine_barrier()

    def dram(name, shape, dt):
        return nc.dram_tensor(name, shape, dt, kind="Internal").ap()

    def sb(ctx, name, shape, dt=F32):
        return ctx.enter_context(nc.sbuf_tensor(name, shape, dt))

    def banks(ctx, n):
        return [ctx.enter_context(nc.psum_tensor(f"{ctx_name[0]}_bank{i}", [P, 512], F32)) for i in range(n)]

    ctx_name = ["p"]
    tallies = {}

    def link(eng, s, ins):
        tallies[s] = tallies.get(s, 0) + 1
        ins.then_inc(sem(s), 1)
        eng.wait_ge(sem(s), tallies[s])

    e_dst = dram("edges_dst", [ET * P, 1], I32)
    e_src = dram("edges_src", [ET * P, 1], I32)
    off_d = dram("step_offsets", [SG * P], I32)
    table = [dram(f"rows_layer{i}", [n * P, D], F32) for i, n in enumerate((NT, BLOCKS))]
    rows_x = dram("rows_x", [1 + NT * P, D], F32)
    sums = dram("sums", [1 + N + TS, D], F32)
    w_hi = dram("w_hi", [P, NT * SPLIT], F32)
    w_lo = dram("w_lo", [P, NT * SPLIT], F32)
    e_dst_rows = e_dst.rearrange("(t p) o -> t (p o)", p=P)
    e_src_rows = e_src.rearrange("(t p) o -> t (p o)", p=P)

    def by_turn(eng, body):
        body(0, 0, True)
        body(1, 1, True)
        with eng.Fori(1, NT // 2) as n:
            body(n * 2, 0, False)
            body(n * 2 + 1, 1, False)
        body(NT - 1, 0, False)

    with whole, nc.allow_non_contiguous_dma("a few columns of one word"):
        node = sb(whole, "node", [P, BLOCKS, D])
        ident = sb(whole, "ident", [P, P])
        ones = sb(whole, "ones", [P, P])
        dis = sb(whole, "dis", [P, BLOCKS])
        valid = sb(whole, "valid", [P, NT])
        w_qkv = sb(whole, "w_qkv", [P, KC, 3 * D])
        w_proj = sb(whole, "w_proj", [P, KC, D])
        w_g = [sb(whole, f"w_g{i}", [P, KC, D]) for i in range(2)]
        b_g = [sb(whole, f"b_g{i}", [P, D]) for i in range(2)]
        b_proj = sb(whole, "b_proj", [P, D])
        w_r = sb(whole, "w_r", [P, KC, NX])
        b_r = sb(whole, "b_r", [P, NX])
        slot_row = sb(whole, "slot_row", [P, SC], I32)
        slot_sum = sb(whole, "slot_sum", [P, SC], I32)
        slot_w = sb(whole, "slot_w", [P, SC])

        which_i = sb(whole, "which_i", [1, FT], I32)

        acc_ctx = ExitStack()
        acc = sb(acc_ctx, "acc", [P, BLOCKS * D])
        accv = acc[:, :].rearrange("p (t d) -> p t d", d=D)
        steps_ctx = ExitStack()
        iota_n = sb(steps_ctx, "iota_n", [P, P])
        dloc = sb(steps_ctx, "dloc", [P, SG * P])
        srcs = sb(steps_ctx, "srcs", [P, SG * P], I32)
        offs = sb(steps_ctx, "offs", [1, NT * OFFROW], I32)
        ctx_q = sb(steps_ctx, "ctx_q", [P, KC, D])
        ks_h = sb(steps_ctx, "ks_h", [P, KC, HEADS])
        hmask = sb(steps_ctx, "hmask", [P, KC, HEADS])
        zero = sb(steps_ctx, "zero", [P, D])

        with ExitStack() as ph:
            ctx_name[0] = "order"
            d_pm = sb(ph, "d_pm", [SP_P, SP_W + 1], I32)
            s_pm = sb(ph, "s_pm", [SP_P, SP_W], I32)
            b_i = sb(ph, "b_i", [SP_P, SP_W + 1], I32)
            b_f = sb(ph, "b_f", [SP_P, SP_W + 1])
            mask = sb(ph, "mask", [SP_P, SP_W])
            scan = sb(ph, "scan", [SP_P, SP_W])
            onesr = sb(ph, "onesr", [SP_P, SP_W])
            rank = sb(ph, "rank", [SP_P, SP_W])
            rank_i = sb(ph, "rank_i", [SP_P, SP_W], I32)
            tri = sb(ph, "tri", [P, P])
            bcur = sb(ph, "bcur", [SP_P, 1])
            base = sb(ph, "base", [SP_P, 1])
            shift = sb(ph, "shift", [SP_P, 1])
            viol = sb(ph, "viol", [SP_P, 1])
            flag = sb(ph, "flag", [1, 1], I32)
            padd = sb(ph, "padd", [1, EPAD], I32)
            pads = sb(ph, "pads", [1, EPAD], I32)
            ps = banks(ph, 2)
            with nc.Block() as block:
                @block.sync
                def _(sp):
                    sp.dma_start(e_dst[0:E, :].rearrange("(a b) o -> a (b o)", a=32),
                                 dst.rearrange("(a b) -> a b", a=32)).then_inc(sem("copy_d"), 16)
                    sp.dma_start(e_src[0:E, :].rearrange("(a b) o -> a (b o)", a=32),
                                 src.rearrange("(a b) -> a b", a=32)).then_inc(sem("copy_s"), 16)
                    sp.dma_start(d_pm[:, 0:SP_W], dst.rearrange("(p w) -> p w", w=SP_W)).then_inc(sem("dpm"), 16)
                    sp.wait_ge(sem("edge_mem"), 3)
                    sp.dma_start(d_pm[0:SP_P - 1, SP_W:SP_W + 1],
                                 dst.rearrange("(p w) -> p w", w=SP_W)[1:SP_P, 0:1]).then_inc(sem("dpm_next"), 16)
                    sp.dma_start(e_dst[E:ET * P, :].rearrange("n o -> o n"), padd[:, :]).then_inc(sem("pad_d"), 16)
                    sp.dma_start(e_src[E:ET * P, :].rearrange("n o -> o n"), pads[:, :]).then_inc(sem("pad_s"), 16)
                    for s in ("copy_d", "copy_s", "pad_d", "pad_s"):
                        sp.wait_ge(sem(s), 16)

                @block.gpsimd
                def _(pool):
                    pool.memset(ones[:, :], 1.0).then_inc(sem("consts"), 1)
                    pool.memset(ident[:, :], 0.0).then_inc(sem("consts"), 1)
                    pool.memset(onesr[:, :], 1.0).then_inc(sem("consts"), 1)
                    pool.memset(valid[:, :], 1.0).then_inc(sem("consts"), 1)
                    pool.memset(hmask[:, :, :], 1.0).then_inc(sem("consts"), 1)
                    pool.iota(iota_n[:, :], pattern=[[1, P]], base=0, channel_multiplier=0,
                              allow_small_or_imprecise_dtypes=True).then_inc(sem("consts"), 1)
                    pool.wait_ge(sem("consts"), 6)
                    pool.affine_select(out=ident[:, :], in_=ident[:, :], compare_op=ALU.not_equal, fill=1.0, base=0,
                                       pattern=[[-1, P]], channel_multiplier=1).then_inc(sem("consts"), 1)
                    pool.affine_select(out=tri[:, :], in_=ones[:, :], compare_op=ALU.is_gt, fill=0.0, base=0,
                                       pattern=[[1, P]], channel_multiplier=-1).then_inc(sem("consts"), 1)
                    pool.affine_select(out=valid[:, :], in_=valid[:, :], compare_op=ALU.is_gt, fill=0.0, base=N,
                                       pattern=[[-P, NT]], channel_multiplier=-1).then_inc(sem("consts"), 1)
                    pool.affine_select(out=hmask[:, :, :], in_=hmask[:, :, :], compare_op=ALU.is_ge, fill=0.0, base=0,
                                       pattern=[[P, KC], [-HD, HEADS]], channel_multiplier=1).then_inc(sem("consts"), 1)
                    pool.wait_ge(sem("consts"), 10)
                    pool.affine_select(out=hmask[:, :, :], in_=hmask[:, :, :], compare_op=ALU.is_gt, fill=0.0, base=HD,
                                       pattern=[[-P, KC], [HD, HEADS]], channel_multiplier=-1).then_inc(sem("consts"), 1)

                @block.vector
                def _(v):
                    v.memset(padd[:, :], PAD_DST).then_inc(sem("edge_mem"), 1)
                    v.memset(pads[:, :], 0).then_inc(sem("edge_mem"), 1)
                    v.memset(d_pm[:, SP_W:SP_W + 1], PAD_DST).then_inc(sem("edge_mem"), 1)
                    v.memset(zero[:, :], 0.0).then_inc(sem("zeroed"), 1)
                    v.memset(dis[:, NT:BLOCKS], 0.0)
                    v.memset(node[:, NT - 1:BLOCKS, :], 0.0).then_inc(sem("tail0"), 1)
                    v.wait_ge(sem("dpm"), 16)
                    v.wait_ge(sem("dpm_next"), 16)
                    link(v, "ord", v.tensor_scalar(b_i[:, :], d_pm[:, :], 7, None, ALU.arith_shift_right))
                    link(v, "ord", v.tensor_scalar(b_f[:, :], b_i[:, :], float(NT - 1), None, ALU.min))
                    link(v, "ord", v.tensor_tensor(mask[:, :], b_f[:, 0:SP_W], b_f[:, 1:SP_W + 1], ALU.is_gt))
                    v.tensor_reduce(viol[:, :], mask[:, :], AX.X, ALU.max).then_inc(sem("viol"), 1)
                    v.wait_ge(sem("viol_sum"), 1)
                    v.tensor_scalar(flag[:, :], ps[0][0:1, 0:1], 1.0, None, ALU.min).then_inc(sem("flag"), 1)

                @block.tensor
                def _(t):
                    t.wait_ge(sem("consts"), 11)
                    t.wait_ge(sem("viol"), 1)
                    t.matmul(ps[0][0:1, 0:1], viol[:, :], ones[0:SP_P, 0:1], start=True, stop=True).then_inc(sem("viol_sum"), 1)

            with nc.Block() as block:
                @block.sync
                def _(sp):
                    sp.dma_start(s_pm[:, :], src.rearrange("(p w) -> p w", w=SP_W)).then_inc(sem("spm"), 16)
                    sp.wait_ge(sem("spm"), 16)

                @block.vector
                def _(v):
                    unordered = v.value_load(flag[0:1, 0:1], min_val=0, max_val=1)
                    with v.If(unordered > 0):
                        link(v, "ord2", v.memset(bcur[:, :], 0.0))
                        link(v, "ord2", v.memset(base[:, :], -1.0))
                        link(v, "ord2", v.memset(rank[:, :], 0.0))
                        done = tallies["ord2"]
                        per = 7
                        with v.Fori(0, NT) as b:
                            n = b * per + done
                            v.tensor_scalar(mask[:, :], b_f[:, 0:SP_W], bcur[:, :], None, ALU.is_equal).then_inc(sem("ord2"), 1)
                            v.wait_ge(sem("ord2"), n + 1)
                            v.tensor_tensor_scan(scan[:, :], onesr[:, :], mask[:, :], 0.0, ALU.mult, ALU.add).then_inc(sem("ord2"), 1)
                            v.wait_ge(sem("ord2"), n + 2)
                            v.tensor_copy(viol[:, :], scan[:, SP_W - 1:SP_W]).then_inc(sem("ord_tot"), 1)
                            v.wait_ge(sem("ord_sum"), b + 1)
                            v.tensor_tensor(shift[:, :], ps[0][0:SP_P, 0:1], base[:, :], ALU.add).then_inc(sem("ord2"), 1)
                            v.wait_ge(sem("ord2"), n + 3)
                            v.scalar_tensor_tensor(scan[:, :], scan[:, :], shift[:, :], mask[:, :], ALU.add, ALU.mult).then_inc(sem("ord2"), 1)
                            v.wait_ge(sem("ord2"), n + 4)
                            v.tensor_tensor(rank[:, :], rank[:, :], scan[:, :], ALU.add).then_inc(sem("ord2"), 1)
                            v.tensor_tensor(base[:, :], base[:, :], ps[1][0:SP_P, 0:1], ALU.add).then_inc(sem("ord2"), 1)
                            v.tensor_scalar(bcur[:, :], bcur[:, :], 1.0, None, ALU.add).then_inc(sem("ord2"), 1)
                            v.wait_ge(sem("ord2"), n + per)
                        v.tensor_copy(rank_i[:, :], rank[:, :]).then_inc(sem("ranked"), 1)

                @block.tensor
                def _(t):
                    unordered = t.value_load(flag[0:1, 0:1], min_val=0, max_val=1)
                    with t.If(unordered > 0):
                        with t.Fori(0, NT) as b:
                            t.wait_ge(sem("ord_tot"), b + 1)
                            t.matmul(ps[0][0:SP_P, 0:1], tri[0:SP_P, 0:SP_P], viol[:, :], start=True, stop=True)
                            t.matmul(ps[1][0:SP_P, 0:1], ones[0:SP_P, 0:SP_P], viol[:, :], start=True, stop=True).then_inc(sem("ord_sum"), 1)

                @block.gpsimd
                def _(pool):
                    unordered = pool.value_load(flag[0:1, 0:1], min_val=0, max_val=1)
                    with pool.If(unordered > 0):
                        pool.wait_ge(sem("ranked"), 1)
                        pool.wait_ge(sem("spm"), 16)
                        with pool.Fori(0, SP_W) as j:
                            pool.tensor_copy(b_i[:, 0:1], rank_i[:, bass.ds(j, 1)]).then_inc(sem("ord_col"), 1)
                            pool.tensor_copy(b_i[:, 1:2], d_pm[:, bass.ds(j, 1)]).then_inc(sem("ord_col"), 1)
                            pool.tensor_copy(b_i[:, 2:3], s_pm[:, bass.ds(j, 1)]).then_inc(sem("ord_col"), 1)
                            pool.wait_ge(sem("ord_col"), j * 3 + 3)
                            pool.nop(nofuse=True)
                            pool.indirect_dma_start(e_dst, bass.IndirectOffsetOnAxis(ap=b_i[:, 0:1], axis=0),
                                                    b_i[:, 1:2], None).then_inc(sem("ord_dma"), 16)
                            pool.indirect_dma_start(e_src, bass.IndirectOffsetOnAxis(ap=b_i[:, 0:1], axis=0),
                                                    b_i[:, 2:3], None).then_inc(sem("ord_dma2"), 16)
                            pool.wait_ge(sem("ord_dma"), j * 16 + 16)
                            pool.wait_ge(sem("ord_dma2"), j * 16 + 16)

        with ExitStack() as ph:
            ctx_name[0] = "prep"
            first = sb(ph, "first", [1, ET], I32)
            first_b = sb(ph, "first_b", [1, ET], I32)
            tb = sb(ph, "tb", [1, ET])
            iota_t = sb(ph, "iota_t", [1, ET])
            tb_all = sb(ph, "tb_all", [P, ET])
            junk = sb(ph, "junk", [P, ET])
            s_no = sb(ph, "s_no", [P, SG])
            cnt = sb(ph, "cnt", [P, SG])
            t_i = sb(ph, "t_i", [P, SG], I32)
            b_s = sb(ph, "b_s", [P, SG])
            b_128 = sb(ph, "b_128", [P, SG])
            off_i = sb(ph, "off_i", [P, SG], I32)
            rows_i = sb(ph, "rows_i", [P, 2, SG, P], I32)
            rows_f = sb(ph, "rows_f", [P, 2, SG, P])
            iota_b = sb(ph, "iota_b", [P, P], BF16)
            ones_b = sb(ph, "ones_b", [P, 1], BF16)
            iota_k = sb(ph, "iota_k", [P, NT])
            onehot = sb(ph, "onehot", [P, 2, SPI, P], BF16)
            dist2 = sb(ph, "dist2", [P, 2, P], BF16)
            nmr = sb(ph, "nmr0", [P, NT])
            cnt_n = sb(ph, "cnt_n", [P, SG * P])
            cnt_t = sb(ph, "cnt_t", [P, SG, P])
            bind = sb(ph, "bind", [P, SG, NT])
            stat = sb(ph, "stat", [P, NT, 6])
            mv = sb(ph, "mv", [P, NT, 2])
            rstd = sb(ph, "rstd", [P, NT])
            deg = sb(ph, "deg", [P, NT])
            ps = banks(ph, 6)
            H2 = ET // 2
            OF_V, OF_A, OF_P = ((0, 6), (10, 16)), (6, 16), ((7, 9), (9, 10))
            HALVES = ((0, 9), (9, SPI))
            PER_P, PER_A = OF_P[1][1] - OF_P[0][0], len(OF_A)
            d_col = sb(ph, "d_col", [P, PER_P])
            SCALE = [(0, 1, 2), (3, 4), (5, 6)]

            def scale_rows(eng, who):
                eng.wait_ge(sem("dis"), 1)
                eng.wait_ge(sem("normed"), NT)
                with eng.Fori(0, XIN) as c:
                    for t in SCALE[who]:
                        to, of, by = (b[:, bass.ds(c * XCH + t, 1)] for b in (accv, node, dis))
                        to, of = (b.rearrange("p o d -> p (o d)") for b in (to, of))
                        if who == 1:
                            ins = eng.activation(to, of, ACT.Copy, scale=by)
                        elif who == 2:
                            ins = eng.tensor_tensor(to, of, by.to_broadcast([P, D]), ALU.mult)
                        else:
                            ins = eng.tensor_scalar(to, of, by, None, ALU.mult)
                        ins.then_inc(sem(f"scaled_{who}"), 1)
            with nc.Block() as block:
                @block.sync
                def _(sp):
                    with nc.allow_non_contiguous_dma("one word per row of edges"):
                        sp.dma_start(first[:, :], e_dst_rows[:, 0:1].rearrange("t o -> o t")).then_inc(sem("first"), 16)
                    sp.wait_ge(sem("off_i"), 1)
                    with nc.allow_non_contiguous_dma("small"):
                        sp.dma_start(off_d.rearrange("(g p) -> p g", p=P), off_i[:, :]).then_inc(sem("off_d"), 16)
                    sp.wait_ge(sem("off_d"), 16)
                    sp.dma_start(offs[:, :].rearrange("o (i k) -> o i k", k=OFFROW)[:, :, 0:SPI],
                                 off_d[0:STEPS].rearrange("(o i k) -> o i k", o=1, k=SPI)).then_inc(sem("offs"), 16)
                    sp.dma_start(w_qkv[:, :, :], wqkv.rearrange("(c p) n -> p c n", p=P)).then_inc(sem("weights"), 16)
                    sp.dma_start(w_proj[:, :, :], wproj.rearrange("(c p) n -> p c n", p=P)).then_inc(sem("weights"), 16)
                    for i, (w, b) in enumerate(((gw1, gb1), (gw2, gb2))):
                        sp.dma_start(w_g[i][:, :, :], w.rearrange("(c p) n -> p c n", p=P)).then_inc(sem("weights"), 16)
                        sp.dma_start(b_g[i][:, :], b[None, :].to_broadcast([P, D])).then_inc(sem("weights"), 16)
                    sp.dma_start(b_proj[:, :], bproj[None, :].to_broadcast([P, D])).then_inc(sem("weights"), 16)
                    with nc.allow_non_contiguous_dma("small"):
                        sp.dma_start(w_r[:, :, :], wr.rearrange("(c p) n -> p c n", p=P)).then_inc(sem("weights"), 16)
                        sp.dma_start(b_r[:, :], br[None, :].to_broadcast([P, NX])).then_inc(sem("weights"), 16)
                    sp.wait_ge(sem("offs"), 16)
                    sp.wait_ge(sem("weights"), 9 * 16)
                    for c in range(XIN):
                        for who, tiles in enumerate(SCALE):
                            sp.wait_ge(sem(f"scaled_{who}"), (c + 1) * len(tiles))
                        sp.dma_start(table[0][c * XCH * P:(c + 1) * XCH * P, :].rearrange("(t p) d -> p t d", p=P),
                                     accv[:, c * XCH:(c + 1) * XCH, :]).then_inc(sem("tab0"), 16)
                    sp.wait_ge(sem("tab0"), XIN * 16)

                @block.gpsimd
                def _(pool):
                    pool.iota(iota_t[:, :], pattern=[[1, ET]], base=0, channel_multiplier=0,
                              allow_small_or_imprecise_dtypes=True).then_inc(sem("prep_c"), 1)
                    pool.iota(s_no[:, :], pattern=[[P, SG]], base=0, channel_multiplier=1,
                              allow_small_or_imprecise_dtypes=True).then_inc(sem("prep_c"), 1)
                    pool.iota(iota_k[:, :], pattern=[[1, NT]], base=0, channel_multiplier=0,
                              allow_small_or_imprecise_dtypes=True).then_inc(sem("prep_c"), 1)
                    pool.memset(ones_b[:, :], 1.0).then_inc(sem("prep_c"), 1)
                    pool.memset(cnt_n[:, :], 0.0).then_inc(sem("prep_c"), 1)
                    pool.memset(acc[:, NT * D:BLOCKS * D], 0.0).then_inc(sem("prep_c"), 1)
                    for g in range(SG):
                        pool.wait_ge(sem("t_i"), g + 1)
                        at = bass.IndirectOffsetOnAxis(ap=t_i[:, g:g + 1], axis=0)
                        pool.indirect_dma_start(rows_i[:, 0, g, :], None, e_dst_rows, at).then_inc(sem("rows_d"), 16)
                    for g in range(SG):
                        at = bass.IndirectOffsetOnAxis(ap=t_i[:, g:g + 1], axis=0)
                        pool.indirect_dma_start(rows_i[:, 1, g, :], None, e_src_rows, at).then_inc(sem("rows_s"), 16)
                    pool.wait_ge(sem("iota_b"), 1)
                    pool.wait_ge(sem("dloc"), 2)

                    def one_hots(i, q, is_first):
                        if not (is_first and q == 0):
                            pool.wait_ge(sem("onehot_p"), i * PER_P)
                        pool.tensor_copy(d_col[:, :], dloc[:, bass.ds(i * SPI + OF_P[0][0], PER_P)]).then_inc(sem("d_col"), 1)
                        pool.wait_ge(sem("d_col"), i + 1)
                        for h, (lo, hi) in enumerate(OF_P):
                            if not is_first:
                                pool.wait_ge(sem("counted"), i * 2 + h - 3)
                            pool.nop(nofuse=True)
                            for k in range(lo, hi):
                                d = k - OF_P[0][0]
                                pool.tensor_scalar(onehot[:, q, k, :], iota_b[:, :], d_col[:, d:d + 1], None,
                                                   ALU.is_equal).then_inc(sem("onehot_p"), 1)
                    by_turn(pool, one_hots)
                    scale_rows(pool, 2)

                @block.vector
                def _(v):
                    v.tensor_copy(iota_b[:, :], iota_n[:, :]).then_inc(sem("iota_b"), 1)
                    v.wait_ge(sem("first"), 16)
                    v.wait_ge(sem("prep_c"), 6)
                    link(v, "prp", v.tensor_scalar(first_b[:, :], first[:, :], 7, None, ALU.arith_shift_right))
                    link(v, "prp", v.tensor_scalar(tb[:, :], first_b[:, :], float(NT - 1), None, ALU.min))
                    v.tensor_tensor(tb[:, :], tb[:, :], iota_t[:, :], ALU.add).then_inc(sem("tb"), 1)
                    v.wait_ge(sem("tb_all"), 1)
                    v.tensor_copy(tb_all[:, 0:H2], ps[0][:, 0:H2]).then_inc(sem("prp"), 1)
                    tallies["prp"] += 1
                    link(v, "prp", v.tensor_copy(tb_all[:, H2:ET], ps[1][:, 0:ET - H2]))
                    for g in range(SG):
                        link(v, "prp", v.tensor_scalar(junk[:, :], tb_all[:, :], s_no[:, g:g + 1], 0.0, ALU.is_le, ALU.add,
                                                       accum_out=cnt[:, g:g + 1]))
                        v.tensor_scalar(t_i[:, g:g + 1], cnt[:, g:g + 1], -1.0, None, ALU.add).then_inc(sem("t_i"), 1)
                    link(v, "prp", v.scalar_tensor_tensor(b_s[:, :], s_no[:, :], 1.0, cnt[:, :], ALU.add, ALU.subtract))
                    v.tensor_scalar(off_i[:, :], b_s[:, :], float(D), None, ALU.mult).then_inc(sem("off_i"), 1)
                    link(v, "prp", v.tensor_scalar(b_128[:, :], b_s[:, :], float(P), None, ALU.mult))
                    def means(lo, hi):
                        for c in range(lo, hi):
                            v.wait_ge(sem(f"x_in{c}"), 16)
                            if c == XIN - 1:
                                v.wait_ge(sem("x_last"), 16)
                            for t in range(c * XCH, (c + 1) * XCH):
                                v.bn_stats(stat[:, t, :], node[:, t, :]).then_inc(sem("stat"), 1)
                    means(0, 2)
                    v.wait_ge(sem("rows_d"), SG * 16)
                    for g in range(SG):
                        v.tensor_scalar(rows_f[:, 0, g, :], rows_i[:, 0, g, :], b_128[:, g:g + 1], None,
                                        ALU.subtract).then_inc(sem("rows_f"), 1)
                    means(2, XIN)
                    v.wait_ge(sem("stat"), NT)
                    for t in range(NT):
                        v.bn_aggr(mv[:, t, :], stat[:, t, :]).then_inc(sem("mv"), 1)
                    v.wait_ge(sem("mv"), NT)
                    v.tensor_scalar(rstd[:, :], mv[:, :, 1], LN_EPS, None, ALU.add).then_inc(sem("var"), 1)
                    v.wait_ge(sem("std"), 1)
                    link(v, "prp", v.reciprocal(rstd[:, :], rstd[:, :]))
                    v.scalar_tensor_tensor(nmr[:, :], mv[:, :, 0], -1.0, rstd[:, :], ALU.mult, ALU.mult
                                           ).then_inc(sem("nmr"), 1)
                    v.wait_ge(sem("dloc"), 2)

                    def one_hots(i, q, is_first):
                        for h, (lo, mid) in enumerate(OF_V):
                            if not is_first:
                                v.wait_ge(sem("counted"), i * 2 + h - 3)
                            v.tensor_tensor(onehot[:, q, lo:mid, :], iota_b[:, None, :].to_broadcast([P, mid - lo, P]),
                                            dloc[:, bass.ds(i * SPI + lo, mid - lo), None].to_broadcast([P, mid - lo, P]),
                                            ALU.is_equal).then_inc(sem("onehot_v"), 1)
                        if not (is_first and q == 0):
                            keep_counts(i - 1, 1 - q)

                    def keep_counts(i, q):
                        v.wait_ge(sem("counted"), i * 2 + 2)
                        v.tensor_copy(cnt_n[:, bass.ds(i * SPI, SPI)], ps[q][:, 0:SPI]).then_inc(sem("cnt_n"), 1)
                    by_turn(v, one_hots)
                    keep_counts(NT - 1, 0)
                    for g in range(SG):
                        v.tensor_scalar(bind[:, g, :], iota_k[:, :], b_s[:, g:g + 1], None, ALU.is_equal).then_inc(sem("bind"), 1)
                    v.wait_ge(sem("rows_s"), SG * 16)
                    v.tensor_copy(rows_f[:, 1, :, :], rows_i[:, 1, :, :]).then_inc(sem("rows_f"), 1)
                    for j in range(2):
                        n = min(4, SG - 4 * j)
                        v.wait_ge(sem("cnt_tp"), j + 1)
                        v.tensor_copy(cnt_t[:, 4 * j:4 * j + n, :].rearrange("p g n -> p (g n)"),
                                      ps[j][:, 0:n * P]).then_inc(sem("cnt_t"), 1)
                    v.wait_ge(sem("deg"), 1)
                    v.tensor_scalar(deg[:, :], ps[2][:, 0:NT], 1.0, None, ALU.add).then_inc(sem("deg1"), 1)
                    v.wait_ge(sem("std"), 2)
                    v.reciprocal(dis[:, 0:NT], deg[:, :]).then_inc(sem("dis"), 1)
                    scale_rows(v, 0)

                @block.tensor
                def _(t):
                    t.wait_ge(sem("tb"), 1)
                    t.matmul(ps[0][:, 0:H2], ones[0:1, :], tb[:, 0:H2], start=True, stop=True)
                    t.matmul(ps[1][:, 0:ET - H2], ones[0:1, :], tb[:, H2:ET], start=True, stop=True).then_inc(sem("tb_all"), 1)

                    def rows_by_step(which):
                        for g in range(SG):
                            t.wait_ge(sem("rows_f"), SG + 1 if which else g + 1)
                            ins = t.transpose(ps[2 + 2 * which + g // 4][:, g % 4 * P:g % 4 * P + P],
                                              rows_f[:, which, g, :], ident[:, :])
                            if g % 4 == 3 or g == SG - 1:
                                ins.then_inc(sem("rows_t"), 1)
                    rows_by_step(0)

                    def counts(i, q, is_first):
                        if not is_first:
                            t.wait_ge(sem("cnt_n"), i - 1)
                        for h, (lo, hi) in enumerate(HALVES):
                            t.wait_ge(sem("onehot_v"), i * 2 + h + 1)
                            t.wait_ge(sem("onehot_p"), i * PER_P + OF_P[h][1] - OF_P[0][0])
                            t.wait_ge(sem("onehot_a"), i * PER_A + h + 1)
                            for k in range(lo, hi):
                                ins = t.matmul(ps[q][:, k:k + 1], onehot[:, q, k, :], ones_b[:, :],
                                               start=True, stop=True)
                            ins.then_inc(sem("counted"), 1)
                    by_turn(t, counts)
                    t.wait_ge(sem("cnt_n"), NT)
                    for g in range(SG):
                        ins = t.transpose(ps[g // 4][:, g % 4 * P:g % 4 * P + P], cnt_n[:, g * P:(g + 1) * P], ident[:, :])
                        if g % 4 == 3 or g == SG - 1:
                            ins.then_inc(sem("cnt_tp"), 1)
                    rows_by_step(1)
                    t.wait_ge(sem("cnt_t"), 2)
                    t.wait_ge(sem("bind"), SG)
                    t.wait_ge(sem("dloc"), 2)
                    for g in range(SG):
                        ins = t.matmul(ps[2][:, 0:NT], cnt_t[:, g, :], bind[:, g, :], start=(g == 0), stop=(g == SG - 1))
                    ins.then_inc(sem("deg"), 1)

                @block.scalar
                def _(a):
                    a.wait_ge(sem("first"), 16)
                    for c in range(XIN):
                        n = XCH - (c == XIN - 1)
                        a.dma_start(node[:, c * XCH:c * XCH + n, :],
                                    x[c * XCH * P:(c * XCH + n) * P, :].rearrange("(t p) d -> p t d", p=P)
                                    ).then_inc(sem(f"x_in{c}"), 16)
                    a.wait_ge(sem("tail0"), 1)
                    a.dma_start(node[0:TAIL, NT - 1, :], x[(NT - 1) * P:N, :]).then_inc(sem("x_last"), 16)
                    for j in range(2):
                        n = min(4, SG - 4 * j) * P
                        a.wait_ge(sem("rows_t"), j + 1)
                        a.activation(dloc[:, j * 512:j * 512 + n], ps[2 + j][:, 0:n], ACT.Copy).then_inc(sem("dloc"), 1)
                    a.wait_ge(sem("var"), 1)
                    a.activation(rstd[:, :], rstd[:, :], ACT.Sqrt).then_inc(sem("std"), 1)
                    a.wait_ge(sem("iota_b"), 1)
                    a.wait_ge(sem("dloc"), 2)

                    def one_hots(i, q, is_first):
                        if not (is_first and q == 0):
                            a.wait_ge(sem("onehot_a"), i * PER_A)
                        for h, k in enumerate(OF_A):
                            a.activation(dist2[:, h, :], iota_b[:, :], ACT.Square, scale=-1.0,
                                         bias=dloc[:, bass.ds(i * SPI + k, 1)]).then_inc(sem("dist2"), 1)
                        if is_first and q == 0:
                            a.wait_ge(sem("nmr"), 1)
                        row = node[:, bass.ds(i, 1), :].rearrange("p o d -> p (o d)")
                        a.activation(row, row, ACT.Identity, scale=rstd[:, bass.ds(i, 1)], bias=nmr[:, bass.ds(i, 1)]
                                     ).then_inc(sem("normed"), 1)
                        for h, k in enumerate(OF_A):
                            a.wait_ge(sem("dist2"), i * PER_A + h + 1)
                            if not is_first:
                                a.wait_ge(sem("counted"), i * 2 + h - 3)
                            a.activation(onehot[:, q, k, :], dist2[:, h, :], ACT.Relu, scale=-1.0, bias=ones[:, 0:1]
                                         ).then_inc(sem("onehot_a"), 1)
                    by_turn(a, one_hots)
                    for j in range(2):
                        n = min(4, SG - 4 * j) * P
                        a.wait_ge(sem("rows_t"), j + 3)
                        a.activation(srcs[:, j * 512:j * 512 + n], ps[4 + j][:, 0:n], ACT.Copy).then_inc(sem("srcs"), 1)
                    a.wait_ge(sem("deg1"), 1)
                    a.activation(deg[:, :], deg[:, :], ACT.Sqrt).then_inc(sem("std"), 1)
                    scale_rows(a, 1)

        retire("zeroed")

        def turn(layer, i):
            return i + layer * NT

        def step_gathers(pool, layer, rows, i, is_first):
            for part, (a, b) in enumerate(QSTAGE):
                pool.wait_ge(sem("staged"), turn(layer, i) * len(QSTAGE) + part + 1)
                for k in range(a, b):
                    if not is_first:
                        pool.wait_ge(sem("summed"), turn(layer, i) * SPI + k + 1 - SPI)
                    pool.nop(nofuse=True)
                    pool.indirect_dma_start(rows[:, k, :], None, table[layer],
                                            bass.IndirectOffsetOnAxis(ap=stage[:, k:k + 1], axis=0)
                                            ).then_inc(sem(f"slot_{k}"), 16)

        def stage_indices(a, layer, i, part, is_first=False):
            lo, hi = QSTAGE[part]
            if not is_first:
                a.wait_ge(sem("summed"), turn(layer, i) * SPI + hi - SPI)
            a.activation(stage[:, lo:hi], srcs[:, bass.ds(i * SPI + lo, hi - lo)], ACT.Copy
                         ).then_inc(sem("staged"), 1)

        def step_select(v, layer, i, k, is_first):
            if not is_first:
                v.wait_ge(sem("summed"), turn(layer, i) * SPI + k + 1 - SPI)
            v.tensor_scalar(sel[:, k, :], iota_n[:, :], dloc[:, bass.ds(i * SPI + k, 1)], None,
                            ALU.is_equal).then_inc(sem("selected"), 1)

        def select_ahead(v, layer, i, k, is_first, is_last):
            if k + AHEAD < SPI:
                step_select(v, layer, i, k + AHEAD, is_first)
            elif not is_last:
                step_select(v, layer, i + 1, k + AHEAD - SPI, False)

        def step_add(v, layer, i, k, off, is_first):
            v.wait_ge(sem("summed"), turn(layer, i) * SPI + k + 1)
            if not (is_first and k == 0):
                v.wait_ge(sem("added"), turn(layer, i) * SPI + k)
            to = acc[:, bass.ds(off, D)]
            v.tensor_tensor(to, to, step_ps[k % PSB][:, 0:D], ALU.add).then_inc(sem("added"), 1)

        def step_sum(t, layer, i, k, is_first):
            t.wait_ge(sem("selected"), turn(layer, i) * SPI + k + 1)
            t.wait_ge(sem(f"slot_{k}"), turn(layer, i) * 16 + 16)
            last = k - PSB if k >= PSB else max(j for j in range(SPI) if j % PSB == k % PSB) - SPI
            if not (is_first and k < PSB):
                t.wait_ge(sem("added"), turn(layer, i) * SPI + last + 1)
            t.matmul(step_ps[k % PSB][:, 0:D], sel[:, k, :], rows[:, k, :], start=True, stop=True
                     ).then_inc(sem("summed"), 1)

        def offsets(v, i):
            _, regs = nc.values_load_multi_w_load_instructions(
                offs[0:1, bass.ds(i * OFFROW, SPI)], engines=(DVE_ENGINE,), min_val=0, max_val=(BLOCKS - 1) * D,
                skip_runtime_bounds_check_because="the table holds blocks below BLOCKS")
            return regs

        def dense(ap):
            return ap.rearrange("p o d -> p (o d)")

        def tile(buf, t):
            return dense(buf[:, bass.ds(t, 1), :])

        with ExitStack() as ph:
            ctx_name[0] = "l0"
            stage = sb(ph, "stage0", [P, SPI], I32)
            rows = sb(ph, "rows0", [P, SPI, D])
            sel = sb(ph, "sel0", [P, SPI, P])
            xc = sb(ph, "xc0", [P, D])
            xt = sb(ph, "xt0", [P, KC, P])
            eq = sb(ph, "eq", [P, 2 * D])
            qk = sb(ph, "qk", [P, D])
            vv = sb(ph, "vv", [P, D])
            bk = banks(ph, 8)
            step_ps, ps_t, ps_q, ps_v, ps_c, ps_k = bk[0:3], bk[3], bk[4], bk[5], bk[6], bk[7]
            with nc.Block() as block:
                @block.gpsimd
                def _(pool):
                    step_gathers(pool, 0, rows, 0, True)
                    with pool.Fori(1, NT) as i:
                        step_gathers(pool, 0, rows, i, False)

                @block.scalar
                def _(a):
                    for part in range(len(QSTAGE)):
                        stage_indices(a, 0, 0, part, True)

                    def one(i, is_first, is_last=False):
                        if not is_first:
                            a.wait_ge(sem("m_xt_ps"), i)
                        a.activation(xc[:, :], tile(node, i), ACT.Copy).then_inc(sem("m_xc"), 1)
                        a.wait_ge(sem("m_xt_ps"), i + 1)
                        a.activation(xt[:, :, :].rearrange("p c n -> p (c n)"), ps_t[:, 0:KC * P], ACT.Copy
                                     ).then_inc(sem("m_xt"), 1)
                        a.wait_ge(sem("m_qkv"), i + 1)
                        if not is_first:
                            a.wait_ge(sem("m_k"), i)
                        a.activation(eq[:, :], ps_q[:, :], ACT.Exp).then_inc(sem("m_exp"), 1)
                        if not is_last:
                            stage_indices(a, 0, i + 1, 0)
                        if not is_first:
                            a.wait_ge(sem("m_kv"), i)
                        a.activation(vv[:, :], ps_v[:, 0:D], ACT.Copy).then_inc(sem("m_v"), 1)
                        if not is_last:
                            stage_indices(a, 0, i + 1, 1)
                            stage_indices(a, 0, i + 1, 2)
                    one(0, True)
                    with a.Fori(1, NT - 1) as i:
                        one(i, False)
                    one(NT - 1, False, True)

                @block.vector
                def _(v):
                    def one(i, is_first, is_last):
                        off = offsets(v, i)
                        if is_first:
                            for k in range(AHEAD):
                                step_select(v, 0, 0, k, True)
                        for k in range(SPI):
                            select_ahead(v, 0, i, k, is_first, is_last)
                            step_add(v, 0, i, k, off[k], is_first)
                            if k == 8:
                                v.wait_ge(sem("m_exp"), i + 1)
                                v.tensor_scalar(eq[:, :], eq[:, :], 1.0, None, ALU.min).then_inc(sem("m_min"), 1)
                                v.wait_ge(sem("m_min"), i + 1)
                                v.wait_ge(sem("m_xt_ps"), i + 1)
                                v.scalar_tensor_tensor(tile(node, i), ps_q[:, 0:D], 0.0, eq[:, 0:D],
                                                       ALU.max, ALU.add).then_inc(sem("m_q"), 1)
                                if not is_first:
                                    v.wait_ge(sem("m_kv"), i)
                                v.scalar_tensor_tensor(qk[:, :], ps_q[:, D:2 * D], 0.0, eq[:, D:2 * D],
                                                       ALU.max, ALU.add).then_inc(sem("m_k"), 1)
                    one(0, True, False)
                    with v.Fori(1, NT - 1) as i:
                        one(i, False, False)
                    one(NT - 1, False, True)
                    v.wait_ge(sem("m_closed"), 1)
                    for c in range(KC):
                        v.tensor_tensor(ctx_q[:, c, 0:P].rearrange("p (h d) -> p h d", d=HD),
                                        ps_c[:, c * P:(c + 1) * P].rearrange("p (h d) -> p h d", d=HD),
                                        hmask[:, c, 4 * c:4 * c + 4, None].to_broadcast([P, 4, HD]), ALU.mult
                                        ).then_inc(sem("ctx"), 1)
                        v.tensor_scalar(ks_h[:, c, :], hmask[:, c, :], ps_k[:, c:c + 1], None, ALU.mult
                                        ).then_inc(sem("ctx"), 1)

                @block.tensor
                def _(t):
                    t.wait_ge(sem("zeroed"), 1)
                    t.matmul(ps_c[:, 0:D], zero[:, 0:P], zero[:, 0:D], start=True, stop=False, skip_group_check=True)
                    t.matmul(ps_k[:, 0:KC], zero[:, 0:P], zero[:, 0:KC], start=True, stop=False, skip_group_check=True)

                    def one(i, is_first):
                        for k in range(SPI):
                            step_sum(t, 0, i, k, is_first)
                            if k == 0:
                                if not is_first:
                                    t.wait_ge(sem("m_xt"), i)
                                t.wait_ge(sem("m_xc"), i + 1)
                                for c in range(KC):
                                    ins = t.transpose(ps_t[:, c * P:(c + 1) * P], xc[:, c * P:(c + 1) * P], ident[:, :])
                                ins.then_inc(sem("m_xt_ps"), 1)
                            if k == 3:
                                t.wait_ge(sem("m_xt"), i + 1)
                                if not is_first:
                                    t.wait_ge(sem("m_k"), i)
                                    t.wait_ge(sem("m_v"), i)
                                for lo, n, to in ((0, 2 * D, ps_q), (2 * D, D, ps_v)):
                                    for c in range(KC):
                                        ins = t.matmul(to[:, 0:n], xt[:, c, :], w_qkv[:, c, lo:lo + n],
                                                       start=(c == 0), stop=(c == KC - 1))
                                ins.then_inc(sem("m_qkv"), 1)
                            if k == 13:
                                t.wait_ge(sem("m_k"), i + 1)
                                t.wait_ge(sem("m_v"), i + 1)
                                for c in range(KC):
                                    t.matmul(ps_c[:, c * P:(c + 1) * P], vv[:, c * P:(c + 1) * P], qk[:, c * P:(c + 1) * P],
                                             start=False, stop=False, skip_group_check=True)
                                    ins = t.matmul(ps_k[:, c:c + 1], qk[:, c * P:(c + 1) * P], valid[:, bass.ds(i, 1)],
                                                   start=False, stop=False, skip_group_check=True)
                                ins.then_inc(sem("m_kv"), 1)
                    one(0, True)
                    with t.Fori(1, NT) as i:
                        one(i, False)
                    t.matmul(ps_c[:, 0:D], zero[:, 0:P], zero[:, 0:D], start=False, stop=True, skip_group_check=True)
                    t.matmul(ps_k[:, 0:KC], zero[:, 0:P], zero[:, 0:KC], start=False, stop=True, skip_group_check=True
                             ).then_inc(sem("m_closed"), 1)

        LAG = 2

        def slots(eng, body, lag=LAG):
            def peeled(n):
                body(n, n % 2, lambda d: 0 <= n - d < PAIRS)
            for n in range(4):
                peeled(n)
            with eng.Fori(2, PAIRS // 2 - 1) as turn_no:
                for q in range(2):
                    body(turn_no * 2 + q, q, lambda d: True)
            for n in range(PAIRS - 2, PAIRS + lag):
                peeled(n)

        def later(eng, name, count, n, d):
            if not isinstance(n, int) or n - d >= 0:
                eng.wait_ge(sem(name), count)

        def pair(buf, n):
            return buf[:, bass.ds(n * 2, 2), :]

        def flat2(ap):
            return ap.rearrange("p h d -> p (h d)")

        def conv_scalar(a, layer, more=None, lag=LAG):
            def scale(n, q):
                later(a, f"c_t{layer}", n - 1, n, 2)
                for h in range(2):
                    a.activation(sc[q][:, h, :], tile(accv, n * 2 + h), ACT.Copy, scale=dis[:, bass.ds(n * 2 + h, 1)]
                                 ).then_inc(sem(f"c_sc{layer}"), 1)

            def body(n, q, has):
                if has(-1):
                    scale(n + 1, 1 - q)
                if has(0):
                    a.wait_ge(sem(f"c_t{layer}"), n + 1)
                    later(a, f"c_m{layer}", n - 1, n, 2)
                    a.activation(aggt[q][:, :], ps_t[q][:, :], ACT.Copy).then_inc(sem(f"c_at{layer}"), 1)
                if has(2):
                    a.wait_ge(sem(f"c_z{layer}"), n - 1)
                    later(a, f"c_h{layer}", n - 3, n, 4)
                    a.activation(ez[q][:, :], zz[q][:, :], ACT.Exp).then_inc(sem(f"c_e{layer}"), 1)
                if more:
                    more(n, q, has)
            scale(0, 0)
            slots(a, body, lag)

        def conv_tensor(t, layer, more=None, lag=LAG):
            def body(n, q, has):
                if has(0):
                    t.wait_ge(sem(f"c_sc{layer}"), n * 2 + 2)
                    later(t, f"c_at{layer}", n - 1, n, 2)
                    for j in range(2 * KC):
                        ins = t.transpose(ps_t[q][:, j * P:(j + 1) * P], flat2(sc[q][:, :, :])[:, j * P:(j + 1) * P], ident[:, :])
                    ins.then_inc(sem(f"c_t{layer}"), 1)
                if has(1):
                    t.wait_ge(sem(f"c_at{layer}"), n)
                    later(t, f"c_z{layer}", n - 2, n, 3)
                    for h in range(2):
                        for c in range(KC):
                            j = h * KC + c
                            ins = t.matmul(ps_z[1 - q][:, h * D:(h + 1) * D], aggt[1 - q][:, j * P:(j + 1) * P],
                                           w_g[layer][:, c, :], start=(c == 0), stop=(c == KC - 1))
                    ins.then_inc(sem(f"c_m{layer}"), 1)
                if more:
                    more(n, q, has)
            slots(t, body, lag)

        def conv_vector(v, layer, n, q, has):
            if has(1):
                v.wait_ge(sem(f"c_m{layer}"), n)
                later(v, f"c_e{layer}", n - 2, n, 3)
                later(v, f"c_h{layer}", n - 2, n, 3)
                v.tensor_tensor(zz[1 - q][:, :].rearrange("p (h d) -> p h d", h=2),
                                ps_z[1 - q][:, :].rearrange("p (h d) -> p h d", h=2),
                                b_g[layer][:, None, :].to_broadcast([P, 2, D]), ALU.add).then_inc(sem(f"c_z{layer}"), 1)
            if has(2):
                v.wait_ge(sem(f"c_e{layer}"), n - 1)
                v.tensor_scalar(ez[q][:, :], ez[q][:, :], 1.0, -1.0, ALU.min, ALU.add).then_inc(sem(f"c_k{layer}"), 1)
                v.wait_ge(sem(f"c_k{layer}"), n - 1)
                later(v, f"c_u{layer}", n - 3, n, 4)
                v.scalar_tensor_tensor(hh[q][:, :], zz[q][:, :], 0.0, ez[q][:, :], ALU.max, ALU.add
                                       ).then_inc(sem(f"c_h{layer}"), 1)

        def conv_buffers(ph, layer):
            two = range(2)
            return ([sb(ph, f"sc{layer}_{q}", [P, 2, D]) for q in two],
                    [sb(ph, f"aggt{layer}_{q}", [P, 2 * D]) for q in two],
                    [sb(ph, f"zz{layer}_{q}", [P, 2 * D]) for q in two],
                    [sb(ph, f"ez{layer}_{q}", [P, 2 * D]) for q in two],
                    [sb(ph, f"hh{layer}_{q}", [P, 2 * D]) for q in two])

        with ExitStack() as ph:
            ctx_name[0] = "c0"
            sc, aggt, zz, ez, hh = conv_buffers(ph, 0)
            bk = banks(ph, 5)
            ps_t, ps_z, ps_m = bk[0:2], bk[2:4], bk[4]
            with nc.Block() as block:
                @block.sync
                def _(sp):
                    def body(n, q, has):
                        if has(2):
                            sp.wait_ge(sem("c_u0"), n - 1)
                            sp.dma_start(table[1][bass.ds((n - 2) * 2 * P, 2 * P), :].rearrange("(h p) d -> p h d", p=P),
                                         pair(accv, n - 2)).then_inc(sem("tab1"), 16)
                    slots(sp, body)
                    sp.wait_ge(sem("tab1"), PAIRS * 16)

                @block.gpsimd
                def _(pool):
                    def body(n, q, has):
                        if has(2):
                            pool.wait_ge(sem("c_h0"), n - 1)
                            pool.tensor_tensor(pair(accv, n - 2), hh[q][:, :].rearrange("p (h d) -> p h d", h=2),
                                               dis[:, bass.ds((n - 2) * 2, 2), None].to_broadcast([P, 2, D]), ALU.mult
                                               ).then_inc(sem("c_u0"), 1)
                    slots(pool, body)

                @block.tensor
                def _(t):
                    t.wait_ge(sem("ctx"), 2 * KC)
                    for c in range(KC):
                        ins = t.matmul(ps_m[:, c * D:(c + 1) * D], ctx_q[:, c, 0:P], w_proj[:, c, :], start=True, stop=True)
                    ins.then_inc(sem("ctx_w"), 1)
                    conv_tensor(t, 0)

                @block.scalar
                def _(a):
                    a.wait_ge(sem("ctx_w"), 1)
                    a.activation(ctx_q[:, :, :].rearrange("p c o -> p (c o)"), ps_m[:, :], ACT.Copy).then_inc(sem("ctx_s"), 1)
                    conv_scalar(a, 0)

                @block.vector
                def _(v):
                    slots(v, lambda n, q, has: conv_vector(v, 0, n, q, has))

        with ExitStack() as ph:
            ctx_name[0] = "l1"
            stage = sb(ph, "stage1", [P, SPI], I32)
            rows = sb(ph, "rows1", [P, SPI, D])
            sel = sb(ph, "sel1", [P, SPI, P])
            qc = sb(ph, "qc", [P, D])
            qt = sb(ph, "qt", [P, KC, P])
            qdt = sb(ph, "qdt", [P, KC, P])
            qd = sb(ph, "qd", [P, D])
            xb = sb(ph, "xb", [P, D])
            den = sb(ph, "den", [P, HEADS])
            mixb = sb(ph, "mixb", [P, D])
            wraw = sb(ph, "wraw", [P, SPLIT])
            whi = sb(ph, "whi", [P, SPLIT], F32R)
            wlo = sb(ph, "wlo", [P, SPLIT], F32R)
            bk = banks(ph, 7)
            step_ps, ps_t, ps_d, ps_t2, ps_o = bk[0:3], bk[3], bk[4], bk[5], bk[6]
            with nc.Block() as block:
                @block.sync
                def _(sp):
                    def one(i, is_first, n):
                        if not is_first:
                            sp.wait_ge(sem("a_xadd"), i)
                        sp.dma_start(xb[0:n, :], x[bass.ds(i * P, n), :]).then_inc(sem("a_x"), 16)
                        split_in(i, is_first)
                        split_out(i)

                    def split_in(i, is_first):
                        if not is_first:
                            sp.wait_ge(sem("w_lo"), i)
                        sp.dma_start(wraw[:, :], wide[:, bass.ds(i * SPLIT, SPLIT)]).then_inc(sem("w_raw"), 16)

                    def split_out(i):
                        sp.wait_ge(sem("w_lo"), i + 1)
                        sp.dma_start(w_hi[:, bass.ds(i * SPLIT, SPLIT)], whi[:, :].bitcast(F32)).then_inc(sem("w_st"), 16)
                        sp.dma_start(w_lo[:, bass.ds(i * SPLIT, SPLIT)], wlo[:, :].bitcast(F32)).then_inc(sem("w_st"), 16)
                    one(0, True, P)
                    with sp.Fori(1, NT - 1) as i:
                        one(i, False, P)
                    split_in(NT - 1, False)
                    split_out(NT - 1)
                    sp.wait_ge(sem("a_xzero"), 1)
                    sp.dma_start(xb[0:TAIL, :], x[(NT - 1) * P:N, :]).then_inc(sem("a_x"), 16)
                    sp.wait_ge(sem("a_x"), NT * 16)
                    sp.wait_ge(sem("w_st"), NT * 32)

                @block.gpsimd
                def _(pool):
                    step_gathers(pool, 1, rows, 0, True)
                    with pool.Fori(1, NT) as i:
                        step_gathers(pool, 1, rows, i, False)

                @block.scalar
                def _(a):
                    for part in range(len(QSTAGE)):
                        stage_indices(a, 1, 0, part, True)

                    def one(i, is_first, is_last=False):
                        if not is_first:
                            a.wait_ge(sem("a_t"), i)
                        a.activation(qc[:, :], tile(node, i), ACT.Copy).then_inc(sem("a_qc"), 1)
                        a.wait_ge(sem("a_t"), i + 1)
                        a.activation(qt[:, :, :].rearrange("p c n -> p (c n)"), ps_t[:, 0:KC * P], ACT.Copy
                                     ).then_inc(sem("a_qt"), 1)
                        if not is_last:
                            stage_indices(a, 1, i + 1, 0)
                        a.wait_ge(sem("w_raw"), i * 16 + 16)
                        if not is_first:
                            a.wait_ge(sem("w_st"), i * 32)
                        a.activation(whi[:, :], wraw[:, :], ACT.Copy).then_inc(sem("w_hi"), 1)
                        a.wait_ge(sem("a_t2"), i + 1)
                        a.activation(qdt[:, :, :].rearrange("p c n -> p (c n)"), ps_t2[:, 0:KC * P], ACT.Copy
                                     ).then_inc(sem("a_qdt"), 1)
                        a.wait_ge(sem("a_o"), i + 1)
                        if not is_first:
                            a.wait_ge(sem("a_node"), i)
                        a.activation(mixb[:, :], ps_o[:, 0:D], ACT.Copy).then_inc(sem("a_mix"), 1)
                        if not is_last:
                            stage_indices(a, 1, i + 1, 1)
                            stage_indices(a, 1, i + 1, 2)
                    one(0, True)
                    with a.Fori(1, NT - 1) as i:
                        one(i, False)
                    one(NT - 1, False, True)

                @block.vector
                def _(v):
                    def one(i, is_first, is_last):
                        off = offsets(v, i)
                        if is_last:
                            v.wait_ge(sem("a_xadd"), NT - 1)
                            v.memset(xb[:, :], 0.0).then_inc(sem("a_xzero"), 1)
                        if is_first:
                            for k in range(AHEAD):
                                step_select(v, 1, 0, k, True)
                        for k in range(SPI):
                            select_ahead(v, 1, i, k, is_first, is_last)
                            step_add(v, 1, i, k, off[k], is_first)
                            if k == 5:
                                v.wait_ge(sem("a_den"), i + 1)
                                v.tensor_scalar(den[:, :], ps_d[:, 0:HEADS], DEN_MIN, None, ALU.max).then_inc(sem("a_d1"), 1)
                                v.wait_ge(sem("a_d1"), i + 1)
                                v.reciprocal(den[:, :], den[:, :]).then_inc(sem("a_d2"), 1)
                                v.wait_ge(sem("a_d2"), i + 1)
                                if not is_first:
                                    v.wait_ge(sem("a_t2"), i)
                                v.tensor_tensor(qd[:, :].rearrange("p (h d) -> p h d", d=HD),
                                                tile(node, i).rearrange("p (h d) -> p h d", d=HD),
                                                den[:, :, None].to_broadcast([P, HEADS, HD]), ALU.mult
                                                ).then_inc(sem("a_qd"), 1)
                            if k == 11:
                                v.wait_ge(sem("w_hi"), i + 1)
                                v.tensor_tensor(wlo[:, :], wraw[:, :], whi[:, :].bitcast(F32), ALU.subtract
                                                ).then_inc(sem("w_lo"), 1)
                            if k == 15:
                                v.wait_ge(sem("a_x"), i * 16 + 16)
                                v.wait_ge(sem("a_qd"), i + 1)
                                v.wait_ge(sem("a_t"), i + 1)
                                v.tensor_tensor(tile(node, i), xb[:, :], b_proj[:, :], ALU.add).then_inc(sem("a_xadd"), 1)
                                v.wait_ge(sem("a_xadd"), i + 1)
                                v.wait_ge(sem("a_mix"), i + 1)
                                v.tensor_tensor(tile(node, i), tile(node, i), mixb[:, :], ALU.add).then_inc(sem("a_node"), 1)
                    one(0, True, False)
                    with v.Fori(1, NT - 1) as i:
                        one(i, False, False)
                    one(NT - 1, False, True)

                @block.tensor
                def _(t):
                    def one(i, is_first):
                        for k in range(SPI):
                            step_sum(t, 1, i, k, is_first)
                            if k == 0:
                                if not is_first:
                                    t.wait_ge(sem("a_qt"), i)
                                t.wait_ge(sem("a_qc"), i + 1)
                                for c in range(KC):
                                    ins = t.transpose(ps_t[:, c * P:(c + 1) * P], qc[:, c * P:(c + 1) * P], ident[:, :])
                                ins.then_inc(sem("a_t"), 1)
                            if k == 3:
                                t.wait_ge(sem("a_qt"), i + 1)
                                if not is_first:
                                    t.wait_ge(sem("a_d1"), i)
                                for c in range(KC):
                                    ins = t.matmul(ps_d[:, 0:HEADS], qt[:, c, :], ks_h[:, c, :], start=(c == 0), stop=(c == KC - 1))
                                ins.then_inc(sem("a_den"), 1)
                            if k == 8:
                                t.wait_ge(sem("a_qd"), i + 1)
                                if not is_first:
                                    t.wait_ge(sem("a_qdt"), i)
                                for c in range(KC):
                                    ins = t.transpose(ps_t2[:, c * P:(c + 1) * P], qd[:, c * P:(c + 1) * P], ident[:, :])
                                ins.then_inc(sem("a_t2"), 1)
                            if k == 11:
                                t.wait_ge(sem("a_qdt"), i + 1)
                                if not is_first:
                                    t.wait_ge(sem("a_mix"), i)
                                for c in range(KC):
                                    ins = t.matmul(ps_o[:, 0:D], qdt[:, c, :], ctx_q[:, c, :], start=(c == 0), stop=(c == KC - 1))
                                ins.then_inc(sem("a_o"), 1)
                    one(0, True)
                    with t.Fori(1, NT) as i:
                        one(i, False)
        steps_ctx.close()

        with ExitStack() as ph:
            ctx_name[0] = "route"
            sc, aggt, zz, ez, hh = conv_buffers(ph, 1)
            pos_i, hi_i, lo_i = (sb(ph, n, [P, 2, NT], I32) for n in ("pos_i", "hi_i", "lo_i"))
            hi_f, lo_f = (sb(ph, n, [P, 2, NT]) for n in ("hi_f", "lo_f"))
            places = sb(ph, "places", [P, P])
            nmr = sb(ph, "nmr", [P, NT])
            at_place = sb(ph, "at_place", [P, 2, 2, P])
            at_col = sb(ph, "at_col", [P, 2, 2, 2, SC])
            dist2 = sb(ph, "dist2f", [P, P])
            lo_col = sb(ph, "lo_col", [P, 1])
            slot_no = sb(ph, "slot_no", [P, SC])
            spare = sb(ph, "spare", [P, FT, 2])
            tags = sb(ph, "tags", [P, NT, 2, 2])
            xs = [sb(ph, f"xs{q}", [P, 2, D]) for q in range(2)]
            xst = [sb(ph, f"xst{q}", [P, 2 * D]) for q in range(2)]
            stat = sb(ph, "statf", [P, BLOCKS, 6])
            mv = sb(ph, "mvf", [P, NT, 2])
            rstd = sb(ph, "rstdf", [P, NT])
            both = sb(ph, "both", [P, NT])
            w_sum = sb(ph, "w_sum", [P, NX])
            lg = sb(ph, "lg", [P, NT, NX])
            tri = sb(ph, "trif", [P, P])
            rev = sb(ph, "rev", [P, NX])
            keep = sb(ph, "keep", [P, NX, NT])
            dumpp = sb(ph, "dumpp", [P, 2, NT])
            starts = sb(ph, "starts", [1, FT])
            ea, eb, ec = (sb(ph, f"route_{n}", [P, NT, NX]) for n in "abc")
            oh = [sb(ph, f"oh{i}", [P, NT, NX]) for i in range(2)]
            top = sb(ph, "top", [P, 2, NT])
            small = sb(ph, "small", [P, NT])
            tot = sb(ph, "tot", [P, NX, NT])
            incl = sb(ph, "incl", [P, NX, NT])
            n_f = sb(ph, "n_f", [P, NX])
            n_i = sb(ph, "n_i", [P, NX], I32)
            st = sb(ph, "st", [P, NX])
            one8 = sb(ph, "one8", [P, NX])
            ge = sb(ph, "ge", [1, FT, NX])
            which = sb(ph, "which", [1, FT])
            bk = banks(ph, 7)
            ps_t, ps_z, ps_l, ps_a, ps_b = bk[0:2], bk[2:4], bk[4], bk[5], bk[6]
            ps_xt = (ps_a, ps_b)
            with nc.Block() as block:
                @block.sync
                def _(sp):
                    for c in range(XIN):
                        n = XCH - (c == XIN - 1)
                        sp.wait_ge(sem("c_u1"), -(-(c + 1) * XCH // 2))
                        sp.dma_start(sums[1 + c * XCH * P:1 + (c * XCH + n) * P, :].rearrange("(t p) d -> p t d", p=P),
                                     node[:, c * XCH:c * XCH + n, :]).then_inc(sem("f_sums"), 16)
                    sp.dma_start(sums[1 + (NT - 1) * P:1 + N, :], node[0:TAIL, NT - 1, :]).then_inc(sem("f_sums"), 16)
                    sp.wait_ge(sem("c_u1"), PAIRS)
                    sp.dma_start(sums[1 + N:1 + N + TS, :].rearrange("(t p) d -> p t d", p=P),
                                 node[:, BLOCKS - 2:BLOCKS, :]).then_inc(sem("f_sums"), 16)
                    sp.dma_start(rows_x[0:1, :], node[0:1, BLOCKS - 1, :]).then_inc(sem("f_rows"), 16)
                    for c in range(XIN):
                        sp.wait_ge(sem("f_xn2"), (c + 1) * XCH)
                        sp.dma_start(rows_x[1 + c * XCH * P:1 + (c + 1) * XCH * P, :].rearrange("(t p) d -> p t d", p=P),
                                     accv[:, c * XCH:(c + 1) * XCH, :]).then_inc(sem("f_rows"), 16)
                    sp.wait_ge(sem("f_sums"), (XIN + 2) * 16)
                    sp.wait_ge(sem("f_rows"), (XIN + 1) * 16)

                @block.gpsimd
                def _(pool):
                    pool.iota(rev[:, :], pattern=[[-1, NX]], base=NX, channel_multiplier=0,
                              allow_small_or_imprecise_dtypes=True).then_inc(sem("f_c"), 1)
                    pool.iota(starts[:, :], pattern=[[TS, FT]], base=0, channel_multiplier=0,
                              allow_small_or_imprecise_dtypes=True).then_inc(sem("f_c"), 1)
                    pool.memset(keep[:, :, :], 1.0).then_inc(sem("f_c"), 1)
                    pool.memset(one8[:, :], 1.0).then_inc(sem("f_c"), 1)
                    pool.iota(dumpp[:, :, :], pattern=[[P, 2], [0, NT]], base=DUMP, channel_multiplier=1,
                              allow_small_or_imprecise_dtypes=True).then_inc(sem("f_c"), 1)
                    pool.affine_select(out=tri[:, :], in_=ones[:, :], compare_op=ALU.is_gt, fill=0.0, base=0,
                                       pattern=[[1, P]], channel_multiplier=-1).then_inc(sem("f_c"), 1)
                    pool.iota(tags[:, :, :, :], pattern=[[P, NT], [0, 4]], base=1, channel_multiplier=1,
                              allow_small_or_imprecise_dtypes=True).then_inc(sem("f_tags"), 1)
                    pool.iota(spare[:, :, :], pattern=[[0, FT], [P, 2]], base=1 + N, channel_multiplier=1,
                              allow_small_or_imprecise_dtypes=True).then_inc(sem("f_tags"), 1)
                    pool.iota(places[:, :], pattern=[[1, P]], base=0, channel_multiplier=0,
                              allow_small_or_imprecise_dtypes=True).then_inc(sem("f_tags"), 1)
                    pool.wait_ge(sem("f_c"), 6)
                    pool.affine_select(out=keep[:, :, :], in_=keep[:, :, :], compare_op=ALU.not_equal, fill=0.0, base=0,
                                       pattern=[[0, NX], [1, NT]], channel_multiplier=0).then_inc(sem("f_c"), 1)
                    pool.affine_select(out=dumpp[:, :, :], in_=dumpp[:, :, :], compare_op=ALU.is_ge, fill=0.0, base=-N,
                                       pattern=[[0, 2], [P, NT]], channel_multiplier=1).then_inc(sem("f_c"), 1)
                    def body(n, q, has):
                        if has(2):
                            pool.wait_ge(sem("c_h1"), n - 1)
                            later(pool, "f_t", n - 3, n, 4)
                            later(pool, "f_s", (n - 3) * 2, n, 4)
                            pool.tensor_tensor(xs[q][:, :, :], pair(node, n - 2),
                                               hh[q][:, :].rearrange("p (h d) -> p h d", h=2), ALU.add
                                               ).then_inc(sem("f_xs"), 1)
                            pool.wait_ge(sem("f_xs"), n - 1)
                            pool.nop(nofuse=True)
                            pool.tensor_tensor(pair(node, n - 2), pair(node, n - 2),
                                               hh[q][:, :].rearrange("p (h d) -> p h d", h=2), ALU.add
                                               ).then_inc(sem("c_u1"), 1)
                    slots(pool, body)
                    pool.wait_ge(sem("f_lo"), 2)
                    pool.wait_ge(sem("f_tags"), 3)

                    def one_hots(i, q, is_first):
                        if not (is_first and q == 0):
                            pool.wait_ge(sem("f_at_p"), i)
                        pool.tensor_copy(lo_col[:, :], lo_f[:, 1, bass.ds(i, 1)]).then_inc(sem("f_lo_col"), 1)
                        pool.wait_ge(sem("f_lo_col"), i + 1)
                        if not is_first:
                            pool.wait_ge(sem("f_inv"), i - 1)
                        pool.nop(nofuse=True)
                        pool.tensor_scalar(at_place[:, q, 1, :], places[:, :], lo_col[:, :], None, ALU.is_equal
                                           ).then_inc(sem("f_at_p"), 1)
                    by_turn(pool, one_hots)

                @block.scalar
                def _(a):
                    def copies(n, q, has):
                        if has(3):
                            a.wait_ge(sem("f_t"), n - 2)
                            later(a, "f_l", n - 4, n, 5)
                            a.activation(xst[1 - q][:, :], ps_xt[1 - q][:, :], ACT.Copy).then_inc(sem("f_at"), 1)
                    conv_scalar(a, 1, copies, 3)
                    a.wait_ge(sem("f_var"), 1)
                    a.activation(rstd[:, :], rstd[:, :], ACT.Sqrt).then_inc(sem("f_std"), 1)
                    a.wait_ge(sem("f_var"), 2)
                    a.activation(both[:, :], both[:, :], ACT.Sqrt).then_inc(sem("f_std"), 1)
                    a.wait_ge(sem("f_lmax"), 1)
                    a.activation(ea[:, :, :], ea[:, :, :], ACT.Exp).then_inc(sem("f_exp"), 1)
                    a.wait_ge(sem("f_nmr"), 1)
                    a.wait_ge(sem("c_u1"), PAIRS)
                    with a.Fori(0, XIN) as c:
                        for k in range(XCH):
                            i = c * XCH + k
                            a.activation(tile(accv, i), tile(node, i), ACT.Identity, scale=both[:, bass.ds(i, 1)],
                                         bias=nmr[:, bass.ds(i, 1)]).then_inc(sem("f_xn2"), 1)
                    a.wait_ge(sem("f_lo"), 2)
                    a.wait_ge(sem("f_tags"), 3)

                    def one_hots(i, q, is_first):
                        if not (is_first and q == 0):
                            a.wait_ge(sem("f_at_a"), i)
                        a.activation(dist2[:, :], places[:, :], ACT.Square, scale=-1.0, bias=lo_f[:, 0, bass.ds(i, 1)]
                                     ).then_inc(sem("f_d2"), 1)
                        a.wait_ge(sem("f_d2"), i + 1)
                        if not is_first:
                            a.wait_ge(sem("f_inv"), i - 1)
                        a.activation(at_place[:, q, 0, :], dist2[:, :], ACT.Relu, scale=-1.0, bias=ones[:, 0:1]
                                     ).then_inc(sem("f_at_a"), 1)
                    by_turn(a, one_hots)

                @block.tensor
                def _(t):
                    for c in range(KC):
                        ins = t.matmul(ps_l[:, BLOCKS * NX:(BLOCKS + 1) * NX], ones[:, :], w_r[:, c, :],
                                       start=(c == 0), stop=(c == KC - 1))
                    ins.then_inc(sem("f_ws"), 1)

                    def router(n, q, has):
                        if has(3):
                            t.wait_ge(sem("f_xs"), n - 2)
                            later(t, "f_at", n - 4, n, 5)
                            for j in range(2 * KC):
                                ins = t.transpose(ps_xt[1 - q][:, j * P:(j + 1) * P],
                                                  flat2(xs[1 - q][:, :, :])[:, j * P:(j + 1) * P], ident[:, :])
                            ins.then_inc(sem("f_t"), 1)
                        if has(4):
                            t.wait_ge(sem("f_at"), n - 3)
                            for h in range(2):
                                for c in range(KC):
                                    j = h * KC + c
                                    ins = t.matmul(ps_l[:, bass.ds((n * 2 - 8 + h) * NX, NX)], xst[q][:, j * P:(j + 1) * P],
                                                   w_r[:, c, :], start=(c == 0), stop=(c == KC - 1))
                            ins.then_inc(sem("f_l"), 1)
                    conv_tensor(t, 1, router, 4)
                    t.wait_ge(sem("f_m"), 1)
                    t.wait_ge(sem("f_c"), 6)
                    m = ec[:, :, :].rearrange("p t e -> p (t e)")
                    t.matmul(ps_a[:, 0:NT * NX], tri[:, :], m, start=True, stop=True)
                    t.matmul(ps_b[:, 0:NT * NX], ones[:, :], m, start=True, stop=True).then_inc(sem("f_cnt"), 1)

                    def slots_of(i, q, is_first):
                        for s in ("f_col", "f_at_a", "f_at_p"):
                            t.wait_ge(sem(s), i + 1)
                        for j in range(2):
                            ins = t.matmul(ps_z[0][:, 0:2 * SC], at_place[:, q, j, :],
                                           at_col[:, q, j, :, :].rearrange("p v s -> p (v s)"),
                                           start=is_first and q == 0 and j == 0,
                                           stop=isinstance(i, int) and i == NT - 1 and j == 1, skip_group_check=True)
                        ins.then_inc(sem("f_inv"), 1)
                    by_turn(t, slots_of)

                @block.vector
                def _(v):
                    def b8(ap):
                        return ap[:, :, None].to_broadcast([P, NT, NX])

                    def b49(ap):
                        return ap[:, None, :].to_broadcast([P, NT, NX])

                    def body(n, q, has):
                        conv_vector(v, 1, n, q, has)
                        if has(3):
                            v.wait_ge(sem("f_xs"), n - 2)
                            for h in range(2):
                                v.bn_stats(dense(stat[:, bass.ds((n - 3) * 2 + h, 1), :]), xs[1 - q][:, h, :]
                                           ).then_inc(sem("f_s"), 1)
                    slots(v, body, 3)
                    v.wait_ge(sem("f_s"), BLOCKS)
                    for t in range(NT):
                        v.bn_aggr(mv[:, t, :], stat[:, t, :]).then_inc(sem("f_mv"), 1)
                    v.wait_ge(sem("f_mv"), NT)
                    mean, var = mv[:, :, 0], mv[:, :, 1]
                    v.tensor_scalar(rstd[:, :], var, LN_EPS, None, ALU.add).then_inc(sem("f_var"), 1)
                    v.wait_ge(sem("f_ws"), 1)
                    v.wait_ge(sem("f_l"), PAIRS)
                    link(v, "f_v", v.tensor_copy(w_sum[:, :], ps_l[:, BLOCKS * NX:(BLOCKS + 1) * NX]))
                    link(v, "f_v", v.tensor_tensor(eb[:, :, :], b8(mean), b49(w_sum[:, :]), ALU.mult))
                    link(v, "f_v", v.tensor_tensor(lg[:, :, :], ps_l[:, 0:NT * NX].rearrange("p (t e) -> p t e", e=NX),
                                                   eb[:, :, :], ALU.subtract))
                    v.wait_ge(sem("f_std"), 1)
                    link(v, "f_v", v.reciprocal(rstd[:, :], rstd[:, :]))
                    link(v, "f_v", v.tensor_tensor(both[:, :], rstd[:, :], rstd[:, :], ALU.mult))
                    link(v, "f_v", v.tensor_tensor(both[:, :], both[:, :], var, ALU.mult))
                    v.tensor_scalar(both[:, :], both[:, :], LN_EPS, None, ALU.add).then_inc(sem("f_var"), 1)
                    link(v, "f_v", v.tensor_tensor(lg[:, :, :], lg[:, :, :], b8(rstd[:, :]), ALU.mult))
                    link(v, "f_v", v.tensor_tensor(lg[:, :, :], lg[:, :, :], b49(b_r[:, :]), ALU.add))
                    link(v, "f_v", v.tensor_reduce(small[:, :], lg[:, :, :], AX.X, ALU.max))
                    v.tensor_tensor(ea[:, :, :], lg[:, :, :], b8(small[:, :]), ALU.subtract).then_inc(sem("f_lmax"), 1)
                    v.wait_ge(sem("f_std"), 2)
                    link(v, "f_v", v.reciprocal(both[:, :], both[:, :]))
                    link(v, "f_v", v.tensor_tensor(both[:, :], both[:, :], rstd[:, :], ALU.mult))
                    v.scalar_tensor_tensor(nmr[:, :], mean, -1.0, both[:, :], ALU.mult, ALU.mult).then_inc(sem("f_nmr"), 1)
                    v.wait_ge(sem("f_exp"), 1)
                    link(v, "f_v", v.tensor_reduce(small[:, :], ea[:, :, :], AX.X, ALU.add))
                    link(v, "f_v", v.reciprocal(small[:, :], small[:, :]))
                    link(v, "f_v", v.tensor_tensor(ea[:, :, :], ea[:, :, :], b8(small[:, :]), ALU.mult))
                    v.wait_ge(sem("f_c"), 8)
                    for j in range(2):
                        link(v, "f_v", v.tensor_reduce(top[:, j, :], ea[:, :, :], AX.X, ALU.max))
                        link(v, "f_v", v.tensor_tensor(eb[:, :, :], ea[:, :, :], b8(top[:, j, :]), ALU.is_equal))
                        link(v, "f_v", v.tensor_tensor(eb[:, :, :], eb[:, :, :], b49(rev[:, :]), ALU.mult))
                        link(v, "f_v", v.tensor_reduce(small[:, :], eb[:, :, :], AX.X, ALU.max))
                        link(v, "f_v", v.tensor_tensor(oh[j][:, :, :], eb[:, :, :], b8(small[:, :]), ALU.is_equal))
                        if j == 0:
                            link(v, "f_v", v.scalar_tensor_tensor(
                                ea[:, :, :].rearrange("p t e -> p (t e)"), oh[0][:, :, :].rearrange("p t e -> p (t e)"), -4.0,
                                ea[:, :, :].rearrange("p t e -> p (t e)"), ALU.mult, ALU.add))
                    link(v, "f_v", v.tensor_tensor(small[:, :], top[:, 0, :], top[:, 1, :], ALU.add))
                    link(v, "f_v", v.reciprocal(small[:, :], small[:, :]))
                    v.wait_ge(sem("f_tags"), 3)
                    for j in range(2):
                        v.tensor_tensor(tags[:, :, j, 1], top[:, j, :], small[:, :], ALU.mult).then_inc(sem("f_w"), 1)
                    link(v, "f_v", v.tensor_tensor(ec[:, :, :], oh[0][:, :, :], oh[1][:, :, :], ALU.add))
                    v.tensor_tensor(ec[:, :, :], ec[:, :, :], b8(valid[:, :]), ALU.mult).then_inc(sem("f_m"), 1)
                    v.wait_ge(sem("f_cnt"), 1)
                    link(v, "f_v", v.tensor_copy(tot[:, :, :], ps_b[:, 0:NT * NX].rearrange("p (t e) -> p e t", e=NX)))
                    flat = "p e t -> p (e t)"
                    link(v, "f_v", v.tensor_tensor_scan(incl[:, :, :].rearrange(flat), keep[:, :, :].rearrange(flat),
                                                        tot[:, :, :].rearrange(flat), 0.0, ALU.mult, ALU.add))
                    link(v, "f_v", v.tensor_scalar(n_f[:, :], incl[:, :, NT - 1], float(TS - 1), None, ALU.add))
                    link(v, "f_v", v.tensor_copy(n_i[:, :], n_f[:, :]))
                    link(v, "f_v", v.tensor_scalar(n_i[:, :], n_i[:, :], -TS, None, ALU.bitwise_and))
                    link(v, "f_v", v.tensor_copy(n_f[:, :], n_i[:, :]))
                    link(v, "f_v", v.tensor_tensor_scan(st[:, :], one8[:, :], n_f[:, :], 0.0, ALU.mult, ALU.add))
                    link(v, "f_v", v.tensor_tensor(st[:, :], st[:, :], n_f[:, :], ALU.subtract))
                    link(v, "f_v", v.tensor_tensor(ge[:, :, :], st[0:1, None, :].to_broadcast([1, FT, NX]),
                                                   starts[:, :, None].to_broadcast([1, FT, NX]), ALU.is_le))
                    link(v, "f_v", v.tensor_reduce(which[:, :], ge[:, :, :], AX.X, ALU.add))
                    v.tensor_scalar(which_i[:, :], which[:, :], 1.0, float(-1), ALU.mult, ALU.add).then_inc(sem("f_which"), 1)
                    link(v, "f_v", v.tensor_tensor(incl[:, :, :], incl[:, :, :], tot[:, :, :], ALU.subtract))
                    link(v, "f_v", v.tensor_tensor(incl[:, :, :], incl[:, :, :], st[:, :, None].to_broadcast([P, NX, NT]), ALU.add))
                    link(v, "f_v", v.tensor_tensor(ea[:, :, :], ps_a[:, 0:NT * NX].rearrange("p (t e) -> p t e", e=NX),
                                                   incl[:, :, :].rearrange("p e t -> p t e"), ALU.add))
                    for j in range(2):
                        link(v, "f_v", v.tensor_tensor(eb[:, :, :], ea[:, :, :], oh[j][:, :, :], ALU.mult))
                        link(v, "f_v", v.tensor_reduce(small[:, :], eb[:, :, :], AX.X, ALU.add))
                        link(v, "f_v", v.tensor_tensor(small[:, :], small[:, :], valid[:, :], ALU.mult))
                        link(v, "f_v", v.tensor_tensor(pos_i[:, j, :], small[:, :], dumpp[:, j, :], ALU.add))
                    link(v, "f_v", v.tensor_scalar(lo_i[:, :, :], pos_i[:, :, :], P - 1, None, ALU.bitwise_and))
                    v.tensor_copy(lo_f[:, :, :], lo_i[:, :, :]).then_inc(sem("f_lo"), 2)
                    link(v, "f_v", v.tensor_scalar(hi_i[:, :, :], pos_i[:, :, :], 7, None, ALU.arith_shift_right))
                    link(v, "f_v", v.tensor_copy(hi_f[:, :, :], hi_i[:, :, :]))
                    v.wait_ge(sem("f_w"), 2)

                    def columns(i, q, is_first):
                        if not is_first:
                            v.wait_ge(sem("f_inv"), i - 1)
                        for j in range(2):
                            for c in range(2):
                                ins = v.tensor_scalar(at_col[:, q, j, c, :], places[:, 0:SC], hi_f[:, j, bass.ds(i, 1)],
                                                      tags[:, bass.ds(i, 1), j, c], ALU.is_equal, ALU.mult)
                        ins.then_inc(sem("f_col"), 1)
                    by_turn(v, columns)
                    v.wait_ge(sem("f_inv"), NT)
                    link(v, "f_v", v.tensor_copy(slot_no[:, :], ps_z[0][:, 0:SC]))
                    v.tensor_copy(slot_w[:, :], ps_z[0][:, SC:2 * SC])
                    v.tensor_copy(slot_row[:, :], slot_no[:, :])
                    every = spare[:, :, :].rearrange("p n h -> p (n h)")
                    link(v, "f_v", v.scalar_tensor_tensor(every, slot_no[:, :], 0.0, every, ALU.is_equal, ALU.mult))
                    link(v, "f_v", v.tensor_tensor(slot_sum[:, :], every, slot_no[:, :], ALU.add))

        acc_ctx.close()

        with ExitStack() as ph:
            ctx_name[0] = "ffn"
            wh = [sb(ph, f"wh{i}", [P, WIDE], F32R) for i in range(2)]
            wl = [sb(ph, f"wl{i}", [P, WIDE], F32R) for i in range(2)]
            vec = [sb(ph, f"vec{i}", [P, SMALL]) for i in range(2)]
            xr = [sb(ph, f"xr{i}", [P, 2, D]) for i in range(2)]
            g_row = [sb(ph, f"g_row{i}", [P, 2], I32) for i in range(2)]
            g_sum = [sb(ph, f"g_sum{i}", [P, 2], I32) for i in range(2)]
            xe = sb(ph, "xe", [P, KC, TS])
            xh = sb(ph, "xh", [P, KC, TS], F32R)
            xl = sb(ph, "xl", [P, KC, TS], F32R)
            hr = sb(ph, "hr", [P, 4, TS])
            hh = [sb(ph, f"hhi{i}", [P, HC, TS], F32R) for i in range(2)]
            hl = [sb(ph, f"hlo{i}", [P, HC, TS], F32R) for i in range(2)]
            ys = [sb(ph, f"ys{i}", [P, 2, D]) for i in range(2)]
            bk = banks(ph, 6)
            ps_x, ps_h, ps_y = bk[0], bk[1:5], bk[5]

            def pairs(eng, body, peeled=1):
                body(0, 0, True, False)
                body(1, 1, True, False)
                with eng.Fori(1, FT // 2 - peeled) as n:
                    body(n * 2, 0, False, False)
                    body(n * 2 + 1, 1, False, False)
                for n in range(FT - 2 * peeled, FT):
                    body(n, n % 2, False, n == FT - 1)

            def three(t, to, a, b, first, last):
                t.matmul(to, a[0], b[0], start=first, stop=False)
                t.matmul(to, a[0], b[1], start=False, stop=False)
                return t.matmul(to, a[1], b[0], start=False, stop=last)

            with nc.Block() as block:
                @block.sync
                def _(sp):
                    def first_half(q, e):
                        for to, of in ((wh[q], w_hi), (wl[q], w_lo)):
                            sp.dma_start(to[:, 0:O_W2].bitcast(F32), of[:, bass.ds(e * WIDE, O_W2)]
                                         ).then_inc(sem(f"load_{q}"), 16)
                        sp.dma_start(vec[q][:, 0:O_B2], vectors[:, bass.ds(e * SMALL, O_B2)]).then_inc(sem(f"load_{q}"), 16)

                    def second_half(q, e):
                        for to, of in ((wh[q], w_hi), (wl[q], w_lo)):
                            sp.dma_start(to[:, O_W2:WIDE].bitcast(F32), of[:, bass.ds(e * WIDE + O_W2, WIDE - O_W2)]
                                         ).then_inc(sem(f"load_{2 + q}"), 16)
                        sp.dma_start(vec[q][:, O_B2:SMALL], vectors[:, bass.ds(e * SMALL + O_B2, D)]
                                     ).then_inc(sem(f"load_{2 + q}"), 16)

                    def one(n, q, is_first, is_last):
                        e = sp.value_load(which_i[0:1, bass.ds(n, 1)], min_val=0, max_val=NX - 1)
                        if is_first:
                            first_half(q, e)
                            second_half(q, e)
                        else:
                            was = sp.value_load(which_i[0:1, bass.ds(n - 2, 1)], min_val=0, max_val=NX - 1)
                            sp.wait_ge(sem("e_g"), n * HC - HC)
                            sp.nop(nofuse=True)
                            with sp.If(e - was > 0):
                                first_half(q, e)
                                sp.wait_ge(sem("e_y"), n - 1)
                                sp.wait_ge(sem("e_yb"), n - 1)
                                second_half(q, e)
                            with sp.Else():
                                sp.sem_inc(sem(f"load_{q}"), 48)
                                sp.wait_ge(sem("e_y"), n - 1)
                                sp.nop(nofuse=True)
                                sp.sem_inc(sem(f"load_{2 + q}"), 48)
                    pairs(sp, one)

                @block.scalar
                def _(a):
                    def scaled(n, q, is_first):
                        a.wait_ge(sem(f"load_{q}"), (n - q) * 24 + 48)
                        a.wait_ge(sem("e_t"), n + 1)
                        if not (is_first and q == 0):
                            a.wait_ge(sem("e_xs"), n * 2)
                        for c in range(KC):
                            a.activation(xe[:, c, :], ps_x[:, c * TS:(c + 1) * TS], ACT.Identity,
                                         scale=vec[q][:, O_G + c:O_G + c + 1], bias=vec[q][:, O_B + c:O_B + c + 1]
                                         ).then_inc(sem("e_xe"), 1)

                    def one(n, q, is_first, is_last):
                        for m in range(HC):
                            a.wait_ge(sem("e_h"), n * HC + m + 1)
                            if not (is_first and q == 0 and m < 4):
                                a.wait_ge(sem("e_hs"), (n * HC + m - 3) * 2)
                            a.activation(hr[:, m % 4, :], ps_h[m % 4][:, 0:TS], ACT.Gelu,
                                         bias=vec[q][:, O_B1 + m:O_B1 + m + 1]).then_inc(sem("e_g"), 1)
                        if not is_last:
                            scaled(n + 1, 1 - q, is_first and q == 0)
                    scaled(0, 0, True)
                    pairs(a, one)

                @block.vector
                def _(v):
                    def split_x(n, q, is_first):
                        v.wait_ge(sem("e_xe"), n * KC + KC)
                        if not (is_first and q == 0):
                            v.wait_ge(sem("e_h"), n * HC)
                        v.tensor_copy(xh[:, :, :], xe[:, :, :]).then_inc(sem("e_xs"), 1)
                        v.wait_ge(sem("e_xs"), n * 2 + 1)
                        v.tensor_tensor(xl[:, :, :], xe[:, :, :], xh[:, :, :].bitcast(F32), ALU.subtract).then_inc(sem("e_xs"), 1)

                    def one(n, q, is_first, is_last):
                        if not is_first:
                            v.wait_ge(sem("e_y"), n - 1)
                        for m in range(HC):
                            v.wait_ge(sem("e_g"), n * HC + m + 1)
                            v.tensor_copy(hh[q][:, m, :], hr[:, m % 4, :]).then_inc(sem("e_hs"), 1)
                            v.wait_ge(sem("e_hs"), (n * HC + m) * 2 + 1)
                            v.tensor_tensor(hl[q][:, m, :], hr[:, m % 4, :], hh[q][:, m, :].bitcast(F32), ALU.subtract
                                            ).then_inc(sem("e_hs"), 1)
                        if not is_last:
                            split_x(n + 1, 1 - q, False)
                        v.wait_ge(sem("e_y"), n + 1)
                        v.wait_ge(sem(f"load_{2 + q}"), (n - q) * 24 + 48)
                        if not is_first:
                            for h in range(2):
                                v.wait_ge(sem(f"e_add{h}"), (n - 1) * 16)
                        v.tensor_tensor(ys[q][:, :, :], ps_y[:, :].rearrange("p (h d) -> p h d", h=2),
                                        vec[q][:, None, O_B2:O_B2 + D].to_broadcast([P, 2, D]), ALU.add
                                        ).then_inc(sem("e_yb"), 1)
                        v.wait_ge(sem("e_yb"), n + 1)
                        for h in range(2):
                            ins = v.tensor_scalar(ys[q][:, h, :], ys[q][:, h, :], slot_w[:, bass.ds(n * 2 + h, 1)], None, ALU.mult)
                        ins.then_inc(sem("e_ys"), 1)
                    split_x(0, 0, True)
                    pairs(v, one)

                @block.gpsimd
                def _(pool):
                    def gather(n, q, is_first):
                        if not is_first:
                            pool.wait_ge(sem("e_t"), n - 1)
                        pool.tensor_copy(g_row[q][:, :], slot_row[:, bass.ds(n * 2, 2)]).then_inc(sem("e_row"), 1)
                        pool.wait_ge(sem("e_row"), n + 1)
                        pool.nop(nofuse=True)
                        for h in range(2):
                            pool.indirect_dma_start(xr[q][:, h, :], None, rows_x,
                                                    bass.IndirectOffsetOnAxis(ap=g_row[q][:, h:h + 1], axis=0)
                                                    ).then_inc(sem(f"rows_{q}"), 16)

                    def one(n, q, is_first, is_last):
                        if not (isinstance(n, int) and n + 3 >= FT):
                            gather(n + 3, 1 - q, False)
                        if not (is_first and q == 0):
                            for h in range(2):
                                pool.wait_ge(sem(f"e_add{h}"), n * 16)
                        pool.tensor_copy(g_sum[q][:, :], slot_sum[:, bass.ds(n * 2, 2)]).then_inc(sem("e_sum"), 1)
                        pool.wait_ge(sem("e_sum"), n + 1)
                        pool.wait_ge(sem("e_ys"), n + 1)
                        pool.nop(nofuse=True)
                        for h in range(2):
                            pool.indirect_dma_start(sums, bass.IndirectOffsetOnAxis(ap=g_sum[q][:, h:h + 1], axis=0),
                                                    ys[q][:, h, :], None, compute_op=ALU.add).then_inc(sem(f"e_add{h}"), 16)
                    gather(0, 0, True)
                    gather(1, 1, True)
                    gather(2, 0, False)
                    pairs(pool, one, 2)
                    for h in range(2):
                        pool.wait_ge(sem(f"e_add{h}"), FT * 16)

                @block.tensor
                def _(t):
                    def transposes(n, q, is_first):
                        t.wait_ge(sem(f"rows_{q}"), (n - q) * 16 + 32)
                        if not is_first:
                            t.wait_ge(sem("e_xe"), n * KC)
                        for h in range(2):
                            for c in range(KC):
                                ins = t.transpose(ps_x[:, c * TS + h * P:c * TS + (h + 1) * P],
                                                  xr[q][:, h, c * P:(c + 1) * P], ident[:, :])
                        ins.then_inc(sem("e_t"), 1)

                    def one(n, q, is_first, is_last):
                        t.wait_ge(sem("e_xs"), n * 2 + 2)
                        t.wait_ge(sem(f"load_{q}"), (n - q) * 24 + 48)
                        for m in range(HC):
                            if not (is_first and q == 0 and m < 4):
                                t.wait_ge(sem("e_g"), n * HC + m - 3)
                            for c in range(KC):
                                at = slice(c * HID + m * P, c * HID + (m + 1) * P)
                                ins = three(t, ps_h[m % 4][:, 0:TS], (wh[q][:, at], wl[q][:, at]),
                                            (xh[:, c, :], xl[:, c, :]), c == 0, c == KC - 1)
                            ins.then_inc(sem("e_h"), 1)
                        if not is_last:
                            transposes(n + 1, 1 - q, False)
                        t.wait_ge(sem(f"load_{2 + q}"), (n - q) * 24 + 48)
                        if not (is_first and q == 0):
                            t.wait_ge(sem("e_yb"), n)
                        for h in range(2):
                            for m in range(HC):
                                if h == 0:
                                    t.wait_ge(sem("e_hs"), (n * HC + m) * 2 + 2)
                                at = slice(O_W2 + m * D, O_W2 + (m + 1) * D)
                                ins = three(t, ps_y[:, h * D:(h + 1) * D],
                                            (hh[q][:, m, h * P:(h + 1) * P], hl[q][:, m, h * P:(h + 1) * P]),
                                            (wh[q][:, at], wl[q][:, at]), m == 0, m == HC - 1)
                        ins.then_inc(sem("e_y"), 1)
                    transposes(0, 0, True)
                    pairs(t, one)

        with nc.Block() as block:
            @block.sync
            def _(sp):
                sp.dma_start(out.rearrange("n d -> (n d)").rearrange("(a b) -> a b", a=P),
                             sums[1:1 + N, :].rearrange("n d -> (n d)").rearrange("(a b) -> a b", a=P)
                             ).then_inc(sem("out"), 16)
                sp.wait_ge(sem("out"), 16)


def _layout(inputs):
    import numpy as np
    f = {k: np.ascontiguousarray(v) for k, v in inputs.items()}
    wide = np.concatenate([
        f["L0_ffn_W1"].reshape(NX, KC, P, HID).transpose(2, 0, 1, 3).reshape(P, NX, KC * HID),
        f["L0_ffn_W2"].reshape(NX, HC, P, D).transpose(2, 0, 1, 3).reshape(P, NX, HC * D),
    ], axis=2).reshape(P, NX * WIDE)
    vectors = np.concatenate([
        f["L0_ffn_b1"].reshape(NX, HC, P).transpose(2, 0, 1),
        f["L0_ffn_ln_g"].reshape(NX, KC, P).transpose(2, 0, 1),
        f["L0_ffn_ln_b"].reshape(NX, KC, P).transpose(2, 0, 1),
        np.repeat(f["L0_ffn_b2"][None], P, axis=0),
    ], axis=2).reshape(P, NX * SMALL)
    return {
        "x": f["x"], "src": f["src"], "dst": f["dst"],
        "wqkv": np.concatenate([f["L0_mix_Wq"].T, f["L0_mix_Wkv"].T], axis=1),
        "wproj": np.ascontiguousarray(f["L0_mix_Wproj"].T), "bproj": f["L0_mix_bproj"],
        "gw1": f["L0_gnn_W1"], "gb1": f["L0_gnn_b1"], "gw2": f["L0_gnn_W2"], "gb2": f["L0_gnn_b2"],
        "wr": f["L0_ffn_Wr"], "br": f["L0_ffn_br"],
        "wide": np.pad(wide, ((0, 0), (0, NT * SPLIT - NX * WIDE))), "vectors": vectors,
    }


def kernel(**inputs):
    import numpy as np
    import concourse.bacc as bacc
    from concourse.bass_utils import run_bass_kernel_spmd

    arrays = _layout(inputs)
    nc = bacc.Bacc("TRN2", target_bir_lowering=False, num_devices=1)
    args = [nc.dram_tensor(name, a.shape, mybir.dt.from_np(a.dtype), kind="ExternalInput").ap()
            for name, a in arrays.items()]
    out = nc.dram_tensor("out", (N, D), F32, kind="ExternalOutput").ap()
    gps_layer(nc, *args, out)
    r = run_bass_kernel_spmd(nc, [arrays], core_ids=[0])
    return r.results[0]["out"]
```
